# Optimizing a Trainium2 kernel written in Bass

```python
import numpy as np
import jax
import jax.numpy as jnp

def _softmax(x, axis=-1):
    return jax.nn.softmax(x, axis=axis)

def _gelu(x):
    return jax.nn.gelu(x, approximate=True)

def _silu(x):
    return jax.nn.silu(x)

def _sigmoid(x):
    return jax.nn.sigmoid(x)

def _layernorm(x, axis=-1, eps=1e-05):
    m = jnp.mean(x, axis=axis, keepdims=True)
    v = jnp.var(x, axis=axis, keepdims=True)
    return (x - m) / jnp.sqrt(v + eps)

def _scatter_add(tgt, idx, src, axis=0):
    return tgt.at[idx].add(src)

def _segment_sum(src, seg, n):
    return jax.ops.segment_sum(src, seg, n)
kernel_name = 'mk_gnn_resnorm_d4_gnn_r8_872fdf'

def setup_inputs(seed: int=0):
    np.random.seed(seed)
    _w = jnp.asarray

    def _rec_inputs():
        import jax
        import jax.numpy as jnp
        _gk = jax.random.key(seed)
        x = -7.329e-05 + 0.9999 * jax.random.normal(jax.random.fold_in(_gk, 1), (1250, 1024), jnp.float32)
        _s = jax.random.randint(jax.random.fold_in(_gk, 2), (10000,), 0, 1250, jnp.int32)
        _d = jax.random.randint(jax.random.fold_in(_gk, 3), (10000,), 0, 1250, jnp.int32)
        _loop = jnp.arange(1250, dtype=jnp.int32)
        src = jnp.concatenate([_s, _d, _loop])
        dst = jnp.concatenate([_d, _s, _loop])
        _o = jnp.argsort(dst, stable=True)
        src = src[_o]
        dst = dst[_o]
        edge_weight = -0.000130211 + 0.031236 * jax.random.normal(jax.random.fold_in(_gk, 13), (21250,), jnp.float32)
        return (x, src, dst, edge_weight)
    x, src, dst, edge_weight = _rec_inputs()

    def _L0_gnn_setup():
        import jax, jax.numpy as jnp
        import numpy as np
        INDIM = 1024
        OUTDIM = 1024
        NNZ = 8192
        N = 6250
        key = jax.random.key(seed)
        k1, k2, k3, k4, k5 = jax.random.split(key, 5)
        x = jax.random.normal(k1, (N, INDIM), dtype=jnp.float32)
        stdv = np.sqrt(6.0 / (INDIM + OUTDIM))
        nnz_weight = jax.random.uniform(k2, (NNZ,), dtype=jnp.float32, minval=-stdv, maxval=stdv)
        bias = jax.random.normal(k3, (OUTDIM,), dtype=jnp.float32) * 0.02
        row = jax.random.randint(k4, (NNZ,), 0, OUTDIM, dtype=jnp.int64)
        col = jax.random.randint(k5, (NNZ,), 0, INDIM, dtype=jnp.int64)
        edge_index = jnp.stack([row, col])
        return {'x': x, 'nnz_weight': nnz_weight, 'bias': bias, 'edge_index': edge_index}
    _L0_gnn_all = _L0_gnn_setup()
    _L0_gnn_in = {k: v for k, v in _L0_gnn_all.items() if k in ('bias',)}
    del _L0_gnn_all

    def _L1_gnn_setup():
        import jax, jax.numpy as jnp
        import numpy as np
        N = 2500
        E = 40000
        IN = 1024
        HID = 256
        H = 4
        D = HID // H
        OUT = 1024
        EPS = 1e-06
        NEG_SLOPE = 0.2
        key = jax.random.key(seed)
        ks = jax.random.split(key, 8)
        x = jax.random.normal(ks[0], (N, IN), dtype=jnp.float32)
        edge_index = jax.random.randint(ks[1], (2, E), 0, N, dtype=jnp.int64)
        s = 0.02
        return {'x': x, 'edge_index': edge_index, 'rms_w': jnp.ones((IN,), dtype=jnp.float32), 'W_down': jax.random.normal(ks[2], (IN, HID), dtype=jnp.float32) * s, 'Wl': jax.random.normal(ks[3], (HID, HID), dtype=jnp.float32) * s, 'Wr': jax.random.normal(ks[4], (HID, HID), dtype=jnp.float32) * s, 'att': jax.random.normal(ks[5], (H, D), dtype=jnp.float32) * s, 'W_up': jax.random.normal(ks[6], (HID, OUT), dtype=jnp.float32) * s}
    _L1_gnn_all = _L1_gnn_setup()
    _L1_gnn_in = {k: v for k, v in _L1_gnn_all.items() if k in ('rms_w', 'W_down', 'Wl', 'Wr', 'att', 'W_up')}
    del _L1_gnn_all

    def _L2_gnn_setup():
        import jax, jax.numpy as jnp
        import numpy as np
        N_NODES = 1250
        N_EDGES = 20000
        DIM = 1024
        key = jax.random.key(seed)
        k1, k2, k3 = jax.random.split(key, 3)
        x = jax.random.normal(k1, (N_NODES, DIM), dtype=jnp.float32)
        edge_index = jax.random.randint(k2, (2, N_EDGES), 0, N_NODES, dtype=jnp.int64)
        W = jax.random.normal(k3, (DIM, DIM), dtype=jnp.float32) * (1.0 / np.sqrt(DIM))
        b = jnp.zeros((DIM,), dtype=jnp.float32)
        return {'x': x, 'edge_index': edge_index, 'W': W, 'b': b}
    _L2_gnn_all = _L2_gnn_setup()
    _L2_gnn_in = {k: v for k, v in _L2_gnn_all.items() if k in ('W', 'b')}
    del _L2_gnn_all

    def _L3_gnn_setup():
        import jax, jax.numpy as jnp
        import numpy as np
        N_NODES = 3125
        N_EDGES = 50000
        D = 1024

        def _sage_layer(h, edge_src, edge_dst, deg_inv, W_self, W_neigh, b):
            msg = h[edge_src]
            agg = jax.ops.segment_sum(msg, edge_dst, num_segments=h.shape[0])
            mean = agg * deg_inv[:, None]
            return h @ W_self + mean @ W_neigh + b
        key = jax.random.key(seed)
        ks = jax.random.split(key, 8)
        s = 1.0 / np.sqrt(D)
        return {'x': jax.random.normal(ks[0], (N_NODES, D), dtype=jnp.float32), 'edge_src': jax.random.randint(ks[1], (N_EDGES,), 0, N_NODES, dtype=jnp.int32), 'edge_dst': jax.random.randint(ks[2], (N_EDGES,), 0, N_NODES, dtype=jnp.int32), 'W_self0': jax.random.normal(ks[3], (D, D), dtype=jnp.float32) * s, 'W_neigh0': jax.random.normal(ks[4], (D, D), dtype=jnp.float32) * s, 'b0': jnp.zeros((D,), dtype=jnp.float32), 'W_self1': jax.random.normal(ks[5], (D, D), dtype=jnp.float32) * s, 'W_neigh1': jax.random.normal(ks[6], (D, D), dtype=jnp.float32) * s, 'b1': jnp.zeros((D,), dtype=jnp.float32)}
    _L3_gnn_all = _L3_gnn_setup()
    _L3_gnn_in = {k: v for k, v in _L3_gnn_all.items() if k in ('W_self0', 'W_neigh0', 'b0', 'W_self1', 'W_neigh1', 'b1')}
    del _L3_gnn_all
    return {'x': x, 'src': src, 'dst': dst, 'edge_weight': edge_weight, 'L0_gnn_bias': _L0_gnn_in['bias'], 'L1_gnn_rms_w': _L1_gnn_in['rms_w'], 'L1_gnn_W_down': _L1_gnn_in['W_down'], 'L1_gnn_Wl': _L1_gnn_in['Wl'], 'L1_gnn_Wr': _L1_gnn_in['Wr'], 'L1_gnn_att': _L1_gnn_in['att'], 'L1_gnn_W_up': _L1_gnn_in['W_up'], 'L2_gnn_W': _L2_gnn_in['W'], 'L2_gnn_b': _L2_gnn_in['b'], 'L3_gnn_W_self0': _L3_gnn_in['W_self0'], 'L3_gnn_W_neigh0': _L3_gnn_in['W_neigh0'], 'L3_gnn_b0': _L3_gnn_in['b0'], 'L3_gnn_W_self1': _L3_gnn_in['W_self1'], 'L3_gnn_W_neigh1': _L3_gnn_in['W_neigh1'], 'L3_gnn_b1': _L3_gnn_in['b1']}

def reference(x, src, dst, edge_weight, L0_gnn_bias, L1_gnn_rms_w, L1_gnn_W_down, L1_gnn_Wl, L1_gnn_Wr, L1_gnn_att, L1_gnn_W_up, L2_gnn_W, L2_gnn_b, L3_gnn_W_self0, L3_gnn_W_neigh0, L3_gnn_b0, L3_gnn_W_self1, L3_gnn_W_neigh1, L3_gnn_b1):
    import jax
    import jax.numpy as jnp

    def _L0_gnn_ref(x, nnz_weight, bias, edge_index):
        import jax, jax.numpy as jnp
        import numpy as np
        INDIM = 1024
        OUTDIM = 1024
        NNZ = 8192
        N = 6250
        row, col = (edge_index[0], edge_index[1])
        W = jnp.zeros((OUTDIM, INDIM), dtype=nnz_weight.dtype).at[row, col].add(nnz_weight)
        return x @ W.T + bias

    def _L1_gnn_ref(x, edge_index, rms_w, W_down, Wl, Wr, att, W_up):
        import jax, jax.numpy as jnp
        import numpy as np
        N = 2500
        E = 40000
        IN = 1024
        HID = 256
        H = 4
        D = HID // H
        OUT = 1024
        EPS = 1e-06
        NEG_SLOPE = 0.2
        n = x.shape[0]
        ms = jnp.mean(jnp.square(x), axis=-1, keepdims=True)
        x = x * jax.lax.rsqrt(ms + EPS) * rms_w
        x = x @ W_down
        loop = jnp.arange(n, dtype=edge_index.dtype)
        src = jnp.concatenate([edge_index[0], loop])
        dst = jnp.concatenate([edge_index[1], loop])
        xl = (x @ Wl).reshape(n, H, D)
        xr = (x @ Wr).reshape(n, H, D)
        msg = xl[src] + xr[dst]
        act = jnp.where(msg > 0, msg, NEG_SLOPE * msg)
        e = jnp.einsum('ehd,hd->eh', act, att)
        m = jax.ops.segment_max(e, dst, num_segments=n)
        p = jnp.exp(e - m[dst])
        denom = jax.ops.segment_sum(p, dst, num_segments=n)
        alpha = p / (denom[dst] + 1e-16)
        out = jax.ops.segment_sum(alpha[..., None] * xl[src], dst, num_segments=n)
        out = out.reshape(n, HID)
        return out @ W_up

    def _L2_gnn_ref(x, edge_index, W, b):
        import jax, jax.numpy as jnp
        import numpy as np
        N_NODES = 1250
        N_EDGES = 20000
        DIM = 1024
        'GCNConv (add_self_loops=True, symmetric norm) -> Dropout(eval=identity) -> ReLU.'
        n = x.shape[0]
        loops = jnp.arange(n, dtype=edge_index.dtype)
        src = jnp.concatenate([edge_index[0], loops])
        dst = jnp.concatenate([edge_index[1], loops])
        deg = jax.ops.segment_sum(jnp.ones_like(dst, dtype=x.dtype), dst, num_segments=n)
        dinv = jnp.where(deg > 0, jax.lax.rsqrt(deg), jnp.zeros_like(deg))
        norm = dinv[src] * dinv[dst]
        h = x @ W
        msg = h[src] * norm[:, None]
        out = jax.ops.segment_sum(msg, dst, num_segments=n) + b
        return jax.nn.relu(out)

    def _L3_gnn_ref(x, edge_src, edge_dst, W_self0, W_neigh0, b0, W_self1, W_neigh1, b1):
        import jax, jax.numpy as jnp
        import numpy as np
        N_NODES = 3125
        N_EDGES = 50000
        D = 1024

        def _sage_layer(h, edge_src, edge_dst, deg_inv, W_self, W_neigh, b):
            msg = h[edge_src]
            agg = jax.ops.segment_sum(msg, edge_dst, num_segments=h.shape[0])
            mean = agg * deg_inv[:, None]
            return h @ W_self + mean @ W_neigh + b
        N = x.shape[0]
        deg = jax.ops.segment_sum(jnp.ones_like(edge_dst, dtype=x.dtype), edge_dst, num_segments=N)
        deg_inv = 1.0 / jnp.maximum(deg, 1.0)
        h = jax.nn.relu(_sage_layer(x, edge_src, edge_dst, deg_inv, W_self0, W_neigh0, b0))
        out = _sage_layer(h, edge_src, edge_dst, deg_inv, W_self1, W_neigh1, b1)
        return out
    edge_index = jnp.stack([src, dst])
    x = _layernorm(x + _L0_gnn_ref(x, edge_weight, L0_gnn_bias, edge_index), axis=-1)
    x = _layernorm(x + _L1_gnn_ref(x, edge_index, L1_gnn_rms_w, L1_gnn_W_down, L1_gnn_Wl, L1_gnn_Wr, L1_gnn_att, L1_gnn_W_up), axis=-1)
    x = _layernorm(x + _L2_gnn_ref(x, edge_index, L2_gnn_W, L2_gnn_b), axis=-1)
    x = _layernorm(x + _L3_gnn_ref(x, src, dst, L3_gnn_W_self0, L3_gnn_W_neigh0, L3_gnn_b0, L3_gnn_W_self1, L3_gnn_W_neigh1, L3_gnn_b1), axis=-1)
    return x

_drawn_inputs = setup_inputs


def setup_inputs(seed=0):
    import zlib

    import numpy as np

    out = dict(_drawn_inputs(seed))
    spreads = {'L1_gnn_rms_w': (1.0, 0.6),
     'L2_gnn_b': (0.0, 0.1),
     'L3_gnn_b0': (0.0, 0.1),
     'L3_gnn_b1': (0.0, 0.1)}
    factors = {'L1_gnn_W_down': 3.25,
     'L1_gnn_Wl': 3.272,
     'L1_gnn_Wr': 8.0,
     'L1_gnn_att': 8.0,
     'L1_gnn_W_up': 3.268}
    for name, (base, spread) in spreads.items():
        noise = np.random.default_rng([zlib.crc32(name.encode()), seed]).standard_normal(out[name].shape)
        drawn = base * np.exp(spread * noise) if base else spread * noise
        out[name] = jnp.asarray(drawn.astype(out[name].dtype))
    for name, factor in factors.items():
        out[name] = (out[name] * factor).astype(out[name].dtype)
    return out
```

```python
from contextlib import ExitStack

import concourse.bass as bass
from concourse import mybir

DT = mybir.dt
F32, F32R, BF16, I32 = DT.float32, DT.float32r, DT.bfloat16, DT.int32
ALU = mybir.AluOpType
ACT = mybir.ActivationFunctionType
AX = mybir.AxisListType

P = 128
NODES, EDGES = 1250, 21250
FEAT, HID, HEADS = 1024, 256, 4
HEAD_DIM = HID // HEADS
BLOCKS = -(-NODES // P)
ROWS = BLOCKS * P
KB = FEAT // P
HALF = 512
PAIR = 2 * P
PAIRS = -(-EDGES // PAIR)
SELF = PAIRS
TILES = 2 * (PAIRS + BLOCKS)
PAD_NODE = ROWS - 1
NO_NODE = 4 * ROWS
FAR = 1000.0
EPS = 1e-5
RMS_EPS = 1e-6
SLOPE = 0.2
BOUND = 40.0
MASKED = -1.0e30


class Memory:

    def __init__(self, nc, ctx, stage):
        self.nc, self.ctx, self.stage, self.named = nc, ctx, stage, []

    def sb(self, name, shape, dtype=F32):
        return self.ctx.enter_context(self.nc.sbuf_tensor(f"{self.stage}_{name}", shape, dtype))

    def ps(self, name, shape):
        return self.ctx.enter_context(self.nc.psum_tensor(f"{self.stage}_{name}", shape, F32))

    def sem(self, name):
        self.named.append(self.ctx.enter_context(self.nc.semaphore(f"{self.stage}_{name}")))
        return self.named[-1]

    def sems(self, name, n=2):
        return [self.sem(f"{name}{i}") for i in range(n)]

    def block(self):
        self.ctx.callback(self.clear)
        return self.ctx.enter_context(self.nc.Block())

    def clear(self):
        for sem in self.named:
            self.nc.gpsimd.sem_clear(sem)
        self.nc.all_engine_barrier()


def setup(nc, io, g):
    with ExitStack() as ctx:
        m = Memory(nc, ctx, "setup")
        iota_i = m.sb("iota_i", [P, ROWS], I32)
        node_i = m.sb("node_i", [P, BLOCKS], I32)
        pair_i = m.sb("pair_i", [P, 1], I32)
        dst_rows = m.sb("dst_rows", [P, PAIR], I32)
        dst_i = m.sb("dst_i", [P, TILES], I32)
        src_i = m.sb("src_i", [P, TILES], I32)
        reach = m.sb("reach", [P, 2])
        first = m.sb("first", [P, BLOCKS])
        last = m.sb("last", [P, BLOCKS])
        hit = m.sb("hit", [P, 2, BLOCKS])
        rank = m.sb("rank", [P, 2])
        found = m.sb("found", [P, P])
        most = m.sb("most", [P, 1])
        limits = m.sb("limits", [1, 2 * BLOCKS])
        found_t = m.ps("found_t", [P, P])
        most_t = m.ps("most_t", [1, P])
        loaded = m.sem("loaded")
        made = m.sem("made")
        step = m.sem("step")
        turned = m.sem("turned")
        ident_step = m.sem("ident_step")
        block = m.block()

        @block.sync
        def _(sp):
            sp.dma_start(dst_rows[:, :], io["dst_rows"]).then_inc(loaded, 16)
            sp.dma_start(dst_i[:, :], io["dst_cols"]).then_inc(loaded, 16)
            sp.dma_start(src_i[:, :], io["src_cols"]).then_inc(loaded, 16)
            sp.dma_start(g["weight"][:, :], io["weight_cols"]).then_inc(loaded, 16)

        @block.gpsimd
        def _(pool):
            pool.iota(iota_i[:, :], pattern=[[1, ROWS]], base=0, channel_multiplier=0).then_inc(made, 1)
            pool.iota(node_i[:, :], pattern=[[P, BLOCKS]], base=0, channel_multiplier=1).then_inc(made, 1)
            pool.iota(pair_i[:, :], pattern=[[0, 1]], base=0, channel_multiplier=1).then_inc(made, 1)
            pool.memset(g["ident"][:, :], 0.0).then_inc(ident_step, 1)
            pool.wait_ge(ident_step, 1)
            pool.affine_select(out=g["ident"][:, :], in_=g["ident"][:, :], compare_op=ALU.not_equal,
                               fill=1.0, base=0, pattern=[[-1, P]], channel_multiplier=1).then_inc(made, 1)

        @block.vector
        def _(dve):
            n = [0]

            def after(instruction):
                n[0] += 1
                instruction.then_inc(step, 1)
                dve.wait_ge(step, n[0])

            nc.vector.memset(found[:, :], 0.0)
            nc.vector.memset(g["eps"][:, :], EPS)
            nc.vector.memset(g["rms_eps"][:, :], RMS_EPS)
            nc.vector.memset(g["one"][:, :], 1.0)
            dve.wait_ge(made, 4)
            nc.vector.tensor_copy(g["iota"][:, :], iota_i[:, :])
            nc.vector.tensor_copy(g["ident_r"][:, :], g["ident"][:, :])
            nc.vector.tensor_copy(g["ident_b"][:, :], g["ident"][:, :])
            nc.vector.tensor_copy(g["node"][:, :], node_i[:, :])
            nc.vector.tensor_scalar(rank[:, 0:1], pair_i[:, :], -1.0, FAR, ALU.mult, ALU.add)
            nc.vector.tensor_scalar(rank[:, 1:2], pair_i[:, :], 1.0, None, ALU.add)
            after(nc.vector.tensor_copy(
                first[:, :], iota_i[:, :].rearrange("p (b n) -> p b n", n=P)[:, :, 0]))
            dve.wait_ge(loaded, 64)
            nc.vector.tensor_scalar(last[:, :], first[:, :], float(P - 1), None, ALU.add)
            nc.vector.tensor_copy(g["dst"][:, :], dst_i[:, :])
            nc.vector.tensor_copy(g["src"][:, :], src_i[:, :])
            nc.vector.tensor_copy(g["src_index"][:, :], src_i[:, :])
            nc.vector.tensor_reduce(reach[:, 0:1], dst_rows[:, :], AX.X, ALU.min)
            nc.vector.tensor_reduce(reach[:, 1:2], dst_rows[:, :], AX.X, ALU.max)
            after(nc.vector.tensor_copy(g["weight_hi"][:, :], g["weight"][:, :]))
            nc.vector.tensor_tensor(g["weight_lo"][:, :], g["weight"][:, :],
                                    g["weight_hi"][:, :].bitcast(F32), ALU.subtract)
            nc.vector.tensor_scalar(hit[:, 0, :], last[:, :], reach[:, 0:1], None, ALU.is_ge)
            after(nc.vector.tensor_scalar(hit[:, 1, :], first[:, :], reach[:, 1:2], None, ALU.is_le))
            after(nc.vector.tensor_tensor(hit[:, 0, :], hit[:, 0, :], hit[:, 1, :], ALU.mult))
            nc.vector.tensor_scalar(found[:, 0:BLOCKS], hit[:, 0, :], rank[:, 0:1], None, ALU.mult)
            nc.vector.tensor_scalar(found[:, BLOCKS:2 * BLOCKS], hit[:, 0, :], rank[:, 1:2], None,
                                    ALU.mult).then_inc(made, 1)
            dve.wait_ge(turned, 1)
            nc.vector.tensor_reduce(most[:, :], found_t[:, :], AX.X, ALU.max).then_inc(made, 1)
            dve.wait_ge(turned, 2)
            nc.vector.tensor_scalar(limits[:, 0:BLOCKS], most_t[:, 0:BLOCKS], -1.0, FAR, ALU.mult, ALU.add)
            after(nc.vector.tensor_copy(limits[:, BLOCKS:], most_t[:, BLOCKS:2 * BLOCKS]))
            after(nc.vector.tensor_scalar(limits[:, 0:BLOCKS], limits[:, 0:BLOCKS], float(PAIRS - 1), None,
                                          ALU.min))
            after(nc.vector.scalar_tensor_tensor(out=limits[:, BLOCKS:], in0=limits[:, 0:BLOCKS], scalar=1.0,
                                                 in1=limits[:, BLOCKS:], op0=ALU.add, op1=ALU.max))
            nc.vector.tensor_copy(g["range"][:, :], limits[:, :])

        @block.tensor
        def _(pe):
            pe.wait_ge(made, 5)
            nc.tensor.transpose(found_t[:, :], found[:, :], g["ident"][:, :]).then_inc(turned, 1)
            pe.wait_ge(made, 6)
            nc.tensor.matmul(most_t[:, :], most[:, :], g["ident"][:, :], start=True, stop=True)\
                .then_inc(turned, 1)


def pair_range(engine, g, j):
    first = engine.value_load(g["range"][0:1, bass.ds(j, 1)], min_val=0, max_val=PAIRS - 1)
    end = engine.value_load(g["range"][0:1, bass.ds(j + BLOCKS, 1)], min_val=1, max_val=PAIRS)
    return first, end


def build_graph(nc, g, wt_hi, wt_lo):
    SLOTS = 2
    with ExitStack() as ctx:
        m = Memory(nc, ctx, "build")
        src_hot = m.sb("src_hot", [P, SLOTS, ROWS], F32R)
        dst_hot = m.sb("dst_hot", [P, SLOTS, P], F32R)
        dst_whi = m.sb("dst_whi", [P, SLOTS, P], F32R)
        dst_wlo = m.sb("dst_wlo", [P, SLOTS, P], F32R)
        zero = m.sb("zero", [P, HALF], F32R)
        counts = m.sb("counts", [P, ROWS])
        counts_t = m.sb("counts_t", [P, BLOCKS, P], F32R)
        count_ps = m.ps("count_ps", [P, 3 * HALF])
        weight_ps = m.ps("weight_ps", [P, 2 * HALF])
        turn_ps = m.ps("turn_ps", [P, 3 * HALF])
        zeroed = m.sem("zeroed")
        hot_ready = m.sems("hot_ready")
        hot_free = m.sems("hot_free")
        summed = m.sem("summed")
        weight_out = m.sem("weight_out")
        weight_hi_out = m.sem("weight_hi_out")
        counts_out = m.sem("counts_out")
        turned = m.sem("turned")
        turn_out = m.sem("turn_out")
        turn_stored = m.sem("turn_stored")
        WIDTHS = [(0, HALF), (HALF, HALF), (2 * HALF, ROWS - 2 * HALF)]
        block = m.block()
        PARTS = ((0, KB, True), (KB, BLOCKS, False))

        @block.sync
        def _(sp):
            sp.sem_inc(turn_stored, 16)
            with sp.Fori(0, BLOCKS) as j:
                c = sp.snap(j + 2)
                sp.wait_ge(turn_out, c)
                sp.dma_start(g["counts_d"][bass.ds(j * P, P), :],
                             counts_t[:, :, :].rearrange("p b n -> p (b n)").bitcast(F32)).then_inc(turn_stored, 16)
            sp.wait_ge(turn_stored, 16 * (BLOCKS + 1))

        @block.vector
        def _(dve):
            nc.vector.memset(zero[:, :].bitcast(F32), 0.0).then_inc(zeroed, 1)
            done = dve.alloc_register("build_dve")
            dve.reg_mov(done, 1)
            for j0, j1, with_weight in PARTS:
                with dve.Fori(j0, j1) as j:
                    first, end = pair_range(dve, g, j)
                    with dve.Fori(first, end) as i:
                        c = dve.snap(done)
                        for u in range(SLOTS):
                            t = i * 2 + u
                            src_t = g["src"][:, bass.ds(t, 1)]
                            dst_t = g["dst"][:, bass.ds(t, 1)]
                            nodes = g["iota"][:, bass.ds(j * P, P)]
                            dve.wait_ge(hot_free[u], c)
                            nc.vector.tensor_scalar(dst_hot[:, u, :], nodes, dst_t, None, ALU.is_equal)
                            if with_weight:
                                nc.vector.tensor_scalar(dst_whi[:, u, :], nodes, dst_t,
                                                        g["weight_hi"][:, bass.ds(t, 1)].bitcast(F32),
                                                        ALU.is_equal, ALU.mult)
                                nc.vector.tensor_scalar(dst_wlo[:, u, :], nodes, dst_t,
                                                        g["weight_lo"][:, bass.ds(t, 1)].bitcast(F32),
                                                        ALU.is_equal, ALU.mult)
                            nc.vector.tensor_scalar(src_hot[:, u, :], g["iota"][:, :], src_t, None,
                                                    ALU.is_equal).then_inc(hot_ready[u], 1)
                        dve.reg_add(done, done, 1)
                    c = dve.snap(j + 1)
                    if with_weight:
                        dve.wait_ge(summed, c)
                        nc.vector.tensor_copy(wt_hi[:, bass.ds(j, 1), :], weight_ps[:, :])\
                            .then_inc(weight_hi_out, 1)
                        dve.wait_ge(weight_hi_out, c)
                        nc.vector.tensor_tensor(wt_lo[:, bass.ds(j, 1), :], weight_ps[:, :],
                                                wt_hi[:, bass.ds(j, 1), :].bitcast(F32), ALU.subtract)\
                            .then_inc(weight_out, 1)

        @block.scalar
        def _(act):
            act.sem_inc(turn_out, 1)
            with act.Fori(0, BLOCKS) as j:
                c = act.snap(j + 1)
                c16 = act.snap(j * 16 + 16)
                act.wait_ge(summed, c)
                nc.scalar.activation(counts[:, :], count_ps[:, 0:ROWS], ACT.Copy,
                                     accum_out=g["degree"][:, bass.ds(j, 1)]).then_inc(counts_out, 1)
                act.wait_ge(turned, c)
                act.wait_ge(turn_stored, c16)
                nc.scalar.activation(counts_t[:, :, :], turn_ps[:, 0:ROWS].rearrange("p (b n) -> p b n", n=P),
                                     ACT.Copy).then_inc(turn_out, 1)

        @block.tensor
        def _(pe):
            pe.wait_ge(zeroed, 1)
            for u in range(SLOTS):
                pe.sem_inc(hot_free[u], 1)
            done = pe.alloc_register("build_pe")
            pe.reg_mov(done, 1)
            for j0, j1, with_weight in PARTS:
                with pe.Fori(j0, j1) as j:
                    first, end = pair_range(pe, g, j)
                    for a, w in WIDTHS:
                        nc.tensor.matmul(count_ps[:, a:a + w], zero[:, 0:P], zero[:, 0:w], start=True,
                                         stop=False, skip_group_check=True)
                    if with_weight:
                        for a in (0, HALF):
                            nc.tensor.matmul(weight_ps[:, a:a + HALF], zero[:, 0:P], zero[:, :], start=True,
                                             stop=False, skip_group_check=True)
                    with pe.Fori(first, end) as i:
                        c = pe.snap(done)
                        for u in range(SLOTS):
                            pe.wait_ge(hot_ready[u], c)
                            for a, w in WIDTHS:
                                last = nc.tensor.matmul(count_ps[:, a:a + w], dst_hot[:, u, :],
                                                        src_hot[:, u, a:a + w], start=False, stop=False,
                                                        skip_group_check=True)
                            if with_weight:
                                for part in (dst_whi, dst_wlo):
                                    for a in (0, HALF):
                                        last = nc.tensor.matmul(weight_ps[:, a:a + HALF], part[:, u, :],
                                                                src_hot[:, u, a:a + HALF], start=False,
                                                                stop=False, skip_group_check=True)
                            last.then_inc(hot_free[u], 1)
                        pe.reg_add(done, done, 1)
                    c = pe.snap(j + 1)
                    for a, w in WIDTHS:
                        last = nc.tensor.matmul(count_ps[:, a:a + w], zero[:, 0:P], zero[:, 0:w], start=False,
                                                stop=True, skip_group_check=True)
                    last.then_inc(summed, 1)
                    pe.wait_ge(counts_out, c)
                    pe.wait_ge(turn_out, c)
                    for b in range(BLOCKS):
                        last = nc.tensor.transpose(turn_ps[:, b * P:(b + 1) * P],
                                                   counts[:, b * P:(b + 1) * P], g["ident"][:, :])
                    last.then_inc(turned, 1)
                    if with_weight:
                        pe.wait_ge(weight_out, c)


def skewed(engine, early, late):
    early(0, 0, 1)
    with engine.Fori(0, BLOCKS // 2 - 1) as i:
        n = engine.snap(i + 1)
        more = engine.snap(i + 2)
        early(i * 2 + 1, 1, n)
        late(i * 2, 0, n)
        early(i * 2 + 2, 0, more)
        late(i * 2 + 1, 1, n)
    early(BLOCKS - 1, 1, BLOCKS // 2)
    late(BLOCKS - 2, 0, BLOCKS // 2)
    late(BLOCKS - 1, 1, BLOCKS // 2)


def plain(engine, step):
    with engine.Fori(0, BLOCKS // 2) as i:
        n = engine.snap(i + 1)
        step(i * 2, 0, n)
        step(i * 2 + 1, 1, n)


def times16(engine, n):
    return 16 * n if isinstance(n, int) else engine.snap(n * 16)


def plus(engine, n, k):
    return n + k if isinstance(n, int) else engine.snap(n + k)


def rows(dram, tile):
    return dram[bass.ds(tile * P, P), :]


class Moves:

    def __init__(self, m):
        self.m, self.loads, self.store_of = m, [], None

    def load(self, name, dram, shape, dtype=F32):
        tiles = self.m.sb(name, [P, 2] + shape, dtype)
        ready, free = self.m.sems(f"{name}_ready"), self.m.sems(f"{name}_free")
        self.loads.append((dram, tiles, ready, free))
        return tiles, ready, free

    def store(self, name, dram):
        tiles = self.m.sb(name, [P, 2, FEAT])
        ready, stored = self.m.sems(f"{name}_ready"), self.m.sems(f"{name}_stored")
        self.store_of = (dram, tiles, ready, stored)
        return tiles, ready, stored

    def program(self, sp):
        dram_out, out, ready_out, stored = self.store_of
        for u in range(2):
            sp.sem_inc(stored[u], 16)

        def load(tile, u, n):
            for dram, tiles, ready, free in self.loads:
                sp.wait_ge(free[u], n)
                dst = tiles[:, u]
                if len(dst.shape) == 3:
                    dst = dst.rearrange("p b n -> p (b n)")
                sp.dma_start(dst.bitcast(F32), rows(dram, tile)).then_inc(ready[u], 16)

        def store(tile, u, n):
            sp.wait_ge(ready_out[u], n)
            sp.dma_start(rows(dram_out, tile), out[:, u, :]).then_inc(stored[u], 16)

        load(0, 0, 1)
        load(1, 1, 1)
        with sp.Fori(1, BLOCKS // 2) as i:
            n = sp.snap(i + 1)
            before = sp.snap(i)
            for u in range(2):
                load(i * 2 + u, u, n)
                store(i * 2 - 2 + u, u, before)
        for u in range(2):
            store(BLOCKS - 2 + u, u, BLOCKS // 2)
        for u in range(2):
            sp.wait_ge(stored[u], 16 * (BLOCKS // 2 + 1))


class WeightSplit:

    def __init__(self, m, name, dram, width, blocks=KB, scale=None):
        self.dram, self.width, self.blocks, self.scale = dram, width, blocks, scale
        self.hi = m.sb(f"{name}_hi", [P, blocks, width], F32R)
        self.lo = m.sb(f"{name}_lo", [P, blocks, width], F32R)
        self.raw = m.sb(f"{name}_raw", [P, 2, width])
        self.raw_ready = m.sems(f"{name}_raw_ready")
        self.raw_free = m.sem(f"{name}_raw_free")
        self.hi_ready = m.sem(f"{name}_hi_ready")

    def load(self, sp):
        for k in range(self.blocks):
            if k >= 2:
                sp.wait_ge(self.raw_free, k - 1)
            sp.dma_start(self.raw[:, k % 2, :], self.dram[k * P:(k + 1) * P, :])\
                .then_inc(self.raw_ready[k % 2], 16)

    def high(self, act, nc):
        for k in range(self.blocks):
            act.wait_ge(self.raw_ready[k % 2], 16 * (k // 2 + 1))
            scale = 1.0 if self.scale is None else self.scale[:, k:k + 1]
            nc.scalar.activation(self.hi[:, k, :], self.raw[:, k % 2, :], ACT.Copy, scale=scale)\
                .then_inc(self.hi_ready, 1)

    def low(self, dve, nc):
        for k in range(self.blocks):
            dve.wait_ge(self.hi_ready, k + 1)
            scale = 1.0 if self.scale is None else self.scale[:, k:k + 1]
            nc.vector.scalar_tensor_tensor(out=self.lo[:, k, :], in0=self.raw[:, k % 2, :], scalar=scale,
                                           in1=self.hi[:, k, :].bitcast(F32), op0=ALU.mult,
                                           op1=ALU.subtract).then_inc(self.raw_free, 1)

    def wait(self, pe):
        pe.wait_ge(self.raw_free, self.blocks)


def product(nc, out, hi, lo, w_hi, w_lo, blocks=KB, width=FEAT):
    step = min(width, HALF)
    for a in range(0, width, step):
        terms = [(x, w, k) for k in range(blocks) for x, w in ((hi, w_hi), (hi, w_lo), (lo, w_hi))]
        for t, (x, w, k) in enumerate(terms):
            last = nc.tensor.matmul(out[:, a:a + step], x[:, k, :], w[:, k, a:a + step], start=(t == 0),
                                    stop=(t == len(terms) - 1))
    return last


class Norm:

    def __init__(self, m):
        self.stats = m.sb("ln_stats", [P, 2, 6])
        self.mean_var = m.sb("ln_mean_var", [P, 2])
        self.rstd = m.sb("ln_rstd", [P, 1])
        self.var_ready, self.std_ready = m.sem("ln_var_ready"), m.sem("ln_std_ready")

    def root(self, act, nc, g, n):
        act.wait_ge(self.var_ready, n)
        nc.scalar.activation(self.rstd[:, :], self.mean_var[:, 1:2], ACT.Sqrt, bias=g["eps"][:, :])\
            .then_inc(self.std_ready, 1)

    def program(self, dve, nc, out, x, n):
        for h in range(2):
            nc.vector.bn_stats(self.stats[:, h, :], x[:, h * HALF:(h + 1) * HALF])
        dve.drain()
        nc.vector.bn_aggr(self.mean_var[:, :], self.stats[:, :, :]).then_inc(self.var_ready, 1)
        dve.wait_ge(self.std_ready, n)
        nc.vector.reciprocal(self.rstd[:, :], self.rstd[:, :])
        dve.drain()
        return nc.vector.tensor_scalar(out, x, self.mean_var[:, 0:1], self.rstd[:, :], ALU.subtract,
                                       ALU.mult)


def dense_stage(nc, g, name, x_d, y_d, bias_d, weight_d=None, weight_parts=None, parts_out=None):
    with ExitStack() as ctx:
        m = Memory(nc, ctx, name)
        w = WeightSplit(m, "w", weight_d, FEAT) if weight_parts is None else None
        w_hi, w_lo = (w.hi, w.lo) if w else weight_parts
        moves = Moves(m)
        x, x_ready, x_free = moves.load("x", x_d, [FEAT])
        y, y_ready, y_stored = moves.store("y", y_d)
        bias = m.sb("bias", [P, FEAT])
        xt_hi = m.sb("xt_hi", [P, 2, KB, P], F32R)
        xt_lo = m.sb("xt_lo", [P, 2, KB, P], F32R)
        norm = Norm(m) if weight_parts else None
        xt_ps = [m.ps(f"xt_ps{u}", [P, KB * P]) for u in range(2)]
        y_ps = [m.ps(f"y_ps{u}", [P, FEAT]) for u in range(2)]
        bias_ready = m.sem("bias_ready")
        turned = m.sems("turned")
        hi_ready = m.sems("hi_ready")
        lo_ready = m.sems("lo_ready")
        multiplied = m.sems("multiplied")
        y_ps_free = m.sems("y_ps_free")
        hi_kept = m.sems("hi_kept")
        block = m.block()

        @block.sync
        def _(sp):
            sp.dma_start(bias[:, :], bias_d.partition_broadcast(P)).then_inc(bias_ready, 16)
            if w:
                w.load(sp)
            moves.program(sp)

        @block.tensor
        def _(pe):
            for u in range(2):
                pe.sem_inc(multiplied[u], 1)

            def turn(tile, u, n):
                pe.wait_ge(x_ready[u], times16(pe, n))
                for k in range(KB):
                    last = nc.tensor.transpose(xt_ps[u][:, k * P:(k + 1) * P], x[:, u, k * P:(k + 1) * P],
                                               g["ident"][:, :])
                last.then_inc(turned[u], 1)

            def multiply(tile, u, n):
                pe.wait_ge(lo_ready[u], n)
                pe.wait_ge(y_ps_free[u], n)
                product(nc, y_ps[u], xt_hi[:, u], xt_lo[:, u], w_hi, w_lo).then_inc(multiplied[u], 1)

            if w:
                w.wait(pe)
            skewed(pe, turn, multiply)

        @block.scalar
        def _(act):
            if w:
                w.high(act, nc)

            def early(tile, u, n):
                act.wait_ge(turned[u], n)
                act.wait_ge(multiplied[u], n)
                nc.scalar.activation(xt_hi[:, u].rearrange("p b n -> p (b n)"), xt_ps[u][:, :], ACT.Copy)\
                    .then_inc(hi_ready[u], 1)

            def keep(tile, u, n):
                early(tile, u, n)
                nc.scalar.activation(parts_out[0][:, bass.ds(tile, 1), :], x[:, u, :], ACT.Copy)\
                    .then_inc(hi_kept[u], 1)

            if norm:
                skewed(act, early, lambda tile, u, n: norm.root(act, nc, g, plus(act, tile, 1)))
            else:
                plain(act, keep if parts_out else early)

        @block.vector
        def _(dve):
            if w:
                w.low(dve, nc)
            for u in range(2):
                dve.sem_inc(y_ps_free[u], 1)
                dve.sem_inc(x_free[u], 1)
            dve.wait_ge(bias_ready, 16)

            def early(tile, u, n):
                dve.wait_ge(hi_ready[u], n)
                nc.vector.tensor_tensor(xt_lo[:, u].rearrange("p b n -> p (b n)"), xt_ps[u][:, :],
                                        xt_hi[:, u].rearrange("p b n -> p (b n)").bitcast(F32),
                                        ALU.subtract).then_inc(lo_ready[u], 1)

            def late(tile, u, n):
                more, whole = plus(dve, n, 1), plus(dve, tile, 1)
                if parts_out:
                    dve.wait_ge(hi_kept[u], n)
                    nc.vector.tensor_tensor(parts_out[1][:, bass.ds(tile, 1), :], x[:, u, :],
                                            parts_out[0][:, bass.ds(tile, 1), :].bitcast(F32), ALU.subtract)\
                        .then_inc(x_free[u], 1)
                dve.wait_ge(y_stored[u], times16(dve, n))
                dve.wait_ge(multiplied[u], more)
                nc.vector.tensor_tensor(y[:, u, :], y_ps[u][:, :], bias[:, :], ALU.add)\
                    .then_inc(y_ps_free[u], 1)
                if norm:
                    dve.drain()
                    nc.vector.tensor_tensor(y[:, u, :], y[:, u, :], x[:, u, :], ALU.add)\
                        .then_inc(x_free[u], 1)
                    dve.drain()
                    norm.program(dve, nc, y[:, u, :], y[:, u, :], whole).then_inc(y_ready[u], 1)
                else:
                    dve.drain()
                    dve.sem_inc(y_ready[u], 1)

            skewed(dve, early, late)


def graph_stage(nc, g, name, parts, y_d, weight_d, scale, kind, added_d=None, bias_d=None, x_d=None):
    with ExitStack() as ctx:
        m = Memory(nc, ctx, name)
        w = WeightSplit(m, "w", weight_d, FEAT)
        moves = Moves(m)
        counts, counts_ready, counts_free = moves.load("counts", g["counts_d"], [BLOCKS, P], F32R)
        if kind != "gcn":
            added, added_ready, added_free = moves.load("added", added_d, [FEAT])
        if kind != "hidden":
            x, x_ready, x_free = moves.load("x", x_d, [FEAT])
        y, y_ready, y_stored = moves.store("y", y_d)
        if kind == "gcn":
            bias = m.sb("bias", [P, FEAT])
            bias_ready = m.sem("bias_ready")
        mean = m.sb("mean", [P, FEAT])
        mean_hi = m.sb("mean_hi", [P, KB, P], F32R)
        mean_lo = m.sb("mean_lo", [P, KB, P], F32R)
        norm = Norm(m) if kind != "hidden" else None
        sum_ps = m.ps("sum_ps", [P, FEAT])
        turn_ps = m.ps("turn_ps", [P, KB * P])
        y_ps = [m.ps(f"y_ps{u}", [P, FEAT]) for u in range(2)]
        mean_ready = m.sem("mean_ready")
        turned = m.sem("turned")
        hi_ready = m.sem("hi_ready")
        lo_ready = m.sem("lo_ready")
        multiplied = m.sems("multiplied")
        y_ps_free = m.sems("y_ps_free")
        ready_to_relu = m.sems("ready_to_relu")
        block = m.block()

        @block.sync
        def _(sp):
            if kind == "gcn":
                sp.dma_start(bias[:, :], bias_d.partition_broadcast(P)).then_inc(bias_ready, 16)
            w.load(sp)
            moves.program(sp)

        @block.tensor
        def _(pe):
            def add_up(tile, u, n):
                whole, n16 = plus(pe, tile, 1), times16(pe, n)
                pe.wait_ge(counts_ready[u], n16)
                pe.wait_ge(mean_ready, whole)
                for a in (0, HALF):
                    terms = [(counts[:, u, k, :], part[:, k, a:a + HALF]) for part in parts
                             for k in range(BLOCKS)]
                    if kind == "gcn":
                        terms += [(g["ident_r"][:, :],
                                   part[:, bass.ds(tile, 1), a:a + HALF].rearrange("p b n -> p (b n)"))
                                  for part in parts]
                    for t, (c, r) in enumerate(terms):
                        last = nc.tensor.matmul(sum_ps[:, a:a + HALF], c, r, start=(t == 0),
                                                stop=(t == len(terms) - 1))
                last.then_inc(counts_free[u], 1)

            def turn(tile, u, n):
                whole = plus(pe, tile, 2)
                pe.wait_ge(mean_ready, whole)
                for k in range(KB):
                    last = nc.tensor.transpose(turn_ps[:, k * P:(k + 1) * P], mean[:, k * P:(k + 1) * P],
                                               g["ident"][:, :])
                last.then_inc(turned, 1)

            def multiply(tile, u, n):
                whole = plus(pe, tile, 1)
                pe.wait_ge(lo_ready, whole)
                pe.wait_ge(y_ps_free[u], n)
                product(nc, y_ps[u], mean_hi, mean_lo, w.hi, w.lo).then_inc(multiplied[u], 1)

            pe.sem_inc(mean_ready, 1)
            add_up(0, 0, 1)
            w.wait(pe)
            with pe.Fori(0, BLOCKS // 2 - 1) as i:
                n = pe.snap(i + 1)
                more = pe.snap(i + 2)
                turn(i * 2, 0, n)
                add_up(i * 2 + 1, 1, n)
                multiply(i * 2, 0, n)
                turn(i * 2 + 1, 1, n)
                add_up(i * 2 + 2, 0, more)
                multiply(i * 2 + 1, 1, n)
            turn(BLOCKS - 2, 0, BLOCKS // 2)
            add_up(BLOCKS - 1, 1, BLOCKS // 2)
            multiply(BLOCKS - 2, 0, BLOCKS // 2)
            turn(BLOCKS - 1, 1, BLOCKS // 2)
            multiply(BLOCKS - 1, 1, BLOCKS // 2)

        @block.scalar
        def _(act):
            w.high(act, nc)

            def take_mean(tile, u, n):
                more = plus(act, n, 1)
                done = plus(act, tile, 1)
                act.wait_ge(counts_free[u], more)
                act.wait_ge(turned, done)
                nc.scalar.activation(mean[:, :], sum_ps[:, :], ACT.Copy, scale=scale[:, bass.ds(tile, 1)])\
                    .then_inc(mean_ready, 1)

            def take_turned(tile, u, n):
                more = plus(act, tile, 2)
                act.wait_ge(turned, more)
                act.wait_ge(multiplied[1 - u], n)
                nc.scalar.activation(mean_hi[:, :, :].rearrange("p b n -> p (b n)"), turn_ps[:, :], ACT.Copy)\
                    .then_inc(hi_ready, 1)

            def root(tile):
                if norm:
                    norm.root(act, nc, g, plus(act, tile, 1))

            for u in range(2):
                act.sem_inc(counts_free[u], 1)
            act.sem_inc(turned, 1)
            act.sem_inc(multiplied[1], 1)
            take_mean(0, 0, 1)
            with act.Fori(0, BLOCKS // 2 - 1) as i:
                n = act.snap(i + 1)
                more = act.snap(i + 2)
                take_turned(i * 2, 0, n)
                take_mean(i * 2 + 1, 1, n)
                root(i * 2)
                take_turned(i * 2 + 1, 1, n)
                take_mean(i * 2 + 2, 0, more)
                root(i * 2 + 1)
            take_turned(BLOCKS - 2, 0, BLOCKS // 2)
            take_mean(BLOCKS - 1, 1, BLOCKS // 2)
            root(BLOCKS - 2)
            take_turned(BLOCKS - 1, 1, BLOCKS // 2)
            root(BLOCKS - 1)

        @block.vector
        def _(dve):
            w.low(dve, nc)
            for u in range(2):
                dve.sem_inc(y_ps_free[u], 1)
                if kind != "gcn":
                    dve.sem_inc(added_free[u], 1)
                if kind != "hidden":
                    dve.sem_inc(x_free[u], 1)
            if kind == "gcn":
                dve.wait_ge(bias_ready, 16)

            def step(tile, u, n):
                whole = dve.snap(tile + 1)
                more = dve.snap(n + u)
                n16 = times16(dve, n)
                dve.wait_ge(hi_ready, whole)
                nc.vector.tensor_tensor(mean_lo[:, :, :].rearrange("p b n -> p (b n)"), turn_ps[:, :],
                                        mean_hi[:, :, :].rearrange("p b n -> p (b n)").bitcast(F32),
                                        ALU.subtract).then_inc(lo_ready, 1)
                out = y[:, u, :]
                dve.wait_ge(y_stored[u], n16)
                if kind == "gcn":
                    dve.wait_ge(x_ready[u], n16)
                    dve.wait_ge(multiplied[u], more)
                    nc.vector.tensor_tensor(out, y_ps[u][:, :], bias[:, :], ALU.add)\
                        .then_inc(y_ps_free[u], 1)
                    dve.drain()
                    nc.vector.scalar_tensor_tensor(out=out, in0=out, scalar=0.0, in1=x[:, u, :], op0=ALU.max,
                                                   op1=ALU.add).then_inc(x_free[u], 1)
                else:
                    dve.wait_ge(added_ready[u], n16)
                    dve.wait_ge(multiplied[u], more)
                    nc.vector.tensor_tensor(out, y_ps[u][:, :], added[:, u, :], ALU.add)\
                        .then_inc(y_ps_free[u], 1)
                    dve.drain()
                    dve.sem_inc(added_free[u], 1)
                    if kind == "hidden":
                        nc.vector.tensor_scalar(out, out, 0.0, None, ALU.max).then_inc(y_ready[u], 1)
                        return
                    dve.wait_ge(x_ready[u], n16)
                    nc.vector.tensor_tensor(out, out, x[:, u, :], ALU.add).then_inc(x_free[u], 1)
                dve.drain()
                norm.program(dve, nc, out, out, whole).then_inc(y_ready[u], 1)

            plain(dve, step)


def project_stage(nc, g, x_d, rms_d, down_d, left_d, right_d, xl_d, xr):
    with ExitStack() as ctx:
        m = Memory(nc, ctx, "project")
        rms_w = m.sb("rms_w", [P, KB])
        w = WeightSplit(m, "down", down_d, HID, scale=rms_w)
        KH = HID // P
        left = WeightSplit(m, "left", left_d, HID, blocks=KH)
        right = WeightSplit(m, "right", right_d, HID, blocks=KH)
        x = m.sb("x", [P, 2, FEAT])
        square = m.sb("square", [P, FEAT])
        rms = m.sb("rms", [P, 2])
        down = m.sb("down", [P, HID])
        xl = m.sb("xl", [P, 2, HID])
        xt_hi = m.sb("xt_hi", [P, KB, P], F32R)
        xt_lo = m.sb("xt_lo", [P, KB, P], F32R)
        dt_hi = m.sb("dt_hi", [P, KH, P], F32R)
        dt_lo = m.sb("dt_lo", [P, KH, P], F32R)
        xt_ps = m.ps("xt_ps", [P, KB * P])
        down_ps = m.ps("down_ps", [P, HID])
        dt_ps = m.ps("dt_ps", [P, HID])
        xl_ps = m.ps("xl_ps", [P, HID])
        xr_ps = m.ps("xr_ps", [P, HID])
        names = "rms_ready turned squared hi_ready lo_ready multiplied down_ready down_turned dt_hi_ready " \
                "dt_lo_ready xl_whole xl_ready xr_ready"
        s = {n: m.sem(n) for n in names.split()}
        x_ready = m.sems("x_ready")
        xl_stored = m.sems("xl_stored")
        block = m.block()

        @block.sync
        def _(sp):
            sp.dma_start(rms_w[:, :], rms_d).then_inc(s["rms_ready"], 16)
            for u in range(2):
                sp.sem_inc(xl_stored[u], 16)
                sp.dma_start(x[:, u, :], rows(x_d, u)).then_inc(x_ready[u], 16)
            w.load(sp)
            left.load(sp)
            right.load(sp)

            def store(tile, u):
                sp.wait_ge(s["xl_ready"], tile + 1 if isinstance(tile, int) else sp.snap(tile + 1))
                sp.dma_start(rows(xl_d, tile), xl[:, u, :]).then_inc(xl_stored[u], 16)

            with sp.Fori(0, BLOCKS // 2 - 1) as i:
                for u in range(2):
                    store(i * 2 + u, u)
                    sp.dma_start(x[:, u, :], rows(x_d, i * 2 + 2 + u)).then_inc(x_ready[u], 16)
            for u in range(2):
                store(BLOCKS - 2 + u, u)
            for u in range(2):
                sp.wait_ge(xl_stored[u], 16 * (BLOCKS // 2 + 1))

        @block.tensor
        def _(pe):
            for split in (w, left, right):
                split.wait(pe)

            def step(tile, u, n):
                c = pe.snap(tile + 1)
                pe.wait_ge(x_ready[u], times16(pe, n))
                for k in range(KB):
                    last = nc.tensor.transpose(xt_ps[:, k * P:(k + 1) * P], x[:, u, k * P:(k + 1) * P],
                                               g["ident"][:, :])
                last.then_inc(s["turned"], 1)
                pe.wait_ge(s["lo_ready"], c)
                product(nc, down_ps, xt_hi, xt_lo, w.hi, w.lo, width=HID).then_inc(s["multiplied"], 1)
                pe.wait_ge(s["down_ready"], c)
                for k in range(KH):
                    last = nc.tensor.transpose(dt_ps[:, k * P:(k + 1) * P], down[:, k * P:(k + 1) * P],
                                               g["ident"][:, :])
                last.then_inc(s["down_turned"], 1)
                pe.wait_ge(s["dt_lo_ready"], c)
                pe.wait_ge(s["xr_ready"], c)
                product(nc, xl_ps, dt_hi, dt_lo, left.hi, left.lo, blocks=KH, width=HID)
                product(nc, xr_ps, dt_hi, dt_lo, right.hi, right.lo, blocks=KH, width=HID)\
                    .then_inc(s["xl_whole"], 1)

            plain(pe, step)

        @block.scalar
        def _(act):
            act.wait_ge(s["rms_ready"], 16)
            for split in (w, left, right):
                split.high(act, nc)

            def step(tile, u, n):
                c = act.snap(tile + 1)
                act.wait_ge(x_ready[u], times16(act, n))
                act.wait_ge(s["turned"], c)
                nc.scalar.activation(xt_hi[:, :, :].rearrange("p b n -> p (b n)"), xt_ps[:, :], ACT.Copy)\
                    .then_inc(s["hi_ready"], 1)
                nc.scalar.activation(square[:, :], x[:, u, :], ACT.Square, accum_out=rms[:, 0:1])
                act.drain()
                nc.scalar.activation(rms[:, 1:2], rms[:, 0:1], ACT.Sqrt, scale=1.0 / FEAT,
                                     bias=g["rms_eps"][:, :]).then_inc(s["squared"], 1)
                act.wait_ge(s["down_turned"], c)
                nc.scalar.activation(dt_hi[:, :, :].rearrange("p b n -> p (b n)"), dt_ps[:, :], ACT.Copy)\
                    .then_inc(s["dt_hi_ready"], 1)
                act.wait_ge(s["xl_whole"], c)
                act.wait_ge(xl_stored[u], times16(act, n))
                nc.scalar.activation(xl[:, u, :], xl_ps[:, :], ACT.Copy).then_inc(s["xl_ready"], 1)

            plain(act, step)

        @block.vector
        def _(dve):
            dve.sem_inc(s["xr_ready"], 1)
            for split in (w, left, right):
                split.low(dve, nc)

            def step(tile, u, n):
                c = dve.snap(tile + 1)
                dve.wait_ge(s["hi_ready"], c)
                nc.vector.tensor_tensor(xt_lo[:, :, :].rearrange("p b n -> p (b n)"), xt_ps[:, :],
                                        xt_hi[:, :, :].rearrange("p b n -> p (b n)").bitcast(F32),
                                        ALU.subtract).then_inc(s["lo_ready"], 1)
                dve.wait_ge(s["squared"], c)
                nc.vector.reciprocal(rms[:, 1:2], rms[:, 1:2])
                dve.drain()
                dve.wait_ge(s["multiplied"], c)
                nc.vector.tensor_scalar(down[:, :], down_ps[:, :], rms[:, 1:2], None, ALU.mult)\
                    .then_inc(s["down_ready"], 1)
                dve.wait_ge(s["dt_hi_ready"], c)
                nc.vector.tensor_tensor(dt_lo[:, :, :].rearrange("p b n -> p (b n)"), dt_ps[:, :],
                                        dt_hi[:, :, :].rearrange("p b n -> p (b n)").bitcast(F32),
                                        ALU.subtract).then_inc(s["dt_lo_ready"], 1)
                dve.wait_ge(s["xl_whole"], c)
                nc.vector.tensor_copy(xr[:, bass.ds(tile, 1), :].rearrange("p b n -> p (b n)"), xr_ps[:, :])\
                    .then_inc(s["xr_ready"], 1)

            plain(dve, step)


def gather_stage(nc, g, xl_d, edge_xl_d):
    SLOTS = len(g["gathered"])
    with ExitStack() as ctx:
        m = Memory(nc, ctx, "gather")
        index = [m.sb(f"index{u}", [P, 1], I32) for u in range(SLOTS)]
        got = [m.sb(f"got{u}", [P, HID]) for u in range(SLOTS)]
        index_ready = m.sems("index_ready", SLOTS)
        gathered = g["gathered"]
        stored = m.sems("stored", SLOTS)
        passed = m.sem("passed")
        block = m.block()

        @block.vector
        def _(dve):
            with dve.Fori(0, TILES // SLOTS) as i:
                n16 = dve.snap(i * 16 + 16)
                for u in range(SLOTS):
                    dve.wait_ge(stored[u], n16)
                    nc.vector.tensor_copy(index[u][:, :], g["src_index"][:, bass.ds(i * SLOTS + u, 1)])\
                        .then_inc(index_ready[u], 1)

        @block.gpsimd
        def _(pool):
            for u in range(SLOTS):
                pool.sem_inc(stored[u], 16)
            with pool.Fori(0, TILES // SLOTS) as i:
                n = pool.snap(i + 1)
                n16 = pool.snap(i * 16 + 16)
                for u in range(SLOTS):
                    pool.wait_ge(index_ready[u], n)
                    pool.wait_ge(stored[u], n16)
                    pool.sem_inc(passed, 1)
                    pool.indirect_dma_start(got[u][:, :], None, xl_d,
                                            bass.IndirectOffsetOnAxis(index[u][:, :], 0))\
                        .then_inc(gathered[u], 16)

        @block.sync
        def _(sp):
            with sp.Fori(0, TILES // SLOTS) as i:
                n16 = sp.snap(i * 16 + 16)
                for u in range(SLOTS):
                    sp.wait_ge(gathered[u], n16)
                    sp.dma_start(edge_xl_d[bass.ds((i * SLOTS + u) * P, P), :], got[u][:, :])\
                        .then_inc(stored[u], 16)
            for u in range(SLOTS):
                sp.wait_ge(stored[u], 16 * (TILES // SLOTS + 1))


def attention_stage(nc, g, att_d, dst_pairs_d, edge_xl_d, xr, mixed_d):
    KH = HID // P
    with ExitStack() as ctx:
        m = Memory(nc, ctx, "attention")
        att = m.sb("att", [P, KH])
        ones = m.sb("ones", [P, P])
        att_wide = m.sb("att_wide", [P, HEADS, P], F32R)
        att_cols = m.sb("att_cols", [P, KH, HEADS])
        dst_all = m.sb("dst_all", [P, (PAIRS + BLOCKS) * PAIR], I32)
        xr_hi = m.sb("xr_hi", [P, HID], F32R)
        xr_lo = m.sb("xr_lo", [P, HID], F32R)
        scores = m.sb("scores", [P, TILES, HEADS])
        rows_in = m.sb("rows_in", [P, 2, HID])
        hot_t = m.sb("hot_t", [P, PAIR], F32R)
        mask = m.sb("mask", [P, PAIR], BF16)
        scaled = m.sb("scaled", [P, KH * PAIR])
        bent = m.sb("bent", [P, KH, PAIR])
        bent_r = m.sb("bent_r", [P, KH, PAIR], F32R)
        tile_max = m.sb("tile_max", [P, HEADS])
        node_max = m.sb("node_max", [P, HEADS])
        rows_mix = m.sb("rows_mix", [P, 2, HID])
        hot_max = m.sb("hot_max", [P, PAIR])
        hot = m.sb("hot", [P, 2, P])
        shifted = m.sb("shifted", [P, 2, HEADS])
        weighted = m.sb("weighted", [P, 2, HID + HEADS])
        zero = m.sb("zero", [P, HID + HEADS])
        inverse = m.sb("inverse", [P, HEADS])
        mixed = m.sb("mixed", [P, HID])
        mixed_stored = m.sem("mixed_stored")
        message_ps = m.ps("message_ps", [P, KH, PAIR])
        spread_ps = m.ps("spread_ps", [P, HEADS, PAIR])
        score_ps = m.ps("score_ps", [P, 2, HEADS])
        max_ps = m.ps("max_ps", [P, 2, HEADS])
        mix_ps = m.ps("mix_ps", [P, HID + HEADS])
        names = "loaded wide_zeroed wide_ready xr_ready hot_ready message_ready scaled_ready bent_ready " \
                "bent_r_ready spread_ready score_kept maxed rows_ready rows_free"
        s = {n: m.sem(n) for n in names.split()}
        names = "rows_ready hot_max_ready max_spread shift_ready exp_ready weighted_ready mixed_in block_mixed " \
                "block_out"
        b = {n: m.sem(f"mix_{n}") for n in names.split()}
        block = m.block()

        def per_block(engine, score_step, mix_step, begin=None, middle=None, finish=None):
            count = engine.alloc_register(f"count_{engine.engine.name}")
            mix_count = engine.alloc_register(f"mix_count_{engine.engine.name}")
            engine.reg_mov(count, 1)
            engine.reg_mov(mix_count, 1)
            with engine.Fori(0, BLOCKS) as j:
                first, end = pair_range(engine, g, j)
                if begin:
                    begin(j)
                for step, counter in ((score_step, count), (mix_step, mix_count)):
                    if step:
                        with engine.Fori(first, end) as i:
                            step(j, i, engine.snap(counter))
                            engine.reg_add(counter, counter, 1)
                        step(j, engine.snap(j + SELF), engine.snap(counter))
                        engine.reg_add(counter, counter, 1)
                    if step is score_step and middle:
                        middle(j, engine.snap(count))
                if finish:
                    finish(j)

        @block.sync
        def _(sp):
            sp.dma_start(att[:, :], att_d).then_inc(s["loaded"], 16)
            sp.dma_start(dst_all[:, :], dst_pairs_d.partition_broadcast(P)).then_inc(s["loaded"], 16)

            def load(sems, tiles):
                def step(j, i, c):
                    sp.wait_ge(sems[0], c)
                    sp.dma_start(tiles[:, :, :], edge_xl_d[bass.ds(i * PAIR, PAIR), :]
                                 .rearrange("(u p) n -> p u n", p=P)).then_inc(sems[1], 16)
                return step

            def finish(j):
                sp.wait_ge(b["block_out"], sp.snap(j + 2))
                sp.dma_start(rows(mixed_d, j), mixed[:, :]).then_inc(mixed_stored, 16)

            sp.sem_inc(mixed_stored, 16)
            per_block(sp, load((s["rows_free"], s["rows_ready"]), rows_in),
                      load((b["weighted_ready"], b["rows_ready"]), rows_mix), finish=finish)
            sp.wait_ge(mixed_stored, 16 * (BLOCKS + 1))

        @block.gpsimd
        def _(pool):
            pool.memset(ones[:, :], 1.0).then_inc(s["wide_zeroed"], 1)
            pool.memset(att_wide[:, :, :].bitcast(F32), 0.0).then_inc(s["wide_zeroed"], 1)
            pool.memset(att_cols[:, :, :], 0.0).then_inc(s["wide_zeroed"], 1)
            pool.memset(zero[:, :], 0.0).then_inc(s["wide_zeroed"], 1)

        @block.vector
        def _(dve):
            dve.wait_ge(s["wide_zeroed"], 4)
            dve.wait_ge(s["loaded"], 32)
            for h in range(HEADS):
                r, k = h * HEAD_DIM % P, h * HEAD_DIM // P
                col = att[r:r + HEAD_DIM, k:k + 1]
                nc.vector.tensor_scalar(att_wide[r:r + HEAD_DIM, h, :], ones[r:r + HEAD_DIM, :], col, None,
                                        ALU.mult)
                nc.vector.tensor_copy(att_cols[r:r + HEAD_DIM, k, h:h + 1], col).then_inc(s["wide_ready"], 1)
            dve.sem_inc(s["maxed"], 1)
            dve.sem_inc(b["weighted_ready"], 1)
            dve.sem_inc(b["block_out"], 1)

            def begin(j):
                c = dve.snap(j + 1)
                nc.vector.memset(node_max[:, :], MASKED)
                nc.vector.tensor_copy(xr_hi[:, :], xr[:, bass.ds(j, 1), :].rearrange("p b n -> p (b n)"))
                dve.drain()
                nc.vector.tensor_tensor(xr_lo[:, :], xr[:, bass.ds(j, 1), :].rearrange("p b n -> p (b n)"),
                                        xr_hi[:, :].bitcast(F32), ALU.subtract).then_inc(s["xr_ready"], 1)

            def score(j, i, c):
                dst = dst_all[:, bass.ds(i * PAIR, PAIR)]
                nc.vector.tensor_scalar(hot_t[:, :], dst, g["node"][:, bass.ds(j, 1)], None, ALU.is_equal)
                dve.drain()
                nc.vector.tensor_scalar(mask[:, :], hot_t[:, :].bitcast(F32), 1.0, -MASKED, ALU.subtract,
                                        ALU.mult).then_inc(s["hot_ready"], 1)
                dve.wait_ge(s["scaled_ready"], c)
                nc.vector.tensor_tensor(bent[:, :, :].rearrange("p k e -> p (k e)"),
                                        message_ps[:, :, :].rearrange("p k e -> p (k e)"), scaled[:, :],
                                        ALU.max).then_inc(s["bent_ready"], 1)
                dve.wait_ge(s["spread_ready"], c)
                nc.vector.tensor_reduce(tile_max[:, :], spread_ps[:, :, :], AX.X, ALU.max)
                dve.drain()
                nc.vector.tensor_tensor(node_max[:, :], node_max[:, :], tile_max[:, :], ALU.max)\
                    .then_inc(s["maxed"], 1)

            def mix(j, i, c):
                nc.vector.tensor_scalar(hot_max[:, :], dst_all[:, bass.ds(i * PAIR, PAIR)],
                                        g["node"][:, bass.ds(j, 1)], None, ALU.is_equal)\
                    .then_inc(b["hot_max_ready"], 1)
                dve.wait_ge(b["max_spread"], c)
                pair_scores = scores[:, bass.ds(i * 2, 2), :]
                nc.vector.tensor_tensor(shifted[:, :, :], pair_scores, max_ps[:, :, :], ALU.subtract)
                dve.drain()
                nc.vector.tensor_scalar(shifted[:, :, :], shifted[:, :, :], BOUND, None, ALU.min)\
                    .then_inc(b["shift_ready"], 1)
                dve.wait_ge(b["mixed_in"], c)
                nc.vector.tensor_scalar(hot[:, 0, :], g["iota"][:, bass.ds(j * P, P)],
                                        g["dst"][:, bass.ds(i * 2, 1)], None, ALU.is_equal)
                nc.vector.tensor_scalar(hot[:, 1, :], g["iota"][:, bass.ds(j * P, P)],
                                        g["dst"][:, bass.ds(i * 2 + 1, 1)], None, ALU.is_equal)
                dve.wait_ge(b["exp_ready"], c)
                dve.wait_ge(b["rows_ready"], times16(dve, c))
                for u in range(2):
                    last = nc.vector.tensor_tensor(
                        weighted[:, u, 0:HID].rearrange("p (h d) -> p h d", h=HEADS),
                        rows_mix[:, u, :].rearrange("p (h d) -> p h d", h=HEADS),
                        weighted[:, u, HID:].unsqueeze(2).to_broadcast([P, HEADS, HEAD_DIM]), ALU.mult)
                last.then_inc(b["weighted_ready"], 1)

            def finish(j):
                c = dve.snap(j + 1)
                dve.wait_ge(b["block_mixed"], c)
                nc.vector.tensor_scalar(inverse[:, :], mix_ps[:, HID:], 1e-16, None, ALU.add)
                dve.drain()
                nc.vector.reciprocal(inverse[:, :], inverse[:, :])
                dve.drain()
                dve.wait_ge(mixed_stored, times16(dve, c))
                nc.vector.tensor_tensor(mixed[:, :].rearrange("p (h d) -> p h d", h=HEADS),
                                        mix_ps[:, 0:HID].rearrange("p (h d) -> p h d", h=HEADS),
                                        inverse[:, :].unsqueeze(2).to_broadcast([P, HEADS, HEAD_DIM]),
                                        ALU.mult).then_inc(b["block_out"], 1)

            per_block(dve, score, mix, begin=begin, finish=finish)

        @block.scalar
        def _(act):
            def score(j, i, c):
                act.wait_ge(s["message_ready"], c)
                nc.scalar.activation(scaled[:, :], message_ps[:, :, :].rearrange("p k e -> p (k e)"),
                                     ACT.Copy, scale=SLOPE).then_inc(s["scaled_ready"], 1)
                act.wait_ge(s["bent_ready"], c)
                nc.scalar.activation(bent_r[:, :, :], bent[:, :, :], ACT.Copy).then_inc(s["bent_r_ready"], 1)
                act.wait_ge(s["spread_ready"], c)
                nc.scalar.activation(scores[:, bass.ds(i * 2, 2), :], score_ps[:, :, :], ACT.Copy)\
                    .then_inc(s["score_kept"], 1)

            def mix(j, i, c):
                act.wait_ge(b["shift_ready"], c)
                act.wait_ge(b["mixed_in"], c)
                nc.scalar.activation(weighted[:, :, HID:], shifted[:, :, :], ACT.Exp)\
                    .then_inc(b["exp_ready"], 1)

            per_block(act, score, mix)

        @block.tensor
        def _(pe):
            pe.sem_inc(s["rows_free"], 1)
            pe.sem_inc(s["score_kept"], 1)
            pe.sem_inc(b["mixed_in"], 1)
            pe.wait_ge(s["wide_ready"], HEADS)

            def score(j, i, c):
                blocks, c16 = pe.snap(j + 1), times16(pe, c)
                pe.wait_ge(s["rows_ready"], c16)
                pe.wait_ge(s["hot_ready"], c)
                for u in range(2):
                    for k in range(KH):
                        last = nc.tensor.matmul(message_ps[:, k, u * P:(u + 1) * P],
                                                rows_in[:, u, k * P:(k + 1) * P], g["ident"][:, :],
                                                is_transpose=True, start=(u == 0 and k == 0), stop=False,
                                                skip_group_check=True)
                last.then_inc(s["rows_free"], 1)
                pe.wait_ge(s["xr_ready"], blocks)
                for k in range(KH):
                    for part in (xr_hi, xr_lo):
                        last = nc.tensor.matmul(message_ps[:, k, :], part[:, k * P:(k + 1) * P], hot_t[:, :],
                                                start=False, stop=(k == KH - 1 and part is xr_lo),
                                                skip_group_check=True)
                last.then_inc(s["message_ready"], 1)
                pe.wait_ge(s["maxed"], c)
                pe.wait_ge(s["score_kept"], c)
                for h in range(0, HEADS, 2):
                    nc.tensor.matmul(spread_ps[:, h:h + 2, :], g["ident_b"][:, :],
                                     mask[:, :].unsqueeze(1).to_broadcast([P, 2, PAIR]), start=True,
                                     stop=False, skip_group_check=True)
                pe.wait_ge(s["bent_r_ready"], c)
                for u in range(2):
                    for k in range(KH):
                        nc.tensor.matmul(score_ps[:, u, :], bent[:, k, u * P:(u + 1) * P], att_cols[:, k, :],
                                         start=(u == 0 and k == 0), stop=(u == 1 and k == KH - 1),
                                         skip_group_check=True)
                for h in range(HEADS):
                    last = nc.tensor.matmul(spread_ps[:, h, :], att_wide[:, h, :],
                                            bent_r[:, h * HEAD_DIM // P, :], start=False, stop=(h % 2 == 1),
                                            skip_group_check=True)
                last.then_inc(s["spread_ready"], 1)

            def middle(j, c):
                out = pe.snap(j + 1)
                pe.wait_ge(s["maxed"], c)
                pe.wait_ge(b["block_out"], out)
                nc.tensor.matmul(mix_ps[:, :], zero[:, 0:P], zero[:, :], start=True, stop=False,
                                 skip_group_check=True)

            def mix(j, i, c):
                more = pe.snap(c + 1)
                pe.wait_ge(b["hot_max_ready"], c)
                for u in range(2):
                    last = nc.tensor.matmul(max_ps[:, u, :], hot_max[:, u * P:(u + 1) * P], node_max[:, :],
                                            start=(u == 0), stop=(u == 1), skip_group_check=True)
                last.then_inc(b["max_spread"], 1)
                pe.wait_ge(b["weighted_ready"], more)
                for u in range(2):
                    last = nc.tensor.matmul(mix_ps[:, :], hot[:, u, :], weighted[:, u, :], start=False,
                                            stop=False, skip_group_check=True)
                last.then_inc(b["mixed_in"], 1)

            def finish(j):
                nc.tensor.matmul(mix_ps[:, :], zero[:, 0:P], zero[:, :], start=False, stop=True,
                                 skip_group_check=True).then_inc(b["block_mixed"], 1)

            per_block(pe, score, mix, middle=middle, finish=finish)


def attention_out_stage(nc, g, mixed_d, up_d, x_d, y_d, parts):
    KH = HID // P
    with ExitStack() as ctx:
        m = Memory(nc, ctx, "attention_out")
        w = WeightSplit(m, "up", up_d, FEAT, blocks=KH)
        moves = Moves(m)
        x, x_ready, x_free = moves.load("x", x_d, [FEAT])
        mixed, mixed_ready, mixed_free = moves.load("mixed", mixed_d, [HID])
        y, y_ready, y_stored = moves.store("y", y_d)
        mt_hi = m.sb("mt_hi", [P, 2, KH, P], F32R)
        mt_lo = m.sb("mt_lo", [P, 2, KH, P], F32R)
        norm = Norm(m)
        mt_ps = [m.ps(f"mt_ps{u}", [P, HID]) for u in range(2)]
        y_ps = [m.ps(f"y_ps{u}", [P, FEAT]) for u in range(2)]
        hi_ready = m.sems("hi_ready")
        lo_ready = m.sems("lo_ready")
        multiplied = m.sems("multiplied")
        y_ps_free = m.sems("y_ps_free")
        part_ready = m.sems("part_ready")
        block = m.block()

        @block.sync
        def _(sp):
            w.load(sp)
            moves.program(sp)

        @block.tensor
        def _(pe):
            for u in range(2):
                pe.sem_inc(multiplied[u], 1)
                pe.sem_inc(mixed_free[u], 1)
            w.wait(pe)

            def turn(tile, u, n):
                pe.wait_ge(mixed_ready[u], times16(pe, n))
                for k in range(KH):
                    last = nc.tensor.transpose(mt_ps[u][:, k * P:(k + 1) * P],
                                               mixed[:, u, k * P:(k + 1) * P], g["ident"][:, :])
                last.then_inc(mixed_free[u], 1)

            def multiply(tile, u, n):
                pe.wait_ge(lo_ready[u], n)
                pe.wait_ge(y_ps_free[u], n)
                product(nc, y_ps[u], mt_hi[:, u], mt_lo[:, u], w.hi, w.lo, blocks=KH)\
                    .then_inc(multiplied[u], 1)

            skewed(pe, turn, multiply)

        @block.scalar
        def _(act):
            w.high(act, nc)

            def early(tile, u, n):
                act.wait_ge(mixed_free[u], plus(act, n, 1))
                act.wait_ge(multiplied[u], n)
                nc.scalar.activation(mt_hi[:, u].rearrange("p b n -> p (b n)"), mt_ps[u][:, :], ACT.Copy)\
                    .then_inc(hi_ready[u], 1)

            def late(tile, u, n):
                norm.root(act, nc, g, plus(act, tile, 1))
                act.wait_ge(y_ready[u], n)
                nc.scalar.activation(parts[0][:, bass.ds(tile, 1), :].rearrange("p b n -> p (b n)"),
                                     y[:, u, :], ACT.Copy, scale=g["root"][:, bass.ds(tile, 1)])\
                    .then_inc(part_ready[u], 1)

            skewed(act, early, late)

        @block.vector
        def _(dve):
            w.low(dve, nc)
            for u in range(2):
                dve.sem_inc(y_ps_free[u], 1)
                dve.sem_inc(x_free[u], 1)

            def early(tile, u, n):
                dve.wait_ge(hi_ready[u], n)
                nc.vector.tensor_tensor(mt_lo[:, u].rearrange("p b n -> p (b n)"), mt_ps[u][:, :],
                                        mt_hi[:, u].rearrange("p b n -> p (b n)").bitcast(F32),
                                        ALU.subtract).then_inc(lo_ready[u], 1)

            def late(tile, u, n):
                more = plus(dve, n, 1)
                n16 = times16(dve, n)
                out = y[:, u, :]
                dve.wait_ge(y_stored[u], n16)
                dve.wait_ge(x_ready[u], n16)
                dve.wait_ge(multiplied[u], more)
                nc.vector.tensor_tensor(out, y_ps[u][:, :], x[:, u, :], ALU.add)\
                    .then_inc(y_ps_free[u], 1)
                dve.drain()
                dve.sem_inc(x_free[u], 1)
                norm.program(dve, nc, out, out, plus(dve, tile, 1)).then_inc(y_ready[u], 1)
                dve.drain()
                dve.wait_ge(part_ready[u], n)
                nc.vector.scalar_tensor_tensor(
                    out=parts[1][:, bass.ds(tile, 1), :].rearrange("p b n -> p (b n)"), in0=out,
                    scalar=g["root"][:, bass.ds(tile, 1)],
                    in1=parts[0][:, bass.ds(tile, 1), :].rearrange("p b n -> p (b n)").bitcast(F32),
                    op0=ALU.mult, op1=ALU.subtract)
                dve.drain()

            skewed(dve, early, late)


def degree_stage(nc, g):
    with ExitStack() as ctx:
        m = Memory(nc, ctx, "degree")
        rooted = m.sem("rooted")
        block = m.block()

        @block.scalar
        def _(act):
            nc.scalar.activation(g["root"][:, :], g["degree"][:, :], ACT.Sqrt, bias=g["one"][:, :])\
                .then_inc(rooted, 1)

        @block.vector
        def _(dve):
            dve.wait_ge(rooted, 1)
            nc.vector.reciprocal(g["root"][:, :], g["root"][:, :])
            nc.vector.tensor_scalar(g["inverse"][:, :], g["degree"][:, :], 1.0, None, ALU.max)
            dve.drain()
            nc.vector.reciprocal(g["inverse"][:, :], g["inverse"][:, :])


def graph_layers(nc, io, out):
    def dram(name, shape):
        return nc.dram_tensor(name, shape, F32, kind="Internal").ap()

    x1_d, x2_d, x3_d = (dram(f"x{n}_d", [ROWS, FEAT]) for n in (1, 2, 3))
    self_d, hidden_d = dram("self_d", [ROWS, FEAT]), dram("hidden_d", [ROWS, FEAT])
    xl_d, mixed_d = dram("xl_d", [ROWS, HID]), dram("mixed_d", [ROWS, HID])
    edge_xl_d = dram("edge_xl_d", [TILES * P, HID])
    with ExitStack() as ctx:
        m = Memory(nc, ctx, "all")
        g = {
            "ident": m.sb("ident", [P, P]),
            "ident_r": m.sb("ident_r", [P, P], F32R),
            "ident_b": m.sb("ident_b", [P, P], BF16),
            "eps": m.sb("eps", [P, 1]),
            "rms_eps": m.sb("rms_eps", [P, 1]),
            "one": m.sb("one", [P, 1]),
            "degree": m.sb("degree", [P, BLOCKS]),
            "root": m.sb("root", [P, BLOCKS]),
            "inverse": m.sb("inverse", [P, BLOCKS]),
            "counts_d": dram("counts_d", [ROWS, BLOCKS * P]),
            "gathered": m.sems("gathered", 4),
        }
        with ExitStack() as edges:
            m = Memory(nc, edges, "edges")
            g |= {
                "iota": m.sb("iota", [P, ROWS]),
                "node": m.sb("node", [P, BLOCKS]),
                "dst": m.sb("dst", [P, TILES]),
                "src": m.sb("src", [P, TILES]),
                "src_index": m.sb("src_index", [P, TILES], I32),
                "weight": m.sb("weight", [P, TILES]),
                "weight_hi": m.sb("weight_hi", [P, TILES], F32R),
                "weight_lo": m.sb("weight_lo", [P, TILES], F32R),
                "range": m.sb("range", [1, 2 * BLOCKS], I32),
            }
            setup(nc, io, g)
            with ExitStack() as inner:
                m = Memory(nc, inner, "first")
                wt = [m.sb(f"wt_{x}", [P, KB, FEAT], F32R) for x in ("hi", "lo")]
                build_graph(nc, g, *wt)
                degree_stage(nc, g)
                dense_stage(nc, g, "first", io["x"], x1_d, io["L0_gnn_bias"], weight_parts=wt)
            with ExitStack() as inner:
                xr = Memory(nc, inner, "heads").sb("xr", [P, BLOCKS, HID])
                project_stage(nc, g, x1_d, io["rms_cols"], io["L1_gnn_W_down"], io["L1_gnn_Wl"],
                              io["L1_gnn_Wr"], xl_d, xr)
                gather_stage(nc, g, xl_d, edge_xl_d)
                attention_stage(nc, g, io["att_cols"], io["dst_pairs"], edge_xl_d, xr, mixed_d)
        m = Memory(nc, ctx, "layers")
        parts = [m.sb(f"parts_{x}", [P, BLOCKS, FEAT], F32R) for x in ("hi", "lo")]
        attention_out_stage(nc, g, mixed_d, io["L1_gnn_W_up"], x1_d, x2_d, parts)
        graph_stage(nc, g, "gcn", parts, x3_d, io["L2_gnn_W"], g["root"], "gcn", bias_d=io["L2_gnn_b"],
                    x_d=x2_d)
        dense_stage(nc, g, "self0", x3_d, self_d, io["L3_gnn_b0"], weight_d=io["L3_gnn_W_self0"],
                    parts_out=parts)
        graph_stage(nc, g, "sage0", parts, hidden_d, io["L3_gnn_W_neigh0"], g["inverse"], "hidden",
                    added_d=self_d)
        dense_stage(nc, g, "self1", hidden_d, self_d, io["L3_gnn_b1"], weight_d=io["L3_gnn_W_self1"],
                    parts_out=parts)
        graph_stage(nc, g, "sage1", parts, out, io["L3_gnn_W_neigh1"], g["inverse"], "last",
                    added_d=self_d, x_d=x3_d)


def kernel(**inputs):
    import numpy as np
    import concourse.bacc as bacc
    from concourse.bass_utils import run_bass_kernel_spmd

    edges = {n: np.asarray(inputs[n]) for n in ("src", "dst", "edge_weight")}

    def pad(a, size, value):
        return np.concatenate([a, np.full(size - a.shape[0], value, a.dtype)])

    def columns(a):
        return np.ascontiguousarray(a.reshape(-1, P).T)

    nodes = np.arange(ROWS, dtype=np.int32).reshape(BLOCKS, P)
    loops_dst = np.concatenate([nodes, np.full_like(nodes, NO_NODE)], axis=1).reshape(-1)
    loops_src = np.concatenate([nodes, np.zeros_like(nodes)], axis=1).reshape(-1)
    dst = pad(edges["dst"], PAIRS * PAIR, PAD_NODE)
    src = pad(edges["src"], PAIRS * PAIR, PAD_NODE)
    dst_all = np.concatenate([dst, loops_dst])
    arrays = {
        "x": np.concatenate([np.asarray(inputs["x"]), np.zeros((ROWS - NODES, FEAT), np.float32)]),
        "dst_rows": np.concatenate([dst.reshape(PAIRS, PAIR),
                                    np.full((P - PAIRS, PAIR), NO_NODE, np.int32)]),
        "dst_pairs": dst_all,
        "dst_cols": columns(dst_all),
        "src_cols": columns(np.concatenate([src, loops_src])),
        "weight_cols": columns(pad(edges["edge_weight"], TILES * P, 0)),
        "rms_cols": columns(np.asarray(inputs["L1_gnn_rms_w"])),
        "att_cols": columns(np.asarray(inputs["L1_gnn_att"]).reshape(-1)),
    }
    for name in ("L0_gnn_bias", "L1_gnn_W_down", "L1_gnn_Wl", "L1_gnn_Wr", "L1_gnn_W_up", "L2_gnn_W", "L2_gnn_b",
                 "L3_gnn_W_self0", "L3_gnn_W_neigh0", "L3_gnn_b0", "L3_gnn_W_self1", "L3_gnn_W_neigh1",
                 "L3_gnn_b1"):
        arrays[name] = np.ascontiguousarray(np.asarray(inputs[name]))
    nc = bacc.Bacc("TRN2", target_bir_lowering=False, num_devices=1)
    io = {n: nc.dram_tensor(f"in_{n}", a.shape, mybir.dt.from_np(a.dtype), kind="ExternalInput").ap()
          for n, a in arrays.items()}
    out = nc.dram_tensor("out", (ROWS, FEAT), F32, kind="ExternalOutput").ap()
    graph_layers(nc, io, out)
    result = run_bass_kernel_spmd(nc, [{f"in_{n}": a for n, a in arrays.items()}], core_ids=[0])
    return result.results[0]["out"][:NODES]
```

```python
from contextlib import ExitStack

import concourse.bass as bass
from concourse import mybir

DT = mybir.dt
F32, F32R, BF16, I32 = DT.float32, DT.float32r, DT.bfloat16, DT.int32
ALU = mybir.AluOpType
ACT = mybir.ActivationFunctionType
AX = mybir.AxisListType

P = 128
NODES, EDGES = 1250, 21250
FEAT, HID, HEADS = 1024, 256, 4
HEAD_DIM = HID // HEADS
BLOCKS = -(-NODES // P)
ROWS = BLOCKS * P
KB = FEAT // P
HALF = 512
PAIR = 2 * P
PAIRS = -(-EDGES // PAIR)
SELF = PAIRS
QUADS = -(-PAIRS // 2)
TILES = 2 * (PAIRS + BLOCKS)
PAD_NODE = ROWS - 1
NO_NODE = 4 * ROWS
FAR = 1000.0
EPS = 1e-5
RMS_EPS = 1e-6
SLOPE = 0.2
BOUND = 40.0
MASKED = -1.0e30


class Memory:

    def __init__(self, nc, ctx, stage):
        self.nc, self.ctx, self.stage, self.named = nc, ctx, stage, []

    def sb(self, name, shape, dtype=F32):
        return self.ctx.enter_context(self.nc.sbuf_tensor(f"{self.stage}_{name}", shape, dtype))

    def ps(self, name, shape):
        return self.ctx.enter_context(self.nc.psum_tensor(f"{self.stage}_{name}", shape, F32))

    def sem(self, name):
        self.named.append(self.ctx.enter_context(self.nc.semaphore(f"{self.stage}_{name}")))
        return self.named[-1]

    def sems(self, name, n=2):
        return [self.sem(f"{name}{i}") for i in range(n)]

    def block(self):
        self.ctx.callback(self.clear)
        return self.ctx.enter_context(self.nc.Block())

    def clear(self):
        for sem in self.named:
            self.nc.gpsimd.sem_clear(sem)
        self.nc.all_engine_barrier()


def setup(nc, io, g):
    with ExitStack() as ctx:
        m = Memory(nc, ctx, "setup")
        iota_i = m.sb("iota_i", [P, ROWS], I32)
        node_i = m.sb("node_i", [P, BLOCKS], I32)
        row_i = m.sb("row_i", [P, 1], I32)
        dst_i = m.sb("dst_i", [P, TILES], I32)
        src_i = m.sb("src_i", [P, TILES], I32)
        first = m.sb("first", [P, BLOCKS])
        last = m.sb("last", [P, BLOCKS])
        rank = m.sb("rank", [P, 2])
        groups = [(g["pairs"], io["dst_by_pair"], PAIRS), (g["quads"], io["dst_by_quad"], QUADS)]
        dst_rows = [m.sb(f"dst_rows{n}", [P, d.shape[1]], I32) for n, (_, d, _) in enumerate(groups)]
        reach = [m.sb(f"reach{n}", [P, 2]) for n in range(2)]
        hit = [m.sb(f"hit{n}", [P, 2, BLOCKS]) for n in range(2)]
        found = [m.sb(f"found{n}", [P, P]) for n in range(2)]
        most = [m.sb(f"most{n}", [P, 1]) for n in range(2)]
        limits = [m.sb(f"limits{n}", [1, 2 * BLOCKS]) for n in range(2)]
        found_t = [m.ps(f"found_t{n}", [P, P]) for n in range(2)]
        most_t = [m.ps(f"most_t{n}", [1, P]) for n in range(2)]
        loaded, made, ident_step = (m.sem(n) for n in "loaded made ident_step".split())
        found_ready, found_turned, most_ready, most_turned = (
            m.sem(n) for n in "found_ready found_turned most_ready most_turned".split())
        block = m.block()

        @block.sync
        def _(sp):
            for (_, dram, _), tile in zip(groups, dst_rows):
                sp.dma_start(tile[:, :], dram).then_inc(loaded, 16)
            sp.dma_start(dst_i[:, :], io["dst_cols"]).then_inc(loaded, 16)
            sp.dma_start(src_i[:, :], io["src_cols"]).then_inc(loaded, 16)
            sp.dma_start(g["weight"][:, :], io["weight_cols"]).then_inc(loaded, 16)

        @block.gpsimd
        def _(pool):
            pool.iota(iota_i[:, :], pattern=[[1, ROWS]], base=0, channel_multiplier=0).then_inc(made, 1)
            pool.iota(node_i[:, :], pattern=[[P, BLOCKS]], base=0, channel_multiplier=1).then_inc(made, 1)
            pool.iota(row_i[:, :], pattern=[[0, 1]], base=0, channel_multiplier=1).then_inc(made, 1)
            pool.memset(g["ident"][:, :], 0.0).then_inc(ident_step, 1)
            pool.wait_ge(ident_step, 1)
            pool.affine_select(out=g["ident"][:, :], in_=g["ident"][:, :], compare_op=ALU.not_equal,
                               fill=1.0, base=0, pattern=[[-1, P]], channel_multiplier=1).then_inc(made, 1)

        @block.vector
        def _(dve):
            nc.vector.memset(g["eps"][:, :], EPS)
            nc.vector.memset(g["rms_eps"][:, :], RMS_EPS)
            nc.vector.memset(g["one"][:, :], 1.0)
            for n in range(2):
                nc.vector.memset(found[n][:, :], 0.0)
            dve.wait_ge(made, 4)
            nc.vector.tensor_copy(g["iota"][:, :], iota_i[:, :])
            nc.vector.tensor_copy(g["ident_r"][:, :], g["ident"][:, :])
            nc.vector.tensor_copy(g["ident_b"][:, :], g["ident"][:, :])
            nc.vector.tensor_copy(g["node"][:, :], node_i[:, :])
            nc.vector.tensor_scalar(rank[:, 0:1], row_i[:, :], -1.0, FAR, ALU.mult, ALU.add)
            nc.vector.tensor_scalar(rank[:, 1:2], row_i[:, :], 1.0, None, ALU.add)
            nc.vector.tensor_copy(first[:, :], iota_i[:, :].rearrange("p (b n) -> p b n", n=P)[:, :, 0])
            dve.drain()
            nc.vector.tensor_scalar(last[:, :], first[:, :], float(P - 1), None, ALU.add)
            dve.wait_ge(loaded, 16 * 5)
            nc.vector.tensor_copy(g["dst"][:, :], dst_i[:, :])
            nc.vector.tensor_copy(g["src"][:, :], src_i[:, :])
            nc.vector.tensor_copy(g["src_index"][:, :], src_i[:, :])
            nc.vector.tensor_copy(g["weight_hi"][:, :], g["weight"][:, :])
            for n in range(2):
                nc.vector.tensor_reduce(reach[n][:, 0:1], dst_rows[n][:, :], AX.X, ALU.min)
                nc.vector.tensor_reduce(reach[n][:, 1:2], dst_rows[n][:, :], AX.X, ALU.max)
            dve.drain()
            nc.vector.tensor_tensor(g["weight_lo"][:, :], g["weight"][:, :],
                                    g["weight_hi"][:, :].bitcast(F32), ALU.subtract)
            for n in range(2):
                nc.vector.tensor_scalar(hit[n][:, 0, :], last[:, :], reach[n][:, 0:1], None, ALU.is_ge)
                nc.vector.tensor_scalar(hit[n][:, 1, :], first[:, :], reach[n][:, 1:2], None, ALU.is_le)
            dve.drain()
            for n in range(2):
                nc.vector.tensor_tensor(hit[n][:, 0, :], hit[n][:, 0, :], hit[n][:, 1, :], ALU.mult)
            dve.drain()
            for n in range(2):
                nc.vector.tensor_scalar(found[n][:, 0:BLOCKS], hit[n][:, 0, :], rank[:, 0:1], None, ALU.mult)
                nc.vector.tensor_scalar(found[n][:, BLOCKS:2 * BLOCKS], hit[n][:, 0, :], rank[:, 1:2], None,
                                        ALU.mult).then_inc(found_ready, 1)
            dve.wait_ge(found_turned, 2)
            for n in range(2):
                nc.vector.tensor_reduce(most[n][:, :], found_t[n][:, :], AX.X, ALU.max).then_inc(most_ready, 1)
            dve.wait_ge(most_turned, 2)
            for n, (table, _, size) in enumerate(groups):
                nc.vector.tensor_scalar(limits[n][:, 0:BLOCKS], most_t[n][:, 0:BLOCKS], -1.0, FAR, ALU.mult,
                                        ALU.add)
                nc.vector.tensor_copy(limits[n][:, BLOCKS:], most_t[n][:, BLOCKS:2 * BLOCKS])
                dve.drain()
                nc.vector.tensor_scalar(limits[n][:, 0:BLOCKS], limits[n][:, 0:BLOCKS], float(size - 1), None,
                                        ALU.min)
                dve.drain()
                nc.vector.scalar_tensor_tensor(out=limits[n][:, BLOCKS:], in0=limits[n][:, 0:BLOCKS],
                                               scalar=1.0, in1=limits[n][:, BLOCKS:], op0=ALU.add, op1=ALU.max)
                dve.drain()
                nc.vector.tensor_copy(table[:, :], limits[n][:, :])

        @block.tensor
        def _(pe):
            pe.wait_ge(found_ready, 2)
            for n in range(2):
                nc.tensor.transpose(found_t[n][:, :], found[n][:, :], g["ident"][:, :])\
                    .then_inc(found_turned, 1)
            pe.wait_ge(most_ready, 2)
            for n in range(2):
                nc.tensor.matmul(most_t[n][:, :], most[n][:, :], g["ident"][:, :], start=True, stop=True)\
                    .then_inc(most_turned, 1)


def pair_range(engine, g, j):
    first = engine.value_load(g["pairs"][0:1, bass.ds(j, 1)], min_val=0, max_val=PAIRS - 1)
    end = engine.value_load(g["pairs"][0:1, bass.ds(j + BLOCKS, 1)], min_val=1, max_val=PAIRS)
    return first, end


def build_graph(nc, g, wt_hi, wt_lo):
    SLOTS = 2
    with ExitStack() as ctx:
        m = Memory(nc, ctx, "build")
        src_hot = m.sb("src_hot", [P, SLOTS, ROWS], F32R)
        dst_hot = m.sb("dst_hot", [P, SLOTS, P], F32R)
        dst_whi = m.sb("dst_whi", [P, SLOTS, P], F32R)
        dst_wlo = m.sb("dst_wlo", [P, SLOTS, P], F32R)
        zero = m.sb("zero", [P, HALF], F32R)
        counts = m.sb("counts", [P, ROWS])
        counts_t = m.sb("counts_t", [P, BLOCKS, P], F32R)
        count_ps = m.ps("count_ps", [P, 3 * HALF])
        weight_ps = m.ps("weight_ps", [P, 2 * HALF])
        turn_ps = m.ps("turn_ps", [P, 3 * HALF])
        zeroed = m.sem("zeroed")
        hot_ready = m.sems("hot_ready")
        hot_free = m.sems("hot_free")
        summed = m.sem("summed")
        weight_out = m.sem("weight_out")
        weight_hi_out = m.sem("weight_hi_out")
        counts_out = m.sem("counts_out")
        turned = m.sem("turned")
        turn_out = m.sem("turn_out")
        turn_stored = m.sem("turn_stored")
        WIDTHS = [(0, HALF), (HALF, HALF), (2 * HALF, ROWS - 2 * HALF)]
        block = m.block()
        PARTS = ((0, KB, True), (KB, BLOCKS, False))

        @block.sync
        def _(sp):
            sp.sem_inc(turn_stored, 16)
            with sp.Fori(0, BLOCKS) as j:
                c = sp.snap(j + 2)
                sp.wait_ge(turn_out, c)
                sp.dma_start(g["counts_d"][bass.ds(j * P, P), :],
                             counts_t[:, :, :].rearrange("p b n -> p (b n)").bitcast(F32)).then_inc(turn_stored, 16)
            sp.wait_ge(turn_stored, 16 * (BLOCKS + 1))

        @block.vector
        def _(dve):
            nc.vector.memset(zero[:, :].bitcast(F32), 0.0).then_inc(zeroed, 1)
            done = dve.alloc_register("build_dve")
            dve.reg_mov(done, 1)
            for j0, j1, with_weight in PARTS:
                with dve.Fori(j0, j1) as j:
                    first, end = pair_range(dve, g, j)
                    with dve.Fori(first, end) as i:
                        c = dve.snap(done)
                        for u in range(SLOTS):
                            t = i * 2 + u
                            src_t = g["src"][:, bass.ds(t, 1)]
                            dst_t = g["dst"][:, bass.ds(t, 1)]
                            nodes = g["iota"][:, bass.ds(j * P, P)]
                            dve.wait_ge(hot_free[u], c)
                            nc.vector.tensor_scalar(dst_hot[:, u, :], nodes, dst_t, None, ALU.is_equal)
                            if with_weight:
                                nc.vector.tensor_scalar(dst_whi[:, u, :], nodes, dst_t,
                                                        g["weight_hi"][:, bass.ds(t, 1)].bitcast(F32),
                                                        ALU.is_equal, ALU.mult)
                                nc.vector.tensor_scalar(dst_wlo[:, u, :], nodes, dst_t,
                                                        g["weight_lo"][:, bass.ds(t, 1)].bitcast(F32),
                                                        ALU.is_equal, ALU.mult)
                            nc.vector.tensor_scalar(src_hot[:, u, :], g["iota"][:, :], src_t, None,
                                                    ALU.is_equal).then_inc(hot_ready[u], 1)
                        dve.reg_add(done, done, 1)
                    c = dve.snap(j + 1)
                    if with_weight:
                        dve.wait_ge(summed, c)
                        nc.vector.tensor_copy(wt_hi[:, bass.ds(j, 1), :], weight_ps[:, :])\
                            .then_inc(weight_hi_out, 1)
                        dve.wait_ge(weight_hi_out, c)
                        nc.vector.tensor_tensor(wt_lo[:, bass.ds(j, 1), :], weight_ps[:, :],
                                                wt_hi[:, bass.ds(j, 1), :].bitcast(F32), ALU.subtract)\
                            .then_inc(weight_out, 1)

        @block.scalar
        def _(act):
            act.sem_inc(turn_out, 1)
            with act.Fori(0, BLOCKS) as j:
                c = act.snap(j + 1)
                c16 = act.snap(j * 16 + 16)
                act.wait_ge(summed, c)
                nc.scalar.activation(counts[:, :], count_ps[:, 0:ROWS], ACT.Copy,
                                     accum_out=g["degree"][:, bass.ds(j, 1)]).then_inc(counts_out, 1)
                act.wait_ge(turned, c)
                act.wait_ge(turn_stored, c16)
                nc.scalar.activation(counts_t[:, :, :], turn_ps[:, 0:ROWS].rearrange("p (b n) -> p b n", n=P),
                                     ACT.Copy).then_inc(turn_out, 1)

        @block.tensor
        def _(pe):
            pe.wait_ge(zeroed, 1)
            for u in range(SLOTS):
                pe.sem_inc(hot_free[u], 1)
            done = pe.alloc_register("build_pe")
            pe.reg_mov(done, 1)
            for j0, j1, with_weight in PARTS:
                with pe.Fori(j0, j1) as j:
                    first, end = pair_range(pe, g, j)
                    for a, w in WIDTHS:
                        nc.tensor.matmul(count_ps[:, a:a + w], zero[:, 0:P], zero[:, 0:w], start=True,
                                         stop=False, skip_group_check=True)
                    if with_weight:
                        for a in (0, HALF):
                            nc.tensor.matmul(weight_ps[:, a:a + HALF], zero[:, 0:P], zero[:, :], start=True,
                                             stop=False, skip_group_check=True)
                    with pe.Fori(first, end) as i:
                        c = pe.snap(done)
                        for u in range(SLOTS):
                            pe.wait_ge(hot_ready[u], c)
                            for a, w in WIDTHS:
                                last = nc.tensor.matmul(count_ps[:, a:a + w], dst_hot[:, u, :],
                                                        src_hot[:, u, a:a + w], start=False, stop=False,
                                                        skip_group_check=True)
                            if with_weight:
                                for part in (dst_whi, dst_wlo):
                                    for a in (0, HALF):
                                        last = nc.tensor.matmul(weight_ps[:, a:a + HALF], part[:, u, :],
                                                                src_hot[:, u, a:a + HALF], start=False,
                                                                stop=False, skip_group_check=True)
                            last.then_inc(hot_free[u], 1)
                        pe.reg_add(done, done, 1)
                    c = pe.snap(j + 1)
                    for a, w in WIDTHS:
                        last = nc.tensor.matmul(count_ps[:, a:a + w], zero[:, 0:P], zero[:, 0:w], start=False,
                                                stop=True, skip_group_check=True)
                    last.then_inc(summed, 1)
                    pe.wait_ge(counts_out, c)
                    pe.wait_ge(turn_out, c)
                    for b in range(BLOCKS):
                        last = nc.tensor.transpose(turn_ps[:, b * P:(b + 1) * P],
                                                   counts[:, b * P:(b + 1) * P], g["ident"][:, :])
                    last.then_inc(turned, 1)
                    if with_weight:
                        pe.wait_ge(weight_out, c)


def skewed(engine, early, late):
    early(0, 0, 1)
    with engine.Fori(0, BLOCKS // 2 - 1) as i:
        n = engine.snap(i + 1)
        more = engine.snap(i + 2)
        early(i * 2 + 1, 1, n)
        late(i * 2, 0, n)
        early(i * 2 + 2, 0, more)
        late(i * 2 + 1, 1, n)
    early(BLOCKS - 1, 1, BLOCKS // 2)
    late(BLOCKS - 2, 0, BLOCKS // 2)
    late(BLOCKS - 1, 1, BLOCKS // 2)


def plain(engine, step):
    with engine.Fori(0, BLOCKS // 2) as i:
        n = engine.snap(i + 1)
        step(i * 2, 0, n)
        step(i * 2 + 1, 1, n)


def times16(engine, n):
    return 16 * n if isinstance(n, int) else engine.snap(n * 16)


def plus(engine, n, k):
    return n + k if isinstance(n, int) else engine.snap(n + k)


def rows(dram, tile):
    return dram[bass.ds(tile * P, P), :]


class Moves:

    def __init__(self, m):
        self.m, self.loads, self.store_of = m, [], None

    def load(self, name, dram, shape, dtype=F32):
        tiles = self.m.sb(name, [P, 2] + shape, dtype)
        ready, free = self.m.sems(f"{name}_ready"), self.m.sems(f"{name}_free")
        self.loads.append((dram, tiles, ready, free))
        return tiles, ready, free

    def store(self, name, dram):
        tiles = self.m.sb(name, [P, 2, FEAT])
        ready, stored = self.m.sems(f"{name}_ready"), self.m.sems(f"{name}_stored")
        self.store_of = (dram, tiles, ready, stored)
        return tiles, ready, stored

    def program(self, sp):
        dram_out, out, ready_out, stored = self.store_of
        for u in range(2):
            sp.sem_inc(stored[u], 16)

        def load(tile, u, n):
            for dram, tiles, ready, free in self.loads:
                sp.wait_ge(free[u], n)
                dst = tiles[:, u]
                if len(dst.shape) == 3:
                    dst = dst.rearrange("p b n -> p (b n)")
                sp.dma_start(dst.bitcast(F32), rows(dram, tile)).then_inc(ready[u], 16)

        def store(tile, u, n):
            sp.wait_ge(ready_out[u], n)
            sp.dma_start(rows(dram_out, tile), out[:, u, :]).then_inc(stored[u], 16)

        load(0, 0, 1)
        load(1, 1, 1)
        with sp.Fori(1, BLOCKS // 2) as i:
            n = sp.snap(i + 1)
            before = sp.snap(i)
            for u in range(2):
                load(i * 2 + u, u, n)
                store(i * 2 - 2 + u, u, before)
        for u in range(2):
            store(BLOCKS - 2 + u, u, BLOCKS // 2)
        for u in range(2):
            sp.wait_ge(stored[u], 16 * (BLOCKS // 2 + 1))


class WeightSplit:

    def __init__(self, m, name, dram, width, blocks=KB, scale=None):
        self.dram, self.width, self.blocks, self.scale = dram, width, blocks, scale
        self.hi = m.sb(f"{name}_hi", [P, blocks, width], F32R)
        self.lo = m.sb(f"{name}_lo", [P, blocks, width], F32R)
        self.raw = m.sb(f"{name}_raw", [P, 2, width])
        self.raw_ready = m.sems(f"{name}_raw_ready")
        self.raw_free = m.sem(f"{name}_raw_free")
        self.hi_ready = m.sem(f"{name}_hi_ready")

    def load(self, sp):
        for k in range(self.blocks):
            if k >= 2:
                sp.wait_ge(self.raw_free, k - 1)
            sp.dma_start(self.raw[:, k % 2, :], self.dram[k * P:(k + 1) * P, :])\
                .then_inc(self.raw_ready[k % 2], 16)

    def high(self, act, nc):
        for k in range(self.blocks):
            act.wait_ge(self.raw_ready[k % 2], 16 * (k // 2 + 1))
            scale = 1.0 if self.scale is None else self.scale[:, k:k + 1]
            nc.scalar.activation(self.hi[:, k, :], self.raw[:, k % 2, :], ACT.Copy, scale=scale)\
                .then_inc(self.hi_ready, 1)

    def low(self, dve, nc):
        for k in range(self.blocks):
            dve.wait_ge(self.hi_ready, k + 1)
            scale = 1.0 if self.scale is None else self.scale[:, k:k + 1]
            nc.vector.scalar_tensor_tensor(out=self.lo[:, k, :], in0=self.raw[:, k % 2, :], scalar=scale,
                                           in1=self.hi[:, k, :].bitcast(F32), op0=ALU.mult,
                                           op1=ALU.subtract).then_inc(self.raw_free, 1)

    def wait(self, pe):
        pe.wait_ge(self.raw_free, self.blocks)


def product(nc, out, hi, lo, w_hi, w_lo, blocks=KB, width=FEAT):
    step = min(width, HALF)
    for a in range(0, width, step):
        terms = [(x, w, k) for k in range(blocks) for x, w in ((hi, w_hi), (hi, w_lo), (lo, w_hi))]
        for t, (x, w, k) in enumerate(terms):
            last = nc.tensor.matmul(out[:, a:a + step], x[:, k, :], w[:, k, a:a + step], start=(t == 0),
                                    stop=(t == len(terms) - 1))
    return last


class Norm:

    def __init__(self, m):
        self.stats = m.sb("ln_stats", [P, 2, 6])
        self.mean_var = m.sb("ln_mean_var", [P, 2])
        self.rstd = m.sb("ln_rstd", [P, 1])
        self.var_ready, self.std_ready = m.sem("ln_var_ready"), m.sem("ln_std_ready")

    def root(self, act, nc, g, n):
        act.wait_ge(self.var_ready, n)
        nc.scalar.activation(self.rstd[:, :], self.mean_var[:, 1:2], ACT.Sqrt, bias=g["eps"][:, :])\
            .then_inc(self.std_ready, 1)

    def program(self, dve, nc, out, x, n):
        for h in range(2):
            nc.vector.bn_stats(self.stats[:, h, :], x[:, h * HALF:(h + 1) * HALF])
        dve.drain()
        nc.vector.bn_aggr(self.mean_var[:, :], self.stats[:, :, :]).then_inc(self.var_ready, 1)
        dve.wait_ge(self.std_ready, n)
        nc.vector.reciprocal(self.rstd[:, :], self.rstd[:, :])
        dve.drain()
        return nc.vector.tensor_scalar(out, x, self.mean_var[:, 0:1], self.rstd[:, :], ALU.subtract,
                                       ALU.mult)


def dense_stage(nc, g, name, x_d, y_d, bias_d, weight_d=None, weight_parts=None, parts_out=None):
    with ExitStack() as ctx:
        m = Memory(nc, ctx, name)
        w = WeightSplit(m, "w", weight_d, FEAT) if weight_parts is None else None
        w_hi, w_lo = (w.hi, w.lo) if w else weight_parts
        moves = Moves(m)
        x, x_ready, x_free = moves.load("x", x_d, [FEAT])
        y, y_ready, y_stored = moves.store("y", y_d)
        bias = m.sb("bias", [P, FEAT])
        xt_hi = m.sb("xt_hi", [P, 2, KB, P], F32R)
        xt_lo = m.sb("xt_lo", [P, 2, KB, P], F32R)
        norm = Norm(m) if weight_parts else None
        xt_ps = [m.ps(f"xt_ps{u}", [P, KB * P]) for u in range(2)]
        y_ps = [m.ps(f"y_ps{u}", [P, FEAT]) for u in range(2)]
        bias_ready = m.sem("bias_ready")
        turned = m.sems("turned")
        hi_ready = m.sems("hi_ready")
        lo_ready = m.sems("lo_ready")
        multiplied = m.sems("multiplied")
        y_ps_free = m.sems("y_ps_free")
        hi_kept = m.sems("hi_kept")
        block = m.block()

        @block.sync
        def _(sp):
            sp.dma_start(bias[:, :], bias_d.partition_broadcast(P)).then_inc(bias_ready, 16)
            if w:
                w.load(sp)
            moves.program(sp)

        @block.tensor
        def _(pe):
            for u in range(2):
                pe.sem_inc(multiplied[u], 1)

            def turn(tile, u, n):
                pe.wait_ge(x_ready[u], times16(pe, n))
                for k in range(KB):
                    last = nc.tensor.transpose(xt_ps[u][:, k * P:(k + 1) * P], x[:, u, k * P:(k + 1) * P],
                                               g["ident"][:, :])
                last.then_inc(turned[u], 1)

            def multiply(tile, u, n):
                pe.wait_ge(lo_ready[u], n)
                pe.wait_ge(y_ps_free[u], n)
                product(nc, y_ps[u], xt_hi[:, u], xt_lo[:, u], w_hi, w_lo).then_inc(multiplied[u], 1)

            if w:
                w.wait(pe)
            skewed(pe, turn, multiply)

        @block.scalar
        def _(act):
            if w:
                w.high(act, nc)

            def early(tile, u, n):
                act.wait_ge(turned[u], n)
                act.wait_ge(multiplied[u], n)
                nc.scalar.activation(xt_hi[:, u].rearrange("p b n -> p (b n)"), xt_ps[u][:, :], ACT.Copy)\
                    .then_inc(hi_ready[u], 1)

            def keep(tile, u, n):
                early(tile, u, n)
                nc.scalar.activation(parts_out[0][:, bass.ds(tile, 1), :], x[:, u, :], ACT.Copy)\
                    .then_inc(hi_kept[u], 1)

            if norm:
                skewed(act, early, lambda tile, u, n: norm.root(act, nc, g, plus(act, tile, 1)))
            else:
                plain(act, keep if parts_out else early)

        @block.vector
        def _(dve):
            if w:
                w.low(dve, nc)
            for u in range(2):
                dve.sem_inc(y_ps_free[u], 1)
                dve.sem_inc(x_free[u], 1)
            dve.wait_ge(bias_ready, 16)

            def early(tile, u, n):
                dve.wait_ge(hi_ready[u], n)
                nc.vector.tensor_tensor(xt_lo[:, u].rearrange("p b n -> p (b n)"), xt_ps[u][:, :],
                                        xt_hi[:, u].rearrange("p b n -> p (b n)").bitcast(F32),
                                        ALU.subtract).then_inc(lo_ready[u], 1)

            def late(tile, u, n):
                more, whole = plus(dve, n, 1), plus(dve, tile, 1)
                if parts_out:
                    dve.wait_ge(hi_kept[u], n)
                    nc.vector.tensor_tensor(parts_out[1][:, bass.ds(tile, 1), :], x[:, u, :],
                                            parts_out[0][:, bass.ds(tile, 1), :].bitcast(F32), ALU.subtract)\
                        .then_inc(x_free[u], 1)
                dve.wait_ge(y_stored[u], times16(dve, n))
                dve.wait_ge(multiplied[u], more)
                nc.vector.tensor_tensor(y[:, u, :], y_ps[u][:, :], bias[:, :], ALU.add)\
                    .then_inc(y_ps_free[u], 1)
                if norm:
                    dve.drain()
                    nc.vector.tensor_tensor(y[:, u, :], y[:, u, :], x[:, u, :], ALU.add)\
                        .then_inc(x_free[u], 1)
                    dve.drain()
                    norm.program(dve, nc, y[:, u, :], y[:, u, :], whole).then_inc(y_ready[u], 1)
                else:
                    dve.drain()
                    dve.sem_inc(y_ready[u], 1)

            skewed(dve, early, late)


def graph_stage(nc, g, name, parts, y_d, weight_d, scale, kind, added_d=None, bias_d=None, x_d=None):
    with ExitStack() as ctx:
        m = Memory(nc, ctx, name)
        w = WeightSplit(m, "w", weight_d, FEAT)
        moves = Moves(m)
        counts, counts_ready, counts_free = moves.load("counts", g["counts_d"], [BLOCKS, P], F32R)
        if kind != "gcn":
            added, added_ready, added_free = moves.load("added", added_d, [FEAT])
        if kind != "hidden":
            x, x_ready, x_free = moves.load("x", x_d, [FEAT])
        y, y_ready, y_stored = moves.store("y", y_d)
        if kind == "gcn":
            bias = m.sb("bias", [P, FEAT])
            bias_ready = m.sem("bias_ready")
        mean = m.sb("mean", [P, FEAT])
        mean_hi = m.sb("mean_hi", [P, KB, P], F32R)
        mean_lo = m.sb("mean_lo", [P, KB, P], F32R)
        norm = Norm(m) if kind != "hidden" else None
        sum_ps = m.ps("sum_ps", [P, FEAT])
        turn_ps = m.ps("turn_ps", [P, KB * P])
        y_ps = [m.ps(f"y_ps{u}", [P, FEAT]) for u in range(2)]
        mean_ready = m.sem("mean_ready")
        turned = m.sem("turned")
        hi_ready = m.sem("hi_ready")
        lo_ready = m.sem("lo_ready")
        multiplied = m.sems("multiplied")
        y_ps_free = m.sems("y_ps_free")
        ready_to_relu = m.sems("ready_to_relu")
        block = m.block()

        @block.sync
        def _(sp):
            if kind == "gcn":
                sp.dma_start(bias[:, :], bias_d.partition_broadcast(P)).then_inc(bias_ready, 16)
            w.load(sp)
            moves.program(sp)

        @block.tensor
        def _(pe):
            def add_up(tile, u, n):
                whole, n16 = plus(pe, tile, 1), times16(pe, n)
                pe.wait_ge(counts_ready[u], n16)
                pe.wait_ge(mean_ready, whole)
                for a in (0, HALF):
                    terms = [(counts[:, u, k, :], part[:, k, a:a + HALF]) for part in parts
                             for k in range(BLOCKS)]
                    if kind == "gcn":
                        terms += [(g["ident_r"][:, :],
                                   part[:, bass.ds(tile, 1), a:a + HALF].rearrange("p b n -> p (b n)"))
                                  for part in parts]
                    for t, (c, r) in enumerate(terms):
                        last = nc.tensor.matmul(sum_ps[:, a:a + HALF], c, r, start=(t == 0),
                                                stop=(t == len(terms) - 1))
                last.then_inc(counts_free[u], 1)

            def turn(tile, u, n):
                whole = plus(pe, tile, 2)
                pe.wait_ge(mean_ready, whole)
                for k in range(KB):
                    last = nc.tensor.transpose(turn_ps[:, k * P:(k + 1) * P], mean[:, k * P:(k + 1) * P],
                                               g["ident"][:, :])
                last.then_inc(turned, 1)

            def multiply(tile, u, n):
                whole = plus(pe, tile, 1)
                pe.wait_ge(lo_ready, whole)
                pe.wait_ge(y_ps_free[u], n)
                product(nc, y_ps[u], mean_hi, mean_lo, w.hi, w.lo).then_inc(multiplied[u], 1)

            pe.sem_inc(mean_ready, 1)
            add_up(0, 0, 1)
            w.wait(pe)
            with pe.Fori(0, BLOCKS // 2 - 1) as i:
                n = pe.snap(i + 1)
                more = pe.snap(i + 2)
                turn(i * 2, 0, n)
                add_up(i * 2 + 1, 1, n)
                multiply(i * 2, 0, n)
                turn(i * 2 + 1, 1, n)
                add_up(i * 2 + 2, 0, more)
                multiply(i * 2 + 1, 1, n)
            turn(BLOCKS - 2, 0, BLOCKS // 2)
            add_up(BLOCKS - 1, 1, BLOCKS // 2)
            multiply(BLOCKS - 2, 0, BLOCKS // 2)
            turn(BLOCKS - 1, 1, BLOCKS // 2)
            multiply(BLOCKS - 1, 1, BLOCKS // 2)

        @block.scalar
        def _(act):
            w.high(act, nc)

            def take_mean(tile, u, n):
                more = plus(act, n, 1)
                done = plus(act, tile, 1)
                act.wait_ge(counts_free[u], more)
                act.wait_ge(turned, done)
                nc.scalar.activation(mean[:, :], sum_ps[:, :], ACT.Copy, scale=scale[:, bass.ds(tile, 1)])\
                    .then_inc(mean_ready, 1)

            def take_turned(tile, u, n):
                more = plus(act, tile, 2)
                act.wait_ge(turned, more)
                act.wait_ge(multiplied[1 - u], n)
                nc.scalar.activation(mean_hi[:, :, :].rearrange("p b n -> p (b n)"), turn_ps[:, :], ACT.Copy)\
                    .then_inc(hi_ready, 1)

            def root(tile):
                if norm:
                    norm.root(act, nc, g, plus(act, tile, 1))

            for u in range(2):
                act.sem_inc(counts_free[u], 1)
            act.sem_inc(turned, 1)
            act.sem_inc(multiplied[1], 1)
            take_mean(0, 0, 1)
            with act.Fori(0, BLOCKS // 2 - 1) as i:
                n = act.snap(i + 1)
                more = act.snap(i + 2)
                take_turned(i * 2, 0, n)
                take_mean(i * 2 + 1, 1, n)
                root(i * 2)
                take_turned(i * 2 + 1, 1, n)
                take_mean(i * 2 + 2, 0, more)
                root(i * 2 + 1)
            take_turned(BLOCKS - 2, 0, BLOCKS // 2)
            take_mean(BLOCKS - 1, 1, BLOCKS // 2)
            root(BLOCKS - 2)
            take_turned(BLOCKS - 1, 1, BLOCKS // 2)
            root(BLOCKS - 1)

        @block.vector
        def _(dve):
            w.low(dve, nc)
            for u in range(2):
                dve.sem_inc(y_ps_free[u], 1)
                if kind != "gcn":
                    dve.sem_inc(added_free[u], 1)
                if kind != "hidden":
                    dve.sem_inc(x_free[u], 1)
            if kind == "gcn":
                dve.wait_ge(bias_ready, 16)

            def step(tile, u, n):
                whole = dve.snap(tile + 1)
                more = dve.snap(n + u)
                n16 = times16(dve, n)
                dve.wait_ge(hi_ready, whole)
                nc.vector.tensor_tensor(mean_lo[:, :, :].rearrange("p b n -> p (b n)"), turn_ps[:, :],
                                        mean_hi[:, :, :].rearrange("p b n -> p (b n)").bitcast(F32),
                                        ALU.subtract).then_inc(lo_ready, 1)
                out = y[:, u, :]
                dve.wait_ge(y_stored[u], n16)
                if kind == "gcn":
                    dve.wait_ge(x_ready[u], n16)
                    dve.wait_ge(multiplied[u], more)
                    nc.vector.tensor_tensor(out, y_ps[u][:, :], bias[:, :], ALU.add)\
                        .then_inc(y_ps_free[u], 1)
                    dve.drain()
                    nc.vector.scalar_tensor_tensor(out=out, in0=out, scalar=0.0, in1=x[:, u, :], op0=ALU.max,
                                                   op1=ALU.add).then_inc(x_free[u], 1)
                else:
                    dve.wait_ge(added_ready[u], n16)
                    dve.wait_ge(multiplied[u], more)
                    nc.vector.tensor_tensor(out, y_ps[u][:, :], added[:, u, :], ALU.add)\
                        .then_inc(y_ps_free[u], 1)
                    dve.drain()
                    dve.sem_inc(added_free[u], 1)
                    if kind == "hidden":
                        nc.vector.tensor_scalar(out, out, 0.0, None, ALU.max).then_inc(y_ready[u], 1)
                        return
                    dve.wait_ge(x_ready[u], n16)
                    nc.vector.tensor_tensor(out, out, x[:, u, :], ALU.add).then_inc(x_free[u], 1)
                dve.drain()
                norm.program(dve, nc, out, out, whole).then_inc(y_ready[u], 1)

            plain(dve, step)


def project_stage(nc, g, x_d, rms_d, down_d, left_d, right_d, xl_d, xr):
    with ExitStack() as ctx:
        m = Memory(nc, ctx, "project")
        rms_w = m.sb("rms_w", [P, KB])
        w = WeightSplit(m, "down", down_d, HID, scale=rms_w)
        KH = HID // P
        left = WeightSplit(m, "left", left_d, HID, blocks=KH)
        right = WeightSplit(m, "right", right_d, HID, blocks=KH)
        x = m.sb("x", [P, 2, FEAT])
        square = m.sb("square", [P, FEAT])
        rms = m.sb("rms", [P, 2])
        down = m.sb("down", [P, HID])
        xl = m.sb("xl", [P, 2, HID])
        xt_hi = m.sb("xt_hi", [P, KB, P], F32R)
        xt_lo = m.sb("xt_lo", [P, KB, P], F32R)
        dt_hi = m.sb("dt_hi", [P, KH, P], F32R)
        dt_lo = m.sb("dt_lo", [P, KH, P], F32R)
        xt_ps = m.ps("xt_ps", [P, KB * P])
        down_ps = m.ps("down_ps", [P, HID])
        dt_ps = m.ps("dt_ps", [P, HID])
        xl_ps = m.ps("xl_ps", [P, HID])
        xr_ps = m.ps("xr_ps", [P, HID])
        names = "rms_ready turned squared hi_ready lo_ready multiplied down_ready down_turned dt_hi_ready " \
                "dt_lo_ready xl_whole xl_ready xr_ready"
        s = {n: m.sem(n) for n in names.split()}
        x_ready = m.sems("x_ready")
        xl_stored = m.sems("xl_stored")
        block = m.block()

        @block.sync
        def _(sp):
            sp.dma_start(rms_w[:, :], rms_d).then_inc(s["rms_ready"], 16)
            for u in range(2):
                sp.sem_inc(xl_stored[u], 16)
                sp.dma_start(x[:, u, :], rows(x_d, u)).then_inc(x_ready[u], 16)
            w.load(sp)
            left.load(sp)
            right.load(sp)

            def store(tile, u):
                sp.wait_ge(s["xl_ready"], tile + 1 if isinstance(tile, int) else sp.snap(tile + 1))
                sp.dma_start(rows(xl_d, tile), xl[:, u, :]).then_inc(xl_stored[u], 16)

            with sp.Fori(0, BLOCKS // 2 - 1) as i:
                for u in range(2):
                    store(i * 2 + u, u)
                    sp.dma_start(x[:, u, :], rows(x_d, i * 2 + 2 + u)).then_inc(x_ready[u], 16)
            for u in range(2):
                store(BLOCKS - 2 + u, u)
            for u in range(2):
                sp.wait_ge(xl_stored[u], 16 * (BLOCKS // 2 + 1))

        @block.tensor
        def _(pe):
            for split in (w, left, right):
                split.wait(pe)

            def step(tile, u, n):
                c = pe.snap(tile + 1)
                pe.wait_ge(x_ready[u], times16(pe, n))
                for k in range(KB):
                    last = nc.tensor.transpose(xt_ps[:, k * P:(k + 1) * P], x[:, u, k * P:(k + 1) * P],
                                               g["ident"][:, :])
                last.then_inc(s["turned"], 1)
                pe.wait_ge(s["lo_ready"], c)
                product(nc, down_ps, xt_hi, xt_lo, w.hi, w.lo, width=HID).then_inc(s["multiplied"], 1)
                pe.wait_ge(s["down_ready"], c)
                for k in range(KH):
                    last = nc.tensor.transpose(dt_ps[:, k * P:(k + 1) * P], down[:, k * P:(k + 1) * P],
                                               g["ident"][:, :])
                last.then_inc(s["down_turned"], 1)
                pe.wait_ge(s["dt_lo_ready"], c)
                pe.wait_ge(s["xr_ready"], c)
                product(nc, xl_ps, dt_hi, dt_lo, left.hi, left.lo, blocks=KH, width=HID)
                product(nc, xr_ps, dt_hi, dt_lo, right.hi, right.lo, blocks=KH, width=HID)\
                    .then_inc(s["xl_whole"], 1)

            plain(pe, step)

        @block.scalar
        def _(act):
            act.wait_ge(s["rms_ready"], 16)
            for split in (w, left, right):
                split.high(act, nc)

            def step(tile, u, n):
                c = act.snap(tile + 1)
                act.wait_ge(x_ready[u], times16(act, n))
                act.wait_ge(s["turned"], c)
                nc.scalar.activation(xt_hi[:, :, :].rearrange("p b n -> p (b n)"), xt_ps[:, :], ACT.Copy)\
                    .then_inc(s["hi_ready"], 1)
                nc.scalar.activation(square[:, :], x[:, u, :], ACT.Square, accum_out=rms[:, 0:1])
                act.drain()
                nc.scalar.activation(rms[:, 1:2], rms[:, 0:1], ACT.Sqrt, scale=1.0 / FEAT,
                                     bias=g["rms_eps"][:, :]).then_inc(s["squared"], 1)
                act.wait_ge(s["down_turned"], c)
                nc.scalar.activation(dt_hi[:, :, :].rearrange("p b n -> p (b n)"), dt_ps[:, :], ACT.Copy)\
                    .then_inc(s["dt_hi_ready"], 1)
                act.wait_ge(s["xl_whole"], c)
                act.wait_ge(xl_stored[u], times16(act, n))
                nc.scalar.activation(xl[:, u, :], xl_ps[:, :], ACT.Copy).then_inc(s["xl_ready"], 1)

            plain(act, step)

        @block.vector
        def _(dve):
            dve.sem_inc(s["xr_ready"], 1)
            for split in (w, left, right):
                split.low(dve, nc)

            def step(tile, u, n):
                c = dve.snap(tile + 1)
                dve.wait_ge(s["hi_ready"], c)
                nc.vector.tensor_tensor(xt_lo[:, :, :].rearrange("p b n -> p (b n)"), xt_ps[:, :],
                                        xt_hi[:, :, :].rearrange("p b n -> p (b n)").bitcast(F32),
                                        ALU.subtract).then_inc(s["lo_ready"], 1)
                dve.wait_ge(s["squared"], c)
                nc.vector.reciprocal(rms[:, 1:2], rms[:, 1:2])
                dve.drain()
                dve.wait_ge(s["multiplied"], c)
                nc.vector.tensor_scalar(down[:, :], down_ps[:, :], rms[:, 1:2], None, ALU.mult)\
                    .then_inc(s["down_ready"], 1)
                dve.wait_ge(s["dt_hi_ready"], c)
                nc.vector.tensor_tensor(dt_lo[:, :, :].rearrange("p b n -> p (b n)"), dt_ps[:, :],
                                        dt_hi[:, :, :].rearrange("p b n -> p (b n)").bitcast(F32),
                                        ALU.subtract).then_inc(s["dt_lo_ready"], 1)
                dve.wait_ge(s["xl_whole"], c)
                nc.vector.tensor_copy(xr[:, bass.ds(tile, 1), :].rearrange("p b n -> p (b n)"), xr_ps[:, :])\
                    .then_inc(s["xr_ready"], 1)

            plain(dve, step)


def attention_stage(nc, g, att_d, dst_pairs_d, xl_d, edge_xl_d, xr, mixed_d):
    KH = HID // P
    VISITS = BLOCKS * (QUADS + 1)
    with ExitStack() as ctx:
        m = Memory(nc, ctx, "attention")
        att = m.sb("att", [P, KH])
        ones = m.sb("ones", [P, P])
        att_wide = m.sb("att_wide", [P, HEADS, P], F32R)
        att_cols = m.sb("att_cols", [P, KH, HEADS])
        dst_all = m.sb("dst_all", [P, (PAIRS + BLOCKS) * PAIR], I32)
        xr_hi = m.sb("xr_hi", [P, HID], F32R)
        xr_lo = m.sb("xr_lo", [P, HID], F32R)
        self_rows = m.sb("self_rows", [P, HID])
        node_max = m.sb("node_max", [P, BLOCKS, HEADS])
        tile_max = m.sb("tile_max", [P, HEADS])
        zero = m.sb("zero", [P, HID + HEADS])
        inverse = m.sb("inverse", [P, HEADS])
        mixed = m.sb("mixed", [P, HID])

        def slots(name, shape, dtype=F32):
            return [m.sb(f"{name}{s}", shape, dtype) for s in range(2)]

        scores = slots("scores", [P, VISITS * 2, HEADS])
        index = slots("index", [P, 2], I32)
        got = slots("got", [P, 2, HID])
        hot_t = slots("hot_t", [P, PAIR], F32R)
        mask = slots("mask", [P, PAIR], BF16)
        scaled = slots("scaled", [P, KH * PAIR])
        bent = slots("bent", [P, KH * PAIR])
        bent_r = slots("bent_r", [P, KH * PAIR], F32R)
        back = slots("back", [P, 2, HID])
        hot_max = slots("hot_max", [P, PAIR])
        hot = slots("hot", [P, 2, P])
        shifted = slots("shifted", [P, 2, HEADS])
        weighted = slots("weighted", [P, 2, HID + HEADS])
        message_ps = [m.ps(f"message_ps{s}", [P, KH, PAIR]) for s in range(2)]
        spread_ps = [m.ps(f"spread_ps{s}", [P, HEADS, PAIR]) for s in range(2)]
        small_ps = m.ps("small_ps", [P, 2, HEADS])
        mix_ps = m.ps("mix_ps", [P, HID + HEADS])
        score_ps = [small_ps[:, :, :], mix_ps[:, 0:2 * HEADS].rearrange("p (u h) -> p u h", h=HEADS)]
        max_ps = [spread_ps[s][:, 0, 0:2 * HEADS].rearrange("p (u h) -> p u h", h=HEADS) for s in range(2)]
        a = {n: m.sems(f"a_{n}") for n in
             "hot_ready mask_ready message_ready scaled_ready bent_ready bent_r_ready spread_ready maxed "
             "score_kept".split()}
        b = {n: m.sems(f"b_{n}") for n in
             "back_ready hot_max_ready max_spread shift_ready exp_ready pool_weighted dve_weighted "
             "mixed_in".split()}
        gathered = g["gathered"]
        stored = m.sems("stored", 4)
        loaded, zeroed, wide_ready, xr_ready = (m.sem(n) for n in "loaded zeroed wide_ready xr_ready".split())
        self_ready, self_free, block_mixed, block_out, mixed_stored = (
            m.sem(n) for n in "self_ready self_free block_mixed block_out mixed_stored".split())
        passed, passed_first, maxima_whole = m.sem("passed"), m.sem("passed_first"), m.sem("maxima_whole")
        def weigh_tile(engine, s, u):
            return engine.tensor_tensor(weighted[s][:, u, 0:HID].rearrange("p (h d) -> p h d", h=HEADS),
                                        back[s][:, u, :].rearrange("p (h d) -> p h d", h=HEADS),
                                        weighted[s][:, u, HID:].unsqueeze(2)
                                        .to_broadcast([P, HEADS, HEAD_DIM]), ALU.mult)

        block = m.block()

        def one_pass(engine, step, begin=None, finish=None):
            counts = [engine.alloc_register(f"count{s}_{engine.engine.name}_{nc.next_id()}") for s in range(2)]
            for count in counts:
                engine.reg_mov(count, 1)

            def count_of(s):
                return engine.snap(counts[s], min_val=1, max_val=VISITS)

            with engine.Fori(0, BLOCKS) as j:
                first = engine.value_load(g["quads"][0:1, bass.ds(j, 1)], min_val=0, max_val=QUADS - 1)
                end = engine.value_load(g["quads"][0:1, bass.ds(j + BLOCKS, 1)], min_val=1, max_val=QUADS)
                if begin:
                    begin(j)
                with engine.Fori(first, end) as q:
                    step(j, [(s, engine.snap(q * 2 + s, max_val=PAIRS - 1), count_of(s), False)
                             for s in range(2)])
                    for s in range(2):
                        engine.reg_add(counts[s], counts[s], 1)
                step(j, [(0, engine.snap(j + SELF), count_of(0), True)])
                engine.reg_add(counts[0], counts[0], 1)
                if finish:
                    finish(j)
            return [engine.snap(c) for c in counts]

        @block.sync
        def _(sp):
            sp.dma_start(att[:, :], att_d).then_inc(loaded, 16)
            sp.dma_start(dst_all[:, :], dst_pairs_d.partition_broadcast(P)).then_inc(loaded, 16)
            sp.sem_inc(mixed_stored, 16)
            for k in range(4):
                sp.sem_inc(stored[k], 16)

            def store(j, visits):
                c16 = times16(sp, visits[-1][2])
                for s, pair, c, loops in visits:
                    if loops:
                        sp.wait_ge(self_free, sp.snap(j + 1))
                        sp.dma_start(self_rows[:, :], rows(xl_d, j)).then_inc(self_ready, 16)
                        continue
                    for u in range(2):
                        sp.wait_ge(gathered[2 * s + u], c16)
                        sp.dma_start(edge_xl_d[bass.ds((pair * 2 + u) * P, P), :], got[s][:, u, :])\
                            .then_inc(stored[2 * s + u], 16)

            one_pass(sp, store)

            def load(j, visits):
                for s, pair, c, loops in visits:
                    sp.wait_ge(b["mixed_in"][s], c)
                    if loops:
                        sp.dma_start(back[s][:, 0, :], rows(xl_d, j)).then_inc(b["back_ready"][s], 16)
                    else:
                        sp.dma_start(back[s][:, :, :], edge_xl_d[bass.ds(pair * PAIR, PAIR), :]
                                     .rearrange("(u p) n -> p u n", p=P)).then_inc(b["back_ready"][s], 16)

            def finish(j):
                sp.wait_ge(block_out, sp.snap(j + 2))
                sp.dma_start(rows(mixed_d, j), mixed[:, :]).then_inc(mixed_stored, 16)

            sp.wait_ge(passed_first, 1)
            one_pass(sp, load, finish=finish)
            sp.wait_ge(mixed_stored, 16 * (BLOCKS + 1))

        @block.gpsimd
        def _(pool):
            pool.memset(ones[:, :], 1.0).then_inc(zeroed, 1)
            pool.memset(att_wide[:, :, :].bitcast(F32), 0.0).then_inc(zeroed, 1)
            pool.memset(att_cols[:, :, :], 0.0).then_inc(zeroed, 1)
            pool.memset(zero[:, :], 0.0).then_inc(zeroed, 1)

            def gather(j, visits):
                c16 = times16(pool, visits[-1][2])
                for s, pair, c, loops in visits:
                    if loops:
                        continue
                    for u in range(2):
                        pool.wait_ge(stored[2 * s + u], c16)
                    pool.wait_ge(a["message_ready"][s], c)
                    pool.sem_inc(passed, 1)
                    pool.tensor_copy(index[s][:, :], g["src_index"][:, bass.ds(pair * 2, 2)])
                    pool.drain()
                    for u in range(2):
                        pool.indirect_dma_start(got[s][:, u, :], None, xl_d,
                                                bass.IndirectOffsetOnAxis(index[s][:, u:u + 1], 0))\
                            .then_inc(gathered[2 * s + u], 16)

            counts = one_pass(pool, gather)
            last16 = times16(pool, counts[1])
            for k in range(4):
                pool.wait_ge(stored[k], last16)
            pool.sem_inc(passed_first, 1)

            def weigh(j, visits):
                for s, pair, c, loops in visits:
                    more, c16 = plus(pool, c, 1), times16(pool, c)
                    pool.wait_ge(b["exp_ready"][s], more)
                    pool.wait_ge(b["back_ready"][s], c16)
                    weigh_tile(nc.gpsimd, s, 0).then_inc(b["pool_weighted"][s], 1)

            one_pass(pool, weigh)

        @block.vector
        def _(dve):
            dve.wait_ge(zeroed, 4)
            dve.wait_ge(loaded, 32)
            for h in range(HEADS):
                r, k = h * HEAD_DIM % P, h * HEAD_DIM // P
                col = att[r:r + HEAD_DIM, k:k + 1]
                nc.vector.tensor_scalar(att_wide[r:r + HEAD_DIM, h, :], ones[r:r + HEAD_DIM, :], col, None,
                                        ALU.mult)
                nc.vector.tensor_copy(att_cols[r:r + HEAD_DIM, k, h:h + 1], col).then_inc(wide_ready, 1)
            nc.vector.memset(node_max[:, :, :], MASKED)
            for s in range(2):
                nc.vector.memset(back[s][:, :, :], 0.0)
                for sem in (a["maxed"], a["bent_ready"], b["shift_ready"]):
                    dve.sem_inc(sem[s], 1)
            dve.sem_inc(block_out, 1)
            dve.drain()
            dve.sem_inc(wide_ready, 1)

            def begin(j):
                block_xr = xr[:, bass.ds(j, 1), :].rearrange("p b n -> p (b n)")
                nc.vector.tensor_copy(xr_hi[:, :], block_xr)
                dve.drain()
                nc.vector.tensor_tensor(xr_lo[:, :], block_xr, xr_hi[:, :].bitcast(F32), ALU.subtract)\
                    .then_inc(xr_ready, 1)

            def score(j, visits):
                more = {s: plus(dve, c, 1) for s, _, c, _ in visits}
                for s, pair, c, _ in visits:
                    dve.wait_ge(a["mask_ready"][s], c)
                    nc.vector.tensor_scalar(hot_t[s][:, :], dst_all[:, bass.ds(pair * PAIR, PAIR)],
                                            g["node"][:, bass.ds(j, 1)], None, ALU.is_equal)\
                        .then_inc(a["hot_ready"][s], 1)
                for s, pair, c, _ in visits:
                    dve.wait_ge(a["spread_ready"][s], c)
                    dve.wait_ge(a["scaled_ready"][s], c)
                    nc.vector.tensor_tensor(bent[s][:, :], message_ps[s][:, :, :].rearrange("p k e -> p (k e)"),
                                            scaled[s][:, :], ALU.max).then_inc(a["bent_ready"][s], 1)
                for s, pair, c, _ in visits:
                    dve.wait_ge(a["spread_ready"][s], more[s])
                    nc.vector.tensor_reduce(tile_max[:, :], spread_ps[s][:, :, :], AX.X, ALU.max)
                    dve.drain()
                    block_max = node_max[:, bass.ds(j, 1), :].rearrange("p b h -> p (b h)")
                    nc.vector.tensor_tensor(block_max, block_max, tile_max[:, :], ALU.max)\
                        .then_inc(a["maxed"][s], 1)
                    dve.drain()

            one_pass(dve, score, begin=begin)
            dve.sem_inc(maxima_whole, 1)

            def mix(j, visits):
                more = {s: plus(dve, c, 1) for s, _, c, _ in visits}
                c16 = {s: times16(dve, c) for s, _, c, _ in visits}
                for s, pair, c, _ in visits:
                    dve.wait_ge(b["mixed_in"][s], c)
                    nc.vector.tensor_scalar(hot_max[s][:, :], dst_all[:, bass.ds(pair * PAIR, PAIR)],
                                            g["node"][:, bass.ds(j, 1)], None, ALU.is_equal)\
                        .then_inc(b["hot_max_ready"][s], 1)
                for s, pair, c, _ in visits:
                    for u in range(2):
                        nc.vector.tensor_scalar(hot[s][:, u, :], g["iota"][:, bass.ds(j * P, P)],
                                                g["dst"][:, bass.ds(pair * 2 + u, 1)], None, ALU.is_equal)
                for s, pair, c, _ in visits:
                    dve.wait_ge(b["exp_ready"][s], c)
                    dve.wait_ge(b["max_spread"][s], c)
                    nc.vector.tensor_tensor(shifted[s][:, :, :], scores[s][:, bass.ds(c * 2 - 2, 2), :],
                                            max_ps[s], ALU.subtract)
                    dve.drain()
                    nc.vector.tensor_scalar(shifted[s][:, :, :], shifted[s][:, :, :], BOUND, None, ALU.min)\
                        .then_inc(b["shift_ready"][s], 1)
                for s, pair, c, _ in visits:
                    dve.wait_ge(b["exp_ready"][s], more[s])
                    dve.wait_ge(b["back_ready"][s], c16[s])
                    weigh_tile(nc.vector, s, 1).then_inc(b["dve_weighted"][s], 1)

            def finish(j):
                c = dve.snap(j + 1)
                c16 = times16(dve, c)
                dve.wait_ge(block_mixed, c)
                nc.vector.tensor_scalar(inverse[:, :], mix_ps[:, HID:], 1e-16, None, ALU.add)
                dve.drain()
                nc.vector.reciprocal(inverse[:, :], inverse[:, :])
                dve.drain()
                dve.wait_ge(mixed_stored, c16)
                nc.vector.tensor_tensor(mixed[:, :].rearrange("p (h d) -> p h d", h=HEADS),
                                        mix_ps[:, 0:HID].rearrange("p (h d) -> p h d", h=HEADS),
                                        inverse[:, :].unsqueeze(2).to_broadcast([P, HEADS, HEAD_DIM]),
                                        ALU.mult).then_inc(block_out, 1)

            one_pass(dve, mix, finish=finish)

        @block.scalar
        def _(act):
            for s in range(2):
                for sem in (a["mask_ready"], a["score_kept"], b["exp_ready"]):
                    act.sem_inc(sem[s], 1)

            def score(j, visits):
                more = {s: plus(act, c, 1) for s, _, c, _ in visits}
                for s, pair, c, _ in visits:
                    act.wait_ge(a["message_ready"][s], more[s])
                    nc.scalar.activation(scaled[s][:, :], message_ps[s][:, :, :].rearrange("p k e -> p (k e)"),
                                         ACT.Copy, scale=SLOPE).then_inc(a["scaled_ready"][s], 1)
                for s, pair, c, _ in visits:
                    act.wait_ge(a["spread_ready"][s], c)
                    nc.scalar.activation(mask[s][:, :], hot_t[s][:, :].bitcast(F32), ACT.Copy, scale=-MASKED,
                                         bias=MASKED).then_inc(a["mask_ready"][s], 1)
                for s, pair, c, _ in visits:
                    act.wait_ge(a["bent_ready"][s], more[s])
                    nc.scalar.activation(bent_r[s][:, :], bent[s][:, :], ACT.Copy)\
                        .then_inc(a["bent_r_ready"][s], 1)
                for s, pair, c, _ in visits:
                    act.wait_ge(a["spread_ready"][s], more[s])
                    nc.scalar.activation(scores[s][:, bass.ds(c * 2 - 2, 2), :], score_ps[s], ACT.Copy)\
                        .then_inc(a["score_kept"][s], 1)

            one_pass(act, score)

            def mix(j, visits):
                for s, pair, c, _ in visits:
                    act.wait_ge(b["mixed_in"][s], c)
                    act.wait_ge(b["shift_ready"][s], plus(act, c, 1))
                    nc.scalar.activation(weighted[s][:, :, HID:], shifted[s][:, :, :], ACT.Exp)\
                        .then_inc(b["exp_ready"][s], 1)

            one_pass(act, mix)

        @block.tensor
        def _(pe):
            for s in range(2):
                for sem in (a["message_ready"], a["spread_ready"], b["mixed_in"]):
                    pe.sem_inc(sem[s], 1)
            pe.sem_inc(self_free, 1)
            pe.wait_ge(wide_ready, HEADS + 1)

            def score(j, visits):
                blocks = pe.snap(j + 1)
                blocks16 = times16(pe, blocks)
                more = {s: plus(pe, c, 1) for s, _, c, _ in visits}
                c16 = times16(pe, visits[-1][2])
                for s, pair, c, loops in visits:
                    if loops:
                        pe.wait_ge(self_ready, blocks16)
                        tiles = [self_rows]
                    else:
                        for u in range(2):
                            pe.wait_ge(gathered[2 * s + u], c16)
                        tiles = [got[s][:, u, :] for u in range(2)]
                    pe.wait_ge(a["hot_ready"][s], c)
                    pe.wait_ge(a["bent_ready"][s], c)
                    pe.wait_ge(xr_ready, blocks)
                    for u, tile in enumerate(tiles):
                        for k in range(KH):
                            last = nc.tensor.matmul(message_ps[s][:, k, u * P:(u + 1) * P],
                                                    tile[:, k * P:(k + 1) * P], g["ident"][:, :],
                                                    is_transpose=True, start=(u == 0 and k == 0), stop=False,
                                                    skip_group_check=True)
                    if loops:
                        last.then_inc(self_free, 1)
                    for k in range(KH):
                        for part in (xr_hi, xr_lo):
                            last = nc.tensor.matmul(message_ps[s][:, k, :], part[:, k * P:(k + 1) * P],
                                                    hot_t[s][:, :], start=False,
                                                    stop=(k == KH - 1 and part is xr_lo),
                                                    skip_group_check=True)
                    last.then_inc(a["message_ready"][s], 1)
                for s, pair, c, _ in visits:
                    pe.wait_ge(a["maxed"][s], c)
                    pe.wait_ge(a["score_kept"][s], c)
                    pe.wait_ge(a["mask_ready"][s], more[s])
                    for h in range(0, HEADS, 2):
                        nc.tensor.matmul(spread_ps[s][:, h:h + 2, :], g["ident_b"][:, :],
                                         mask[s][:, :].unsqueeze(1).to_broadcast([P, 2, PAIR]), start=True,
                                         stop=False, skip_group_check=True)
                    pe.wait_ge(a["bent_r_ready"][s], c)
                    for u in range(2):
                        for k in range(KH):
                            nc.tensor.matmul(score_ps[s][:, u, :],
                                             bent[s][:, k * PAIR + u * P:k * PAIR + (u + 1) * P],
                                             att_cols[:, k, :], start=(u == 0 and k == 0),
                                             stop=(u == 1 and k == KH - 1), skip_group_check=True)
                    for h in range(HEADS):
                        k = h * HEAD_DIM // P
                        last = nc.tensor.matmul(spread_ps[s][:, h, :], att_wide[:, h, :],
                                                bent_r[s][:, k * PAIR:(k + 1) * PAIR], start=False,
                                                stop=(h % 2 == 1), skip_group_check=True)
                    last.then_inc(a["spread_ready"][s], 1)

            one_pass(pe, score)
            pe.wait_ge(maxima_whole, 1)

            def begin(j):
                pe.wait_ge(block_out, pe.snap(j + 1))
                nc.tensor.matmul(mix_ps[:, :], zero[:, 0:P], zero[:, :], start=True, stop=False,
                                 skip_group_check=True)

            def mix(j, visits):
                for s, pair, c, _ in visits:
                    pe.wait_ge(b["hot_max_ready"][s], c)
                    pe.wait_ge(b["shift_ready"][s], c)
                    for u in range(2):
                        last = nc.tensor.matmul(max_ps[s][:, u, :], hot_max[s][:, u * P:(u + 1) * P],
                                                node_max[:, bass.ds(j, 1), :].rearrange("p b h -> p (b h)"),
                                                start=(u == 0), stop=(u == 1), skip_group_check=True)
                    last.then_inc(b["max_spread"][s], 1)
                for s, pair, c, _ in visits:
                    pe.wait_ge(b["pool_weighted"][s], c)
                    pe.wait_ge(b["dve_weighted"][s], c)
                    for u in range(2):
                        last = nc.tensor.matmul(mix_ps[:, :], hot[s][:, u, :], weighted[s][:, u, :],
                                                start=False, stop=False, skip_group_check=True)
                    last.then_inc(b["mixed_in"][s], 1)

            def finish(j):
                nc.tensor.matmul(mix_ps[:, :], zero[:, 0:P], zero[:, :], start=False, stop=True,
                                 skip_group_check=True).then_inc(block_mixed, 1)

            one_pass(pe, mix, begin=begin, finish=finish)


def attention_out_stage(nc, g, mixed_d, up_d, x_d, y_d, parts):
    KH = HID // P
    with ExitStack() as ctx:
        m = Memory(nc, ctx, "attention_out")
        w = WeightSplit(m, "up", up_d, FEAT, blocks=KH)
        moves = Moves(m)
        x, x_ready, x_free = moves.load("x", x_d, [FEAT])
        mixed, mixed_ready, mixed_free = moves.load("mixed", mixed_d, [HID])
        y, y_ready, y_stored = moves.store("y", y_d)
        mt_hi = m.sb("mt_hi", [P, 2, KH, P], F32R)
        mt_lo = m.sb("mt_lo", [P, 2, KH, P], F32R)
        norm = Norm(m)
        mt_ps = [m.ps(f"mt_ps{u}", [P, HID]) for u in range(2)]
        y_ps = [m.ps(f"y_ps{u}", [P, FEAT]) for u in range(2)]
        hi_ready = m.sems("hi_ready")
        lo_ready = m.sems("lo_ready")
        multiplied = m.sems("multiplied")
        y_ps_free = m.sems("y_ps_free")
        part_ready = m.sems("part_ready")
        block = m.block()

        @block.sync
        def _(sp):
            w.load(sp)
            moves.program(sp)

        @block.tensor
        def _(pe):
            for u in range(2):
                pe.sem_inc(multiplied[u], 1)
                pe.sem_inc(mixed_free[u], 1)
            w.wait(pe)

            def turn(tile, u, n):
                pe.wait_ge(mixed_ready[u], times16(pe, n))
                for k in range(KH):
                    last = nc.tensor.transpose(mt_ps[u][:, k * P:(k + 1) * P],
                                               mixed[:, u, k * P:(k + 1) * P], g["ident"][:, :])
                last.then_inc(mixed_free[u], 1)

            def multiply(tile, u, n):
                pe.wait_ge(lo_ready[u], n)
                pe.wait_ge(y_ps_free[u], n)
                product(nc, y_ps[u], mt_hi[:, u], mt_lo[:, u], w.hi, w.lo, blocks=KH)\
                    .then_inc(multiplied[u], 1)

            skewed(pe, turn, multiply)

        @block.scalar
        def _(act):
            w.high(act, nc)

            def early(tile, u, n):
                act.wait_ge(mixed_free[u], plus(act, n, 1))
                act.wait_ge(multiplied[u], n)
                nc.scalar.activation(mt_hi[:, u].rearrange("p b n -> p (b n)"), mt_ps[u][:, :], ACT.Copy)\
                    .then_inc(hi_ready[u], 1)

            def late(tile, u, n):
                norm.root(act, nc, g, plus(act, tile, 1))
                act.wait_ge(y_ready[u], n)
                nc.scalar.activation(parts[0][:, bass.ds(tile, 1), :].rearrange("p b n -> p (b n)"),
                                     y[:, u, :], ACT.Copy, scale=g["root"][:, bass.ds(tile, 1)])\
                    .then_inc(part_ready[u], 1)

            skewed(act, early, late)

        @block.vector
        def _(dve):
            w.low(dve, nc)
            for u in range(2):
                dve.sem_inc(y_ps_free[u], 1)
                dve.sem_inc(x_free[u], 1)

            def early(tile, u, n):
                dve.wait_ge(hi_ready[u], n)
                nc.vector.tensor_tensor(mt_lo[:, u].rearrange("p b n -> p (b n)"), mt_ps[u][:, :],
                                        mt_hi[:, u].rearrange("p b n -> p (b n)").bitcast(F32),
                                        ALU.subtract).then_inc(lo_ready[u], 1)

            def late(tile, u, n):
                more = plus(dve, n, 1)
                n16 = times16(dve, n)
                out = y[:, u, :]
                dve.wait_ge(y_stored[u], n16)
                dve.wait_ge(x_ready[u], n16)
                dve.wait_ge(multiplied[u], more)
                nc.vector.tensor_tensor(out, y_ps[u][:, :], x[:, u, :], ALU.add)\
                    .then_inc(y_ps_free[u], 1)
                dve.drain()
                dve.sem_inc(x_free[u], 1)
                norm.program(dve, nc, out, out, plus(dve, tile, 1)).then_inc(y_ready[u], 1)
                dve.drain()
                dve.wait_ge(part_ready[u], n)
                nc.vector.scalar_tensor_tensor(
                    out=parts[1][:, bass.ds(tile, 1), :].rearrange("p b n -> p (b n)"), in0=out,
                    scalar=g["root"][:, bass.ds(tile, 1)],
                    in1=parts[0][:, bass.ds(tile, 1), :].rearrange("p b n -> p (b n)").bitcast(F32),
                    op0=ALU.mult, op1=ALU.subtract)
                dve.drain()

            skewed(dve, early, late)


def degree_stage(nc, g):
    with ExitStack() as ctx:
        m = Memory(nc, ctx, "degree")
        rooted = m.sem("rooted")
        block = m.block()

        @block.scalar
        def _(act):
            nc.scalar.activation(g["root"][:, :], g["degree"][:, :], ACT.Sqrt, bias=g["one"][:, :])\
                .then_inc(rooted, 1)

        @block.vector
        def _(dve):
            dve.wait_ge(rooted, 1)
            nc.vector.reciprocal(g["root"][:, :], g["root"][:, :])
            nc.vector.tensor_scalar(g["inverse"][:, :], g["degree"][:, :], 1.0, None, ALU.max)
            dve.drain()
            nc.vector.reciprocal(g["inverse"][:, :], g["inverse"][:, :])


def graph_layers(nc, io, out):
    def dram(name, shape):
        return nc.dram_tensor(name, shape, F32, kind="Internal").ap()

    x1_d, x2_d, x3_d = (dram(f"x{n}_d", [ROWS, FEAT]) for n in (1, 2, 3))
    self_d, hidden_d = dram("self_d", [ROWS, FEAT]), dram("hidden_d", [ROWS, FEAT])
    xl_d, mixed_d = dram("xl_d", [ROWS, HID]), dram("mixed_d", [ROWS, HID])
    edge_xl_d = dram("edge_xl_d", [TILES * P, HID])
    with ExitStack() as ctx:
        m = Memory(nc, ctx, "all")
        g = {
            "ident": m.sb("ident", [P, P]),
            "ident_r": m.sb("ident_r", [P, P], F32R),
            "ident_b": m.sb("ident_b", [P, P], BF16),
            "eps": m.sb("eps", [P, 1]),
            "rms_eps": m.sb("rms_eps", [P, 1]),
            "one": m.sb("one", [P, 1]),
            "degree": m.sb("degree", [P, BLOCKS]),
            "root": m.sb("root", [P, BLOCKS]),
            "inverse": m.sb("inverse", [P, BLOCKS]),
            "counts_d": dram("counts_d", [ROWS, BLOCKS * P]),
            "gathered": m.sems("gathered", 4),
        }
        with ExitStack() as edges:
            m = Memory(nc, edges, "edges")
            g |= {
                "iota": m.sb("iota", [P, ROWS]),
                "node": m.sb("node", [P, BLOCKS]),
                "dst": m.sb("dst", [P, TILES]),
                "src": m.sb("src", [P, TILES]),
                "src_index": m.sb("src_index", [P, TILES], I32),
                "weight": m.sb("weight", [P, TILES]),
                "weight_hi": m.sb("weight_hi", [P, TILES], F32R),
                "weight_lo": m.sb("weight_lo", [P, TILES], F32R),
                "pairs": m.sb("pairs", [1, 2 * BLOCKS], I32),
                "quads": m.sb("quads", [1, 2 * BLOCKS], I32),
            }
            setup(nc, io, g)
            with ExitStack() as inner:
                m = Memory(nc, inner, "first")
                wt = [m.sb(f"wt_{x}", [P, KB, FEAT], F32R) for x in ("hi", "lo")]
                build_graph(nc, g, *wt)
                degree_stage(nc, g)
                dense_stage(nc, g, "first", io["x"], x1_d, io["L0_gnn_bias"], weight_parts=wt)
            with ExitStack() as inner:
                xr = Memory(nc, inner, "heads").sb("xr", [P, BLOCKS, HID])
                project_stage(nc, g, x1_d, io["rms_cols"], io["L1_gnn_W_down"], io["L1_gnn_Wl"],
                              io["L1_gnn_Wr"], xl_d, xr)
                attention_stage(nc, g, io["att_cols"], io["dst_pairs"], xl_d, edge_xl_d, xr, mixed_d)
        m = Memory(nc, ctx, "layers")
        parts = [m.sb(f"parts_{x}", [P, BLOCKS, FEAT], F32R) for x in ("hi", "lo")]
        attention_out_stage(nc, g, mixed_d, io["L1_gnn_W_up"], x1_d, x2_d, parts)
        graph_stage(nc, g, "gcn", parts, x3_d, io["L2_gnn_W"], g["root"], "gcn", bias_d=io["L2_gnn_b"],
                    x_d=x2_d)
        dense_stage(nc, g, "self0", x3_d, self_d, io["L3_gnn_b0"], weight_d=io["L3_gnn_W_self0"],
                    parts_out=parts)
        graph_stage(nc, g, "sage0", parts, hidden_d, io["L3_gnn_W_neigh0"], g["inverse"], "hidden",
                    added_d=self_d)
        dense_stage(nc, g, "self1", hidden_d, self_d, io["L3_gnn_b1"], weight_d=io["L3_gnn_W_self1"],
                    parts_out=parts)
        graph_stage(nc, g, "sage1", parts, out, io["L3_gnn_W_neigh1"], g["inverse"], "last",
                    added_d=self_d, x_d=x3_d)


def kernel(**inputs):
    import numpy as np
    import concourse.bacc as bacc
    from concourse.bass_utils import run_bass_kernel_spmd

    edges = {n: np.asarray(inputs[n]) for n in ("src", "dst", "edge_weight")}

    def pad(a, size, value):
        return np.concatenate([a, np.full(size - a.shape[0], value, a.dtype)])

    def columns(a):
        return np.ascontiguousarray(a.reshape(-1, P).T)

    nodes = np.arange(ROWS, dtype=np.int32).reshape(BLOCKS, P)
    loops_dst = np.concatenate([nodes, np.full_like(nodes, NO_NODE)], axis=1).reshape(-1)
    loops_src = np.concatenate([nodes, np.zeros_like(nodes)], axis=1).reshape(-1)
    dst = pad(edges["dst"], PAIRS * PAIR, PAD_NODE)
    src = pad(edges["src"], PAIRS * PAIR, PAD_NODE)
    dst_all = np.concatenate([dst, loops_dst])
    arrays = {
        "x": np.concatenate([np.asarray(inputs["x"]), np.zeros((ROWS - NODES, FEAT), np.float32)]),
        "dst_by_pair": pad(dst, P * PAIR, NO_NODE).reshape(P, PAIR),
        "dst_by_quad": pad(dst, P * 2 * PAIR, NO_NODE).reshape(P, 2 * PAIR),
        "dst_pairs": dst_all,
        "dst_cols": columns(dst_all),
        "src_cols": columns(np.concatenate([src, loops_src])),
        "weight_cols": columns(pad(edges["edge_weight"], TILES * P, 0)),
        "rms_cols": columns(np.asarray(inputs["L1_gnn_rms_w"])),
        "att_cols": columns(np.asarray(inputs["L1_gnn_att"]).reshape(-1)),
    }
    for name in ("L0_gnn_bias", "L1_gnn_W_down", "L1_gnn_Wl", "L1_gnn_Wr", "L1_gnn_W_up", "L2_gnn_W", "L2_gnn_b",
                 "L3_gnn_W_self0", "L3_gnn_W_neigh0", "L3_gnn_b0", "L3_gnn_W_self1", "L3_gnn_W_neigh1",
                 "L3_gnn_b1"):
        arrays[name] = np.ascontiguousarray(np.asarray(inputs[name]))
    nc = bacc.Bacc("TRN2", target_bir_lowering=False, num_devices=1)
    io = {n: nc.dram_tensor(f"in_{n}", a.shape, mybir.dt.from_np(a.dtype), kind="ExternalInput").ap()
          for n, a in arrays.items()}
    out = nc.dram_tensor("out", (ROWS, FEAT), F32, kind="ExternalOutput").ap()
    graph_layers(nc, io, out)
    result = run_bass_kernel_spmd(nc, [{f"in_{n}": a for n, a in arrays.items()}], core_ids=[0])
    return result.results[0]["out"][:NODES]
```

```python
from contextlib import ExitStack

import concourse.bass as bass
from concourse import mybir

DT = mybir.dt
F32, F32R, BF16, I32 = DT.float32, DT.float32r, DT.bfloat16, DT.int32
ALU = mybir.AluOpType
ACT = mybir.ActivationFunctionType
AX = mybir.AxisListType

P = 128
NODES, EDGES = 1250, 21250
FEAT, HID, HEADS = 1024, 256, 4
HEAD_DIM = HID // HEADS
BLOCKS = -(-NODES // P)
ROWS = BLOCKS * P
KB = FEAT // P
HALF = 512
PAIR = 2 * P
PAIRS = -(-EDGES // PAIR)
SELF = PAIRS
QUADS = -(-PAIRS // 2)
TILES = 2 * (PAIRS + BLOCKS)
BATCH = -(-QUADS // BLOCKS)
BATCHES = -(-QUADS // BATCH)
BATCH_TILES = 4 * BATCH
STORED = BATCH_TILES * (BATCHES + BLOCKS)
PAD_NODE = ROWS - 1
NO_NODE = 4 * ROWS
FAR = 1000.0
EPS = 1e-5
RMS_EPS = 1e-6
SLOPE = 0.2
BOUND = 40.0
MASKED = -1.0e30


class Memory:

    def __init__(self, nc, ctx, stage):
        self.nc, self.ctx, self.stage, self.named = nc, ctx, stage, []

    def sb(self, name, shape, dtype=F32):
        return self.ctx.enter_context(self.nc.sbuf_tensor(f"{self.stage}_{name}", shape, dtype))

    def ps(self, name, shape):
        return self.ctx.enter_context(self.nc.psum_tensor(f"{self.stage}_{name}", shape, F32))

    def sem(self, name):
        self.named.append(self.ctx.enter_context(self.nc.semaphore(f"{self.stage}_{name}")))
        return self.named[-1]

    def sems(self, name, n=2):
        return [self.sem(f"{name}{i}") for i in range(n)]

    def block(self, gpsimd_works=False):
        self.ctx.callback(self.clear)
        return self.ctx.enter_context(self.nc.Block(no_gpsimd_drain=not gpsimd_works))

    def clear(self):
        numbers = sorted(sem.num for sem in self.named)
        ends = [n for n in numbers if n + 1 not in numbers]
        for first, last in zip([n for n in numbers if n - 1 not in numbers], ends):
            self.nc.gpsimd.sem_clear(range(first, last + 1))
        self.nc.all_engine_barrier(sem_only=True)


def setup(nc, io, g):
    with ExitStack() as ctx:
        m = Memory(nc, ctx, "setup")
        iota_i = m.sb("iota_i", [P, ROWS], I32)
        node_i = m.sb("node_i", [P, BLOCKS], I32)
        row_i = m.sb("row_i", [P, 1], I32)
        dst_i = m.sb("dst_i", [P, TILES], I32)
        src_i = m.sb("src_i", [P, TILES], I32)
        first = m.sb("first", [P, BLOCKS])
        last = m.sb("last", [P, BLOCKS])
        rank = m.sb("rank", [P, 2])
        groups = [(g["pairs"], io["dst_by_pair"], PAIRS), (g["quads"], io["dst_by_quad"], QUADS)]
        dst_rows = [m.sb(f"dst_rows{n}", [P, d.shape[1]], I32) for n, (_, d, _) in enumerate(groups)]
        reach = [m.sb(f"reach{n}", [P, 2]) for n in range(2)]
        hit = [m.sb(f"hit{n}", [P, 2, BLOCKS]) for n in range(2)]
        found = [m.sb(f"found{n}", [P, P]) for n in range(2)]
        most = [m.sb(f"most{n}", [P, 1]) for n in range(2)]
        limits = [m.sb(f"limits{n}", [1, 2 * BLOCKS]) for n in range(2)]
        stores = m.sb("stores", [1, BLOCKS + 1])
        batches = m.sb("batches", [1, BLOCKS], I32)
        found_t = [m.ps(f"found_t{n}", [P, P]) for n in range(2)]
        most_t = [m.ps(f"most_t{n}", [1, P]) for n in range(2)]
        loaded, made, ident_step = (m.sem(n) for n in "loaded made ident_step".split())
        found_ready, found_turned, most_ready, most_turned = (
            m.sem(n) for n in "found_ready found_turned most_ready most_turned".split())
        block = m.block(gpsimd_works=True)

        @block.sync
        def _(sp):
            for (_, dram, _), tile in zip(groups, dst_rows):
                sp.dma_start(tile[:, :], dram).then_inc(loaded, 16)
            sp.dma_start(dst_i[:, :], io["dst_cols"]).then_inc(loaded, 16)
            sp.dma_start(src_i[:, :], io["src_cols"]).then_inc(loaded, 16)
            sp.dma_start(g["weight"][:, :], io["weight_cols"]).then_inc(loaded, 16)

        @block.gpsimd
        def _(pool):
            pool.iota(iota_i[:, :], pattern=[[1, ROWS]], base=0, channel_multiplier=0).then_inc(made, 1)
            pool.iota(node_i[:, :], pattern=[[P, BLOCKS]], base=0, channel_multiplier=1).then_inc(made, 1)
            pool.iota(row_i[:, :], pattern=[[0, 1]], base=0, channel_multiplier=1).then_inc(made, 1)
            pool.memset(g["ident"][:, :], 0.0).then_inc(ident_step, 1)
            pool.wait_ge(ident_step, 1)
            pool.affine_select(out=g["ident"][:, :], in_=g["ident"][:, :], compare_op=ALU.not_equal,
                               fill=1.0, base=0, pattern=[[-1, P]], channel_multiplier=1).then_inc(made, 1)

        @block.vector
        def _(dve):
            nc.vector.memset(g["eps"][:, :], EPS)
            nc.vector.memset(g["rms_eps"][:, :], RMS_EPS)
            nc.vector.memset(g["one"][:, :], 1.0)
            nc.vector.memset(g["src_index"][:, TILES:], 0)
            for n in range(2):
                nc.vector.memset(found[n][:, :], 0.0)
            dve.wait_ge(made, 4)
            nc.vector.tensor_copy(g["iota"][:, :], iota_i[:, :])
            nc.vector.tensor_copy(g["ident_r"][:, :], g["ident"][:, :])
            nc.vector.tensor_copy(g["ident_b"][:, :], g["ident"][:, :])
            nc.vector.tensor_copy(g["node"][:, :], node_i[:, :])
            nc.vector.tensor_scalar(rank[:, 0:1], row_i[:, :], -1.0, FAR, ALU.mult, ALU.add)
            nc.vector.tensor_scalar(rank[:, 1:2], row_i[:, :], 1.0, None, ALU.add)
            nc.vector.tensor_copy(first[:, :], iota_i[:, :].rearrange("p (b n) -> p b n", n=P)[:, :, 0])
            dve.drain()
            nc.vector.tensor_scalar(last[:, :], first[:, :], float(P - 1), None, ALU.add)
            dve.wait_ge(loaded, 16 * 5)
            nc.vector.tensor_copy(g["dst"][:, :], dst_i[:, :])
            nc.vector.tensor_copy(g["src"][:, :], src_i[:, :])
            nc.vector.tensor_copy(g["src_index"][:, 0:TILES], src_i[:, :])
            nc.vector.tensor_copy(g["weight_hi"][:, :], g["weight"][:, :])
            for n in range(2):
                nc.vector.tensor_reduce(reach[n][:, 0:1], dst_rows[n][:, :], AX.X, ALU.min)
                nc.vector.tensor_reduce(reach[n][:, 1:2], dst_rows[n][:, :], AX.X, ALU.max)
            dve.drain()
            nc.vector.tensor_tensor(g["weight_lo"][:, :], g["weight"][:, :],
                                    g["weight_hi"][:, :].bitcast(F32), ALU.subtract)
            for n in range(2):
                nc.vector.tensor_scalar(hit[n][:, 0, :], last[:, :], reach[n][:, 0:1], None, ALU.is_ge)
                nc.vector.tensor_scalar(hit[n][:, 1, :], first[:, :], reach[n][:, 1:2], None, ALU.is_le)
            dve.drain()
            for n in range(2):
                nc.vector.tensor_tensor(hit[n][:, 0, :], hit[n][:, 0, :], hit[n][:, 1, :], ALU.mult)
            dve.drain()
            for n in range(2):
                nc.vector.tensor_scalar(found[n][:, 0:BLOCKS], hit[n][:, 0, :], rank[:, 0:1], None, ALU.mult)
                nc.vector.tensor_scalar(found[n][:, BLOCKS:2 * BLOCKS], hit[n][:, 0, :], rank[:, 1:2], None,
                                        ALU.mult).then_inc(found_ready, 1)
            dve.wait_ge(found_turned, 2)
            for n in range(2):
                nc.vector.tensor_reduce(most[n][:, :], found_t[n][:, :], AX.X, ALU.max).then_inc(most_ready, 1)
            dve.wait_ge(most_turned, 2)
            for n, (table, _, size) in enumerate(groups):
                nc.vector.tensor_scalar(limits[n][:, 0:BLOCKS], most_t[n][:, 0:BLOCKS], -1.0, FAR, ALU.mult,
                                        ALU.add)
                nc.vector.tensor_copy(limits[n][:, BLOCKS:], most_t[n][:, BLOCKS:2 * BLOCKS])
                dve.drain()
                nc.vector.tensor_scalar(limits[n][:, 0:BLOCKS], limits[n][:, 0:BLOCKS], float(size - 1), None,
                                        ALU.min)
                dve.drain()
                nc.vector.scalar_tensor_tensor(out=limits[n][:, BLOCKS:], in0=limits[n][:, 0:BLOCKS],
                                               scalar=1.0, in1=limits[n][:, BLOCKS:], op0=ALU.add, op1=ALU.max)
                dve.drain()
                nc.vector.tensor_copy(table[:, :], limits[n][:, :])
            dve.drain()
            nc.vector.memset(stores[:, 0:1], 0.0)
            nc.vector.memset(limits[1][:, 2 * BLOCKS - 1:], float(BATCH * BATCHES))
            dve.drain()
            nc.vector.tensor_scalar(limits[1][:, BLOCKS:], limits[1][:, BLOCKS:], 1.0 / BATCH,
                                    0.5 - 0.5 / BATCH, ALU.mult, ALU.add)
            dve.drain()
            nc.vector.tensor_copy(batches[:, :], limits[1][:, BLOCKS:])
            dve.drain()
            nc.vector.tensor_copy(limits[1][:, BLOCKS:], batches[:, :])
            dve.drain()
            for j in range(BLOCKS):
                nc.vector.scalar_tensor_tensor(out=stores[:, j + 1:j + 2], in0=stores[:, j:j + 1], scalar=1.0,
                                               in1=limits[1][:, BLOCKS + j:BLOCKS + j + 1], op0=ALU.add,
                                               op1=ALU.max)
                dve.drain()
            nc.vector.tensor_copy(g["stores"][:, :], stores[:, :])

        @block.tensor
        def _(pe):
            pe.wait_ge(found_ready, 2)
            for n in range(2):
                nc.tensor.transpose(found_t[n][:, :], found[n][:, :], g["ident"][:, :])\
                    .then_inc(found_turned, 1)
            pe.wait_ge(most_ready, 2)
            for n in range(2):
                nc.tensor.matmul(most_t[n][:, :], most[n][:, :], g["ident"][:, :], start=True, stop=True)\
                    .then_inc(most_turned, 1)


def load_table(nc, g, function):
    nc.scalar.activation(g["table_loaded"][:, :], g["one"][:, :], function)


def pair_range(engine, g, j):
    first = engine.value_load(g["pairs"][0:1, bass.ds(j, 1)], min_val=0, max_val=PAIRS - 1)
    end = engine.value_load(g["pairs"][0:1, bass.ds(j + BLOCKS, 1)], min_val=1, max_val=PAIRS)
    return first, end


def build_graph(nc, g, wt_hi, wt_lo):
    SLOTS = 2
    with ExitStack() as ctx:
        m = Memory(nc, ctx, "build")
        src_hot = m.sb("src_hot", [P, SLOTS, ROWS], F32R)
        dst_hot = m.sb("dst_hot", [P, SLOTS, P], F32R)
        dst_whi = m.sb("dst_whi", [P, SLOTS, P], F32R)
        dst_wlo = m.sb("dst_wlo", [P, SLOTS, P], F32R)
        zero = m.sb("zero", [P, HALF], F32R)
        counts = m.sb("counts", [P, ROWS])
        counts_t = m.sb("counts_t", [P, BLOCKS, P], F32R)
        count_ps = m.ps("count_ps", [P, 3 * HALF])
        weight_ps = m.ps("weight_ps", [P, 2 * HALF])
        turn_ps = m.ps("turn_ps", [P, 3 * HALF])
        zeroed = m.sem("zeroed")
        hot_ready = m.sems("hot_ready")
        dst_ready = m.sems("dst_ready")
        weighted_ready = m.sems("weighted_ready")
        hot_free = m.sems("hot_free")
        summed = m.sem("summed")
        weight_out = m.sem("weight_out")
        weight_hi_out = m.sem("weight_hi_out")
        counts_out = m.sem("counts_out")
        turned = m.sem("turned")
        turn_out = m.sem("turn_out")
        turn_stored = m.sem("turn_stored")
        rooted = m.sem("rooted")
        WIDTHS = [(0, HALF), (HALF, HALF), (2 * HALF, ROWS - 2 * HALF)]
        block = m.block()
        PARTS = ((0, KB, True), (KB, BLOCKS, False))

        @block.sync
        def _(sp):
            sp.sem_inc(turn_stored, 16)
            with sp.Fori(0, BLOCKS) as j:
                c = sp.snap(j + 2)
                sp.wait_ge(turn_out, c)
                sp.dma_start(g["counts_d"][bass.ds(j * P, P), :],
                             counts_t[:, :, :].rearrange("p b n -> p (b n)").bitcast(F32)).then_inc(turn_stored, 16)
            sp.wait_ge(turn_stored, 16 * (BLOCKS + 1))

        @block.vector
        def _(dve):
            nc.vector.memset(zero[:, :].bitcast(F32), 0.0).then_inc(zeroed, 1)
            dve.sem_inc(weight_out, 1)
            done = dve.alloc_register("build_dve")
            dve.reg_mov(done, 1)
            for j0, j1, with_weight in PARTS:
                with dve.Fori(j0, j1) as j:
                    first, end = pair_range(dve, g, j)
                    with dve.Fori(first, end) as i:
                        c = dve.snap(done)
                        for u in range(SLOTS):
                            t = i * 2 + u
                            src_t = g["src"][:, bass.ds(t, 1)]
                            dst_t = g["dst"][:, bass.ds(t, 1)]
                            nodes = g["iota"][:, bass.ds(j * P, P)]
                            dve.wait_ge(hot_free[u], c)
                            nc.vector.tensor_scalar(dst_hot[:, u, :], nodes, dst_t, None, ALU.is_equal)\
                                .then_inc(dst_ready[u], 1)
                            nc.vector.tensor_scalar(src_hot[:, u, :], g["iota"][:, :], src_t, None,
                                                    ALU.is_equal).then_inc(hot_ready[u], 1)
                        dve.reg_add(done, done, 1)
                    c = dve.snap(j + 1)
                    if with_weight:
                        dve.wait_ge(summed, c)
                        nc.vector.tensor_copy(wt_hi[:, bass.ds(j, 1), :], weight_ps[:, :])\
                            .then_inc(weight_hi_out, 1)
                        dve.wait_ge(weight_hi_out, c)
                        nc.vector.tensor_tensor(wt_lo[:, bass.ds(j, 1), :], weight_ps[:, :],
                                                wt_hi[:, bass.ds(j, 1), :].bitcast(F32), ALU.subtract)\
                            .then_inc(weight_out, 1)
            dve.wait_ge(rooted, 1)
            nc.vector.reciprocal(g["root"][:, :], g["root"][:, :])
            nc.vector.tensor_scalar(g["inverse"][:, :], g["degree"][:, :], 1.0, None, ALU.max)
            dve.drain()
            nc.vector.reciprocal(g["inverse"][:, :], g["inverse"][:, :])

        @block.scalar
        def _(act):
            load_table(nc, g, ACT.Copy)
            act.sem_inc(turn_out, 1)
            done = act.alloc_register("build_act")
            act.reg_mov(done, 1)
            for j0, j1, with_weight in PARTS:
                with act.Fori(j0, j1) as j:
                    if with_weight:
                        first, end = pair_range(act, g, j)
                        with act.Fori(first, end) as i:
                            c = act.snap(done)
                            for u in range(SLOTS):
                                act.wait_ge(dst_ready[u], c)
                                for weighted, weight in ((dst_whi, "weight_hi"), (dst_wlo, "weight_lo")):
                                    last = nc.scalar.activation(
                                        weighted[:, u, :], dst_hot[:, u, :].bitcast(F32), ACT.Copy,
                                        scale=g[weight][:, bass.ds(i * 2 + u, 1)].bitcast(F32))
                                last.then_inc(weighted_ready[u], 1)
                            act.reg_add(done, done, 1)
                    c = act.snap(j + 1)
                    c16 = act.snap(j * 16 + 16)
                    act.wait_ge(summed, c)
                    nc.scalar.activation(counts[:, :], count_ps[:, 0:ROWS], ACT.Copy,
                                         accum_out=g["degree"][:, bass.ds(j, 1)]).then_inc(counts_out, 1)
                    act.wait_ge(turned, c)
                    act.wait_ge(turn_stored, c16)
                    nc.scalar.activation(counts_t[:, :, :],
                                         turn_ps[:, 0:ROWS].rearrange("p (b n) -> p b n", n=P),
                                         ACT.Copy).then_inc(turn_out, 1)
            act.drain()
            nc.scalar.activation(g["root"][:, :], g["degree"][:, :], ACT.Sqrt, bias=g["one"][:, :])\
                .then_inc(rooted, 1)

        @block.tensor
        def _(pe):
            pe.wait_ge(zeroed, 1)
            for u in range(SLOTS):
                pe.sem_inc(hot_free[u], 1)
            done = pe.alloc_register("build_pe")
            pe.reg_mov(done, 1)
            for j0, j1, with_weight in PARTS:
                with pe.Fori(j0, j1) as j:
                    first, end = pair_range(pe, g, j)
                    blocks = pe.snap(j + 1)
                    for a, w in WIDTHS:
                        nc.tensor.matmul(count_ps[:, a:a + w], zero[:, 0:P], zero[:, 0:w], start=True,
                                         stop=False, skip_group_check=True)
                    if with_weight:
                        pe.wait_ge(weight_out, blocks)
                        for a in (0, HALF):
                            nc.tensor.matmul(weight_ps[:, a:a + HALF], zero[:, 0:P], zero[:, :], start=True,
                                             stop=False, skip_group_check=True)
                    with pe.Fori(first, end) as i:
                        c = pe.snap(done)
                        for u in range(SLOTS):
                            pe.wait_ge(hot_ready[u], c)
                            for a, w in WIDTHS:
                                last = nc.tensor.matmul(count_ps[:, a:a + w], dst_hot[:, u, :],
                                                        src_hot[:, u, a:a + w], start=False, stop=False,
                                                        skip_group_check=True)
                            if with_weight:
                                pe.wait_ge(weighted_ready[u], c)
                                for part in (dst_whi, dst_wlo):
                                    for a in (0, HALF):
                                        last = nc.tensor.matmul(weight_ps[:, a:a + HALF], part[:, u, :],
                                                                src_hot[:, u, a:a + HALF], start=False,
                                                                stop=False, skip_group_check=True)
                            last.then_inc(hot_free[u], 1)
                        pe.reg_add(done, done, 1)
                    c = pe.snap(j + 1)
                    nc.tensor.matmul(count_ps[:, 0:P], zero[:, 0:P], zero[:, 0:P], start=False, stop=True,
                                     skip_group_check=True).then_inc(summed, 1)
                    pe.wait_ge(counts_out, c)
                    pe.wait_ge(turn_out, c)
                    for b in range(BLOCKS):
                        last = nc.tensor.transpose(turn_ps[:, b * P:(b + 1) * P],
                                                   counts[:, b * P:(b + 1) * P], g["ident"][:, :])
                    last.then_inc(turned, 1)


def skewed(engine, early, late, weight=None):
    early(0, 0, 1)
    if weight:
        weight()
    with engine.Fori(0, BLOCKS // 2 - 1) as i:
        n = engine.snap(i + 1)
        more = engine.snap(i + 2)
        early(i * 2 + 1, 1, n)
        late(i * 2, 0, n)
        early(i * 2 + 2, 0, more)
        late(i * 2 + 1, 1, n)
    early(BLOCKS - 1, 1, BLOCKS // 2)
    late(BLOCKS - 2, 0, BLOCKS // 2)
    late(BLOCKS - 1, 1, BLOCKS // 2)


def interleaved(engine, parts, weights=None):
    def run(now, tile, u, n):
        for t, part in enumerate(part for when, part in parts if when == now):
            part(tile, u, n)
            if weights and now == "early" and t == 0:
                weights()

    def both(tile, u, n, next_n):
        for when, part in parts:
            if when == "early":
                part(plus(engine, tile, 1), 1 - u, next_n)
            else:
                part(tile, u, n)

    run("early", 0, 0, 1)
    with engine.Fori(0, BLOCKS // 2 - 1) as i:
        n = engine.snap(i + 1)
        more = engine.snap(i + 2)
        both(engine.snap(i * 2), 0, n, n)
        both(engine.snap(i * 2 + 1), 1, n, more)
    both(BLOCKS - 2, 0, BLOCKS // 2, BLOCKS // 2)
    run("late", BLOCKS - 1, 1, BLOCKS // 2)


def plain(engine, step):
    with engine.Fori(0, BLOCKS // 2) as i:
        n = engine.snap(i + 1)
        step(i * 2, 0, n)
        step(i * 2 + 1, 1, n)


def times16(engine, n):
    return 16 * n if isinstance(n, int) else engine.snap(n * 16)


def plus(engine, n, k):
    return n + k if isinstance(n, int) else engine.snap(n + k)


def rows(dram, tile):
    return dram[bass.ds(tile * P, P), :]


class Moves:

    def __init__(self, m):
        self.m, self.loads, self.store_of = m, [], None

    def free_when(self, tiles, free):
        self.loads = [(d, t, ready, free if t is tiles else f) for d, t, ready, f in self.loads]

    def load(self, name, dram, shape, dtype=F32):
        tiles = self.m.sb(name, [P, 2] + shape, dtype)
        ready, free = self.m.sems(f"{name}_ready"), self.m.sems(f"{name}_free")
        self.loads.append((dram, tiles, ready, free))
        return tiles, ready, free

    def store(self, name, dram):
        tiles = self.m.sb(name, [P, 2, FEAT])
        ready, stored = self.m.sems(f"{name}_ready"), self.m.sems(f"{name}_stored")
        self.store_of = (dram, tiles, ready, stored)
        return tiles, ready, stored

    def program(self, sp, weight):
        dram_out, out, ready_out, stored = self.store_of
        for u in range(2):
            sp.sem_inc(stored[u], 16)

        def load(tile, u, n):
            for dram, tiles, ready, free in self.loads:
                sp.wait_ge(free[u], n)
                dst = tiles[:, u]
                if len(dst.shape) == 3:
                    dst = dst.rearrange("p b n -> p (b n)")
                sp.dma_start(dst.bitcast(F32), rows(dram, tile)).then_inc(ready[u], 16)

        def store(tile, u, n):
            sp.wait_ge(ready_out[u], n)
            sp.dma_start(rows(dram_out, tile), out[:, u, :]).then_inc(stored[u], 16)

        load(0, 0, 1)
        load(1, 1, 1)
        weight.load(sp)
        with sp.Fori(1, BLOCKS // 2) as i:
            n = sp.snap(i + 1)
            before = sp.snap(i)
            for u in range(2):
                load(i * 2 + u, u, n)
                store(i * 2 - 2 + u, u, before)
        for u in range(2):
            store(BLOCKS - 2 + u, u, BLOCKS // 2)
        for u in range(2):
            sp.wait_ge(stored[u], 16 * (BLOCKS // 2 + 1))


class WeightSplit:

    SLOTS = 4

    def __init__(self, m, name, dram, width, blocks=KB, scale=None):
        self.dram, self.width, self.blocks, self.scale = dram, width, blocks, scale
        self.hi = m.sb(f"{name}_hi", [P, blocks, width], F32R)
        self.lo = m.sb(f"{name}_lo", [P, blocks, width], F32R)
        self.raw = m.sb(f"{name}_raw", [P, self.SLOTS, width])
        self.raw_ready = m.sems(f"{name}_raw_ready", self.SLOTS)
        self.raw_free = m.sem(f"{name}_raw_free")
        self.hi_ready = m.sem(f"{name}_hi_ready")

    def load(self, sp):
        for k in range(self.blocks):
            if k >= self.SLOTS:
                sp.wait_ge(self.raw_free, k - self.SLOTS + 1)
            sp.dma_start(self.raw[:, k % self.SLOTS, :], self.dram[k * P:(k + 1) * P, :])\
                .then_inc(self.raw_ready[k % self.SLOTS], 16)

    def high(self, act, nc, blocks=None):
        for k in blocks or range(self.blocks):
            act.wait_ge(self.raw_ready[k % self.SLOTS], 16 * (k // self.SLOTS + 1))
            scale = 1.0 if self.scale is None else self.scale[:, k:k + 1]
            nc.scalar.activation(self.hi[:, k, :], self.raw[:, k % self.SLOTS, :], ACT.Copy, scale=scale)\
                .then_inc(self.hi_ready, 1)

    def low(self, dve, nc):
        for k in range(self.blocks):
            dve.wait_ge(self.hi_ready, k + 1)
            scale = 1.0 if self.scale is None else self.scale[:, k:k + 1]
            nc.vector.scalar_tensor_tensor(out=self.lo[:, k, :], in0=self.raw[:, k % self.SLOTS, :], scalar=scale,
                                           in1=self.hi[:, k, :].bitcast(F32), op0=ALU.mult,
                                           op1=ALU.subtract).then_inc(self.raw_free, 1)

    def wait(self, pe, k):
        pe.wait_ge(self.raw_free, k + 1)


class MadeWeight:

    def __init__(self, hi, lo):
        self.hi, self.lo, self.blocks = hi, lo, KB

    def load(self, sp):
        pass

    def high(self, act, nc):
        pass

    def low(self, dve, nc):
        pass

    def wait(self, pe, k):
        pass


def product(nc, out, hi, lo, split, width=FEAT):
    step = min(width, HALF)
    for k in range(split.blocks):
        split.wait(nc.tensor, k)
        for t, (x, w) in enumerate(((hi, split.hi), (hi, split.lo), (lo, split.hi))):
            for a in range(0, width, step):
                last = nc.tensor.matmul(out[:, a:a + step], x[:, k, :], w[:, k, a:a + step],
                                        start=(k == 0 and t == 0),
                                        stop=(k == split.blocks - 1 and t == 2))
    return last


class Norm:

    def __init__(self, m):
        self.stats = m.sb("ln_stats", [P, 2, 6])
        self.mean_var = m.sb("ln_mean_var", [P, 2])
        self.rstd = m.sb("ln_rstd", [P, 1])
        self.var_ready, self.std_ready = m.sem("ln_var_ready"), m.sem("ln_std_ready")

    def root(self, act, nc, g, n):
        act.wait_ge(self.var_ready, n)
        nc.scalar.activation(self.rstd[:, :], self.mean_var[:, 1:2], ACT.Sqrt, bias=g["eps"][:, :])\
            .then_inc(self.std_ready, 1)

    def program(self, dve, nc, out, x, n):
        for h in range(2):
            nc.vector.bn_stats(self.stats[:, h, :], x[:, h * HALF:(h + 1) * HALF])
        dve.drain()
        nc.vector.bn_aggr(self.mean_var[:, :], self.stats[:, :, :]).then_inc(self.var_ready, 1)
        dve.wait_ge(self.std_ready, n)
        nc.vector.reciprocal(self.rstd[:, :], self.rstd[:, :])
        dve.drain()
        return nc.vector.tensor_scalar(out, x, self.mean_var[:, 0:1], self.rstd[:, :], ALU.subtract,
                                       ALU.mult)


def dense_stage(nc, g, name, x_d, y_d, bias_d, weight_d=None, weight_parts=None, parts_out=None):
    with ExitStack() as ctx:
        m = Memory(nc, ctx, name)
        w = MadeWeight(*weight_parts) if weight_parts else WeightSplit(m, "w", weight_d, FEAT)
        moves = Moves(m)
        x, x_ready, x_free = moves.load("x", x_d, [FEAT])
        if weight_parts:
            added, added_ready, added_free = moves.load("added", x_d, [FEAT])
        y, y_ready, y_stored = moves.store("y", y_d)
        bias = m.sb("bias", [P, FEAT])
        xt_hi = m.sb("xt_hi", [P, 2, KB, P], F32R)
        xt_lo = m.sb("xt_lo", [P, 2, KB, P], F32R)
        norm = Norm(m) if weight_parts else None
        xt_ps = [m.ps(f"xt_ps{u}", [P, KB * P]) for u in range(2)]
        y_ps = [m.ps(f"y_ps{u}", [P, FEAT]) for u in range(2)]
        bias_ready = m.sem("bias_ready")
        turned = m.sems("turned")
        if weight_parts:
            moves.free_when(x, turned)
        hi_ready = m.sems("hi_ready")
        lo_ready = m.sems("lo_ready")
        multiplied = m.sems("multiplied")
        y_ps_free = m.sems("y_ps_free")
        hi_kept = m.sems("hi_kept")
        block = m.block()

        @block.sync
        def _(sp):
            sp.dma_start(bias[:, :], bias_d.partition_broadcast(P)).then_inc(bias_ready, 16)
            moves.program(sp, w)

        @block.tensor
        def _(pe):
            for u in range(2):
                pe.sem_inc(multiplied[u], 1)
                pe.sem_inc(turned[u], 1)

            def turn(tile, u, n):
                pe.wait_ge(x_ready[u], times16(pe, n))
                for k in range(KB):
                    last = nc.tensor.transpose(xt_ps[u][:, k * P:(k + 1) * P], x[:, u, k * P:(k + 1) * P],
                                               g["ident"][:, :])
                last.then_inc(turned[u], 1)

            def multiply(tile, u, n):
                pe.wait_ge(lo_ready[u], n)
                pe.wait_ge(y_ps_free[u], n)
                product(nc, y_ps[u], xt_hi[:, u], xt_lo[:, u], w).then_inc(multiplied[u], 1)

            skewed(pe, turn, multiply)

        @block.scalar
        def _(act):
            load_table(nc, g, ACT.Sqrt if norm else ACT.Copy)

            def early(tile, u, n):
                act.wait_ge(turned[u], plus(act, n, 1))
                act.wait_ge(multiplied[u], n)
                nc.scalar.activation(xt_hi[:, u].rearrange("p b n -> p (b n)"), xt_ps[u][:, :], ACT.Copy)\
                    .then_inc(hi_ready[u], 1)

            def keep(tile, u, n):
                early(tile, u, n)
                nc.scalar.activation(parts_out[0][:, bass.ds(tile, 1), :], x[:, u, :], ACT.Copy)\
                    .then_inc(hi_kept[u], 1)

            def root(tile, u, n):
                if norm:
                    norm.root(act, nc, g, plus(act, tile, 1))

            skewed(act, keep if parts_out else early, root, lambda: w.high(act, nc))

        @block.vector
        def _(dve):
            for u in range(2):
                dve.sem_inc(y_ps_free[u], 1)
                dve.sem_inc(added_free[u] if norm else x_free[u], 1)
            dve.wait_ge(bias_ready, 16)

            def early(tile, u, n):
                dve.wait_ge(hi_ready[u], n)
                nc.vector.tensor_tensor(xt_lo[:, u].rearrange("p b n -> p (b n)"), xt_ps[u][:, :],
                                        xt_hi[:, u].rearrange("p b n -> p (b n)").bitcast(F32),
                                        ALU.subtract).then_inc(lo_ready[u], 1)
                if parts_out:
                    dve.wait_ge(hi_kept[u], n)
                    nc.vector.tensor_tensor(parts_out[1][:, bass.ds(tile, 1), :], x[:, u, :],
                                            parts_out[0][:, bass.ds(tile, 1), :].bitcast(F32), ALU.subtract)\
                        .then_inc(x_free[u], 1)

            def late(tile, u, n):
                more, whole = plus(dve, n, 1), plus(dve, tile, 1)
                dve.wait_ge(y_stored[u], times16(dve, n))
                dve.wait_ge(multiplied[u], more)
                nc.vector.tensor_tensor(y[:, u, :], y_ps[u][:, :], bias[:, :], ALU.add)\
                    .then_inc(y_ps_free[u], 1)
                if norm:
                    dve.drain()
                    dve.wait_ge(added_ready[u], times16(dve, n))
                    nc.vector.tensor_tensor(y[:, u, :], y[:, u, :], added[:, u, :], ALU.add)\
                        .then_inc(added_free[u], 1)
                    dve.drain()
                    norm.program(dve, nc, y[:, u, :], y[:, u, :], whole).then_inc(y_ready[u], 1)
                else:
                    dve.drain()
                    dve.sem_inc(y_ready[u], 1)

            skewed(dve, early, late, lambda: w.low(dve, nc))


def graph_stage(nc, g, name, parts, y_d, weight_d, scale, kind, added_d=None, bias_d=None, x_d=None):
    with ExitStack() as ctx:
        m = Memory(nc, ctx, name)
        w = WeightSplit(m, "w", weight_d, FEAT)
        moves = Moves(m)
        counts, counts_ready, counts_free = moves.load("counts", g["counts_d"], [BLOCKS, P], F32R)
        if kind != "gcn":
            added, added_ready, added_free = moves.load("added", added_d, [FEAT])
        if kind != "hidden":
            x, x_ready, x_free = moves.load("x", x_d, [FEAT])
        y, y_ready, y_stored = moves.store("y", y_d)
        if kind == "gcn":
            bias = m.sb("bias", [P, FEAT])
            bias_ready = m.sem("bias_ready")
        mean = m.sb("mean", [P, FEAT])
        mean_hi = m.sb("mean_hi", [P, KB, P], F32R)
        mean_lo = m.sb("mean_lo", [P, KB, P], F32R)
        norm = Norm(m) if kind != "hidden" else None
        sum_ps = m.ps("sum_ps", [P, FEAT])
        turn_ps = m.ps("turn_ps", [P, KB * P])
        y_ps = [m.ps(f"y_ps{u}", [P, FEAT]) for u in range(2)]
        mean_ready = m.sem("mean_ready")
        turned = m.sem("turned")
        hi_ready = m.sem("hi_ready")
        lo_ready = m.sem("lo_ready")
        multiplied = m.sems("multiplied")
        y_ps_free = m.sems("y_ps_free")
        ready_to_relu = m.sems("ready_to_relu")
        block = m.block()

        @block.sync
        def _(sp):
            if kind == "gcn":
                sp.dma_start(bias[:, :], bias_d.partition_broadcast(P)).then_inc(bias_ready, 16)
            moves.program(sp, w)

        @block.tensor
        def _(pe):
            def add_up(tile, u, n):
                whole, n16 = plus(pe, tile, 1), times16(pe, n)
                pe.wait_ge(counts_ready[u], n16)
                pe.wait_ge(mean_ready, whole)
                for a in (0, HALF):
                    terms = [(counts[:, u, k, :], part[:, k, a:a + HALF]) for part in parts
                             for k in range(BLOCKS)]
                    if kind == "gcn":
                        terms += [(g["ident_r"][:, :],
                                   part[:, bass.ds(tile, 1), a:a + HALF].rearrange("p b n -> p (b n)"))
                                  for part in parts]
                    for t, (c, r) in enumerate(terms):
                        last = nc.tensor.matmul(sum_ps[:, a:a + HALF], c, r, start=(t == 0),
                                                stop=(t == len(terms) - 1))
                last.then_inc(counts_free[u], 1)

            def turn(tile, u, n):
                whole = plus(pe, tile, 2)
                pe.wait_ge(mean_ready, whole)
                for k in range(KB):
                    last = nc.tensor.transpose(turn_ps[:, k * P:(k + 1) * P], mean[:, k * P:(k + 1) * P],
                                               g["ident"][:, :])
                last.then_inc(turned, 1)

            def multiply(tile, u, n):
                whole = plus(pe, tile, 1)
                pe.wait_ge(lo_ready, whole)
                pe.wait_ge(y_ps_free[u], n)
                product(nc, y_ps[u], mean_hi, mean_lo, w).then_inc(multiplied[u], 1)

            pe.sem_inc(mean_ready, 1)
            add_up(0, 0, 1)
            with pe.Fori(0, BLOCKS // 2 - 1) as i:
                n = pe.snap(i + 1)
                more = pe.snap(i + 2)
                turn(i * 2, 0, n)
                add_up(i * 2 + 1, 1, n)
                multiply(i * 2, 0, n)
                turn(i * 2 + 1, 1, n)
                add_up(i * 2 + 2, 0, more)
                multiply(i * 2 + 1, 1, n)
            turn(BLOCKS - 2, 0, BLOCKS // 2)
            add_up(BLOCKS - 1, 1, BLOCKS // 2)
            multiply(BLOCKS - 2, 0, BLOCKS // 2)
            turn(BLOCKS - 1, 1, BLOCKS // 2)
            multiply(BLOCKS - 1, 1, BLOCKS // 2)

        @block.scalar
        def _(act):
            load_table(nc, g, ACT.Sqrt if norm else ACT.Copy)
            for u in range(2):
                act.sem_inc(counts_free[u], 1)

            def take_mean(tile, u, n):
                more = plus(act, n, 1)
                done = plus(act, tile, 1)
                act.wait_ge(counts_free[u], more)
                act.wait_ge(turned, done)
                nc.scalar.activation(mean[:, :], sum_ps[:, :], ACT.Copy, scale=scale[:, bass.ds(tile, 1)])\
                    .then_inc(mean_ready, 1)

            def take_turned(tile, u, n):
                more = plus(act, tile, 2)
                act.wait_ge(turned, more)
                act.wait_ge(multiplied[1 - u], n)
                nc.scalar.activation(mean_hi[:, :, :].rearrange("p b n -> p (b n)"), turn_ps[:, :], ACT.Copy)\
                    .then_inc(hi_ready, 1)

            def root(tile):
                if norm:
                    norm.root(act, nc, g, plus(act, tile, 1))

            act.sem_inc(turned, 1)
            act.sem_inc(multiplied[1], 1)
            w.high(act, nc, range(0, KB - 3))
            take_mean(0, 0, 1)
            w.high(act, nc, range(KB - 3, KB))
            with act.Fori(0, BLOCKS // 2 - 1) as i:
                n = act.snap(i + 1)
                more = act.snap(i + 2)
                take_turned(i * 2, 0, n)
                take_mean(i * 2 + 1, 1, n)
                root(i * 2)
                take_turned(i * 2 + 1, 1, n)
                take_mean(i * 2 + 2, 0, more)
                root(i * 2 + 1)
            take_turned(BLOCKS - 2, 0, BLOCKS // 2)
            take_mean(BLOCKS - 1, 1, BLOCKS // 2)
            root(BLOCKS - 2)
            take_turned(BLOCKS - 1, 1, BLOCKS // 2)
            root(BLOCKS - 1)

        @block.vector
        def _(dve):
            for u in range(2):
                dve.sem_inc(y_ps_free[u], 1)
                if kind != "gcn":
                    dve.sem_inc(added_free[u], 1)
                if kind != "hidden":
                    dve.sem_inc(x_free[u], 1)
            w.low(dve, nc)
            if kind == "gcn":
                dve.wait_ge(bias_ready, 16)

            def step(tile, u, n):
                whole = dve.snap(tile + 1)
                more = dve.snap(n + u)
                n16 = times16(dve, n)
                dve.wait_ge(hi_ready, whole)
                nc.vector.tensor_tensor(mean_lo[:, :, :].rearrange("p b n -> p (b n)"), turn_ps[:, :],
                                        mean_hi[:, :, :].rearrange("p b n -> p (b n)").bitcast(F32),
                                        ALU.subtract).then_inc(lo_ready, 1)
                out = y[:, u, :]
                dve.wait_ge(y_stored[u], n16)
                if kind == "gcn":
                    dve.wait_ge(x_ready[u], n16)
                    dve.wait_ge(multiplied[u], more)
                    nc.vector.tensor_tensor(out, y_ps[u][:, :], bias[:, :], ALU.add)\
                        .then_inc(y_ps_free[u], 1)
                    dve.drain()
                    nc.vector.scalar_tensor_tensor(out=out, in0=out, scalar=0.0, in1=x[:, u, :], op0=ALU.max,
                                                   op1=ALU.add).then_inc(x_free[u], 1)
                else:
                    dve.wait_ge(added_ready[u], n16)
                    dve.wait_ge(multiplied[u], more)
                    nc.vector.tensor_tensor(out, y_ps[u][:, :], added[:, u, :], ALU.add)\
                        .then_inc(y_ps_free[u], 1)
                    dve.drain()
                    dve.sem_inc(added_free[u], 1)
                    if kind == "hidden":
                        nc.vector.tensor_scalar(out, out, 0.0, None, ALU.max).then_inc(y_ready[u], 1)
                        return
                    dve.wait_ge(x_ready[u], n16)
                    nc.vector.tensor_tensor(out, out, x[:, u, :], ALU.add).then_inc(x_free[u], 1)
                dve.drain()
                norm.program(dve, nc, out, out, whole).then_inc(y_ready[u], 1)

            plain(dve, step)


def project_stage(nc, g, x_d, rms_d, down_d, left_d, right_d, xl_d, xr, dst_pairs_d, dst_all):
    with ExitStack() as ctx:
        m = Memory(nc, ctx, "project")
        rms_w = m.sb("rms_w", [P, KB])
        w = WeightSplit(m, "down", down_d, HID, scale=rms_w)
        KH = HID // P
        left = WeightSplit(m, "left", left_d, HID, blocks=KH)
        right = WeightSplit(m, "right", right_d, HID, blocks=KH)
        x = m.sb("x", [P, 2, FEAT])
        square = m.sb("square", [P, FEAT])
        rms = m.sb("rms", [P, 2])
        down = m.sb("down", [P, HID])
        xl = m.sb("xl", [P, 2, HID])
        xt_hi = m.sb("xt_hi", [P, KB, P], F32R)
        xt_lo = m.sb("xt_lo", [P, KB, P], F32R)
        dt_hi = m.sb("dt_hi", [P, KH, P], F32R)
        dt_lo = m.sb("dt_lo", [P, KH, P], F32R)
        xt_ps = m.ps("xt_ps", [P, KB * P])
        down_ps = m.ps("down_ps", [P, HID])
        dt_ps = m.ps("dt_ps", [P, HID])
        xl_ps = m.ps("xl_ps", [P, HID])
        xr_ps = m.ps("xr_ps", [P, HID])
        names = "rms_ready turned squared hi_ready lo_ready multiplied down_ready down_turned dt_hi_ready " \
                "dt_lo_ready xl_whole xl_ready xr_ready"
        s = {n: m.sem(n) for n in names.split()}
        x_ready = m.sems("x_ready")
        xl_stored = m.sems("xl_stored")
        dst_ready = m.sem("dst_ready")
        PART = dst_all.shape[1] // (BLOCKS - 2)
        assert PART * (BLOCKS - 2) == dst_all.shape[1]
        block = m.block()

        @block.sync
        def _(sp):
            sp.dma_start(rms_w[:, :], rms_d).then_inc(s["rms_ready"], 16)
            for u in range(2):
                sp.sem_inc(xl_stored[u], 16)
                sp.dma_start(x[:, u, :], rows(x_d, u)).then_inc(x_ready[u], 16)
            w.load(sp)
            left.load(sp)
            right.load(sp)

            def store(tile, u):
                sp.wait_ge(s["xl_ready"], tile + 1 if isinstance(tile, int) else sp.snap(tile + 1))
                sp.dma_start(rows(xl_d, tile), xl[:, u, :]).then_inc(xl_stored[u], 16)

            with sp.Fori(0, BLOCKS // 2 - 1) as i:
                for u in range(2):
                    store(i * 2 + u, u)
                    sp.dma_start(x[:, u, :], rows(x_d, i * 2 + 2 + u)).then_inc(x_ready[u], 16)
                    some = bass.ds((i * 2 + u) * PART, PART)
                    sp.dma_start(dst_all[:, some], dst_pairs_d[some].partition_broadcast(P))\
                        .then_inc(dst_ready, 16)
            for u in range(2):
                store(BLOCKS - 2 + u, u)
            for u in range(2):
                sp.wait_ge(xl_stored[u], 16 * (BLOCKS // 2 + 1))
            sp.wait_ge(dst_ready, 16 * (BLOCKS - 2))

        @block.tensor
        def _(pe):
            def turn(tile, u, n):
                pe.wait_ge(x_ready[u], times16(pe, n))
                for k in range(KB):
                    last = nc.tensor.transpose(xt_ps[:, k * P:(k + 1) * P], x[:, u, k * P:(k + 1) * P],
                                               g["ident"][:, :])
                last.then_inc(s["turned"], 1)

            def multiply(tile, u, n):
                pe.wait_ge(s["lo_ready"], plus(pe, tile, 1))
                product(nc, down_ps, xt_hi, xt_lo, w, width=HID).then_inc(s["multiplied"], 1)

            def turn_down(tile, u, n):
                pe.wait_ge(s["down_ready"], plus(pe, tile, 1))
                for k in range(KH):
                    last = nc.tensor.transpose(dt_ps[:, k * P:(k + 1) * P], down[:, k * P:(k + 1) * P],
                                               g["ident"][:, :])
                last.then_inc(s["down_turned"], 1)

            def multiply_down(tile, u, n):
                c = plus(pe, tile, 1)
                pe.wait_ge(s["dt_lo_ready"], c)
                pe.wait_ge(s["xr_ready"], c)
                product(nc, xl_ps, dt_hi, dt_lo, left, width=HID)
                product(nc, xr_ps, dt_hi, dt_lo, right, width=HID).then_inc(s["xl_whole"], 1)

            interleaved(pe, [("late", turn_down), ("early", turn), ("late", multiply_down),
                             ("early", multiply)])

        @block.scalar
        def _(act):
            load_table(nc, g, ACT.Sqrt)

            def split_high():
                act.wait_ge(s["rms_ready"], 16)
                for split in (w, left, right):
                    split.high(act, nc)

            def take_turned(tile, u, n):
                c = plus(act, tile, 1)
                act.wait_ge(x_ready[u], times16(act, n))
                act.wait_ge(s["turned"], c)
                nc.scalar.activation(xt_hi[:, :, :].rearrange("p b n -> p (b n)"), xt_ps[:, :], ACT.Copy)\
                    .then_inc(s["hi_ready"], 1)
                nc.scalar.activation(square[:, :], x[:, u, :], ACT.Square, accum_out=rms[:, 0:1])
                act.drain()
                nc.scalar.activation(rms[:, 1:2], rms[:, 0:1], ACT.Sqrt, scale=1.0 / FEAT,
                                     bias=g["rms_eps"][:, :]).then_inc(s["squared"], 1)

            def take_down(tile, u, n):
                act.wait_ge(s["down_turned"], plus(act, tile, 1))
                nc.scalar.activation(dt_hi[:, :, :].rearrange("p b n -> p (b n)"), dt_ps[:, :], ACT.Copy)\
                    .then_inc(s["dt_hi_ready"], 1)

            def take_xl(tile, u, n):
                c, n16 = plus(act, tile, 1), times16(act, n)
                act.wait_ge(s["xl_whole"], c)
                act.wait_ge(xl_stored[u], n16)
                nc.scalar.activation(xl[:, u, :], xl_ps[:, :], ACT.Copy).then_inc(s["xl_ready"], 1)

            interleaved(act, [("late", take_down), ("early", take_turned), ("late", take_xl)],
                        split_high)

        @block.vector
        def _(dve):
            dve.sem_inc(s["xr_ready"], 1)

            def split_low():
                for split in (w, left, right):
                    split.low(dve, nc)

            def take_turned(tile, u, n):
                dve.wait_ge(s["hi_ready"], plus(dve, tile, 1))
                nc.vector.tensor_tensor(xt_lo[:, :, :].rearrange("p b n -> p (b n)"), xt_ps[:, :],
                                        xt_hi[:, :, :].rearrange("p b n -> p (b n)").bitcast(F32),
                                        ALU.subtract).then_inc(s["lo_ready"], 1)

            def scale_down(tile, u, n):
                c = plus(dve, tile, 1)
                dve.wait_ge(s["squared"], c)
                nc.vector.reciprocal(rms[:, 1:2], rms[:, 1:2])
                dve.drain()
                dve.wait_ge(s["multiplied"], c)
                nc.vector.tensor_scalar(down[:, :], down_ps[:, :], rms[:, 1:2], None, ALU.mult)\
                    .then_inc(s["down_ready"], 1)

            def take_down(tile, u, n):
                dve.wait_ge(s["dt_hi_ready"], plus(dve, tile, 1))
                nc.vector.tensor_tensor(dt_lo[:, :, :].rearrange("p b n -> p (b n)"), dt_ps[:, :],
                                        dt_hi[:, :, :].rearrange("p b n -> p (b n)").bitcast(F32),
                                        ALU.subtract).then_inc(s["dt_lo_ready"], 1)

            def take_xr(tile, u, n):
                dve.wait_ge(s["xl_whole"], plus(dve, tile, 1))
                nc.vector.tensor_copy(xr[:, bass.ds(tile, 1), :].rearrange("p b n -> p (b n)"), xr_ps[:, :])\
                    .then_inc(s["xr_ready"], 1)

            interleaved(dve, [("late", take_down), ("early", take_turned), ("late", take_xr),
                              ("early", scale_down)], split_low)


def attention_stage(nc, g, att_d, dst_all, xl_d, edge_xl_d, xr, mixed_d):
    KH = HID // P
    VISITS = BLOCKS * (QUADS + 1)
    with ExitStack() as ctx:
        m = Memory(nc, ctx, "attention")
        att = m.sb("att", [P, KH])
        ones = m.sb("ones", [P, P])
        att_wide = m.sb("att_wide", [P, HEADS, P], F32R)
        att_cols = m.sb("att_cols", [P, KH, HEADS])
        xr_hi = m.sb("xr_hi", [P, HID], F32R)
        xr_lo = m.sb("xr_lo", [P, HID], F32R)
        node_max = m.sb("node_max", [P, BLOCKS, HEADS])
        tile_max = m.sb("tile_max", [P, HEADS])
        zero = m.sb("zero", [P, HID + HEADS])
        inverse = m.sb("inverse", [P, HEADS])
        mixed = m.sb("mixed", [P, HID])
        index = m.sb("index", [P, BATCH_TILES], I32)
        fetched = m.sb("fetched", [P, BATCH_TILES, HID])

        def slots(name, shape, dtype=F32):
            return [m.sb(f"{name}{s}", shape, dtype) for s in range(2)]

        scores = slots("scores", [P, VISITS * 2, HEADS])
        got = slots("got", [P, 2, HID])
        hot_t = slots("hot_t", [P, PAIR], F32R)
        mask = slots("mask", [P, PAIR], BF16)
        scaled = slots("scaled", [P, KH * PAIR])
        bent = slots("bent", [P, KH * PAIR])
        bent_r = slots("bent_r", [P, KH * PAIR], F32R)
        back = slots("back", [P, 2, HID])
        hot_max = slots("hot_max", [P, PAIR])
        hot = slots("hot", [P, 2, P])
        shifted = slots("shifted", [P, 2, HEADS])
        weighted = slots("weighted", [P, 2, HID + HEADS])
        message_ps = [m.ps(f"message_ps{s}", [P, KH, PAIR]) for s in range(2)]
        spread_ps = [m.ps(f"spread_ps{s}", [P, HEADS, PAIR]) for s in range(2)]
        small_ps = m.ps("small_ps", [P, 2, HEADS])
        mix_ps = m.ps("mix_ps", [P, HID + HEADS])
        score_ps = [small_ps[:, :, :], mix_ps[:, 0:2 * HEADS].rearrange("p (u h) -> p u h", h=HEADS)]
        max_ps = [spread_ps[s][:, 0, 0:2 * HEADS].rearrange("p (u h) -> p u h", h=HEADS) for s in range(2)]
        a = {n: m.sems(f"a_{n}") for n in
             "got_ready hot_ready mask_ready message_ready scaled_ready bent_ready bent_r_ready spread_ready "
             "maxed score_kept".split()}
        b = {n: m.sems(f"b_{n}") for n in
             "back_ready hot_max_ready max_spread shift_ready exp_ready pool_weighted dve_weighted "
             "mixed_in".split()}
        gathered = g["gathered"]
        edges_stored, index_ready = m.sems("edges_stored", BATCH), m.sem("index_ready")
        loaded, wide_ready, xr_ready = (m.sem(n) for n in "loaded wide_ready xr_ready".split())
        block_mixed, block_out, mixed_stored, maxima_whole, scores_whole, passed, batches_passed = (
            m.sem(n) for n in "block_mixed block_out mixed_stored maxima_whole scores_whole passed batches_passed".split())

        def visits(engine, early=None, late=None, begin=None, finish=None):
            count = engine.alloc_register(f"quads_{engine.engine.name}_{nc.next_id()}")
            engine.reg_mov(count, 1)
            with engine.Fori(0, BLOCKS) as j:
                first = engine.value_load(g["quads"][0:1, bass.ds(j, 1)], min_val=0, max_val=QUADS - 1)
                end = engine.value_load(g["quads"][0:1, bass.ds(j + BLOCKS, 1)], min_val=1, max_val=QUADS)
                quads = engine.snap(count, min_val=1, max_val=BLOCKS * QUADS + 1)
                if begin:
                    begin(j)
                if early:
                    early(j, 1, engine.snap(j + SELF), engine.snap(quads + j, max_val=VISITS), True,
                          (engine.snap(first * 2, max_val=PAIRS - 2), quads))
                with engine.Fori(first, end) as q:
                    n0 = engine.snap(count, min_val=1, max_val=BLOCKS * QUADS)
                    pending = engine.snap(n0 + j, max_val=VISITS - 1)
                    n1 = engine.snap(n0 + j + 1, max_val=VISITS)
                    pair = engine.snap(q * 2, max_val=PAIRS - 2)
                    other = engine.snap(q * 2 + 1, max_val=PAIRS - 1)
                    if early:
                        early(j, 0, pair, n0, False, (other, n1))
                    if late:
                        late(j, 1, pending)
                    if early:
                        early(j, 1, other, n1, False, (engine.snap(q * 2 + 2, max_val=PAIRS),
                                                       engine.snap(n0 + 1, max_val=BLOCKS * QUADS + 1)))
                    if late:
                        late(j, 0, n0)
                    engine.reg_add(count, count, 1)
                if late:
                    quads = engine.snap(count, min_val=1, max_val=BLOCKS * QUADS + 1)
                    late(j, 1, engine.snap(quads + j, max_val=VISITS))
                if finish:
                    finish(j)

        def stores_of(engine, j):
            return [engine.value_load(g["stores"][0:1, bass.ds(k, 1)] if not isinstance(k, int) else
                                      g["stores"][0:1, k:k + 1], min_val=low, max_val=high)
                    for k, low, high in ((j, 0, BATCHES + BLOCKS), (j + 1, 1, BATCHES + BLOCKS))]

        def hot_by_edge(dve, tiles, free, ready):
            def make(s, pair, j, n):
                dve.wait_ge(free[s], n)
                nc.vector.tensor_scalar(tiles[s][:, :], dst_all[:, bass.ds(pair * PAIR, PAIR)],
                                        g["node"][:, bass.ds(j, 1)], None, ALU.is_equal)\
                    .then_inc(ready[s], 1)

            def ahead(j, s, pair, n, loops, following):
                if loops:
                    make(1, pair, j, n)
                make(1 - s, following[0], j, following[1])

            return ahead

        def weigh_tile(engine, s, u):
            return engine.tensor_tensor(weighted[s][:, u, 0:HID].rearrange("p (h d) -> p h d", h=HEADS),
                                        back[s][:, u, :].rearrange("p (h d) -> p h d", h=HEADS),
                                        weighted[s][:, u, HID:].unsqueeze(2)
                                        .to_broadcast([P, HEADS, HEAD_DIM]), ALU.mult)

        block = m.block(gpsimd_works=True)

        @block.sync
        def _(sp):
            sp.dma_start(att[:, :], att_d).then_inc(loaded, 16)
            sp.sem_inc(mixed_stored, 16)

            def load_pair(tiles, s, pair, ready):
                sp.dma_start(tiles[s][:, :, :], edge_xl_d[bass.ds(pair * PAIR, PAIR), :]
                             .rearrange("(u p) n -> p u n", p=P)).then_inc(ready[s], 16)

            def store_batches(j):
                first, end = stores_of(sp, j)
                with sp.Fori(first, end) as t:
                    got16 = sp.snap(t * 16 + 16)
                    for q in range(BATCH):
                        for k in range(4 * q, 4 * q + 4):
                            sp.wait_ge(gathered[k], got16)
                        sp.dma_start(edge_xl_d[bass.ds((t * BATCH + q) * 4 * P, 4 * P), :]
                                     .rearrange("(k p) n -> p k n", p=P), fetched[:, 4 * q:4 * q + 4, :])\
                            .then_inc(edges_stored[q], 16)

            def load(j, s, pair, n, loops, following):
                if loops:
                    stored16 = times16(sp, stores_of(sp, j)[1])
                    sp.wait_ge(a["message_ready"][s], n)
                    sp.dma_start(got[s][:, 0, :], rows(xl_d, j)).then_inc(a["got_ready"][s], 16)
                    for q in range(BATCH):
                        sp.wait_ge(edges_stored[q], stored16)
                    sp.sem_inc(batches_passed, 1)
                    return
                sp.wait_ge(a["message_ready"][s], n)
                load_pair(got, s, pair, a["got_ready"])

            visits(sp, early=load, begin=store_batches)

            def load_back(j, s, pair, n, loops, following):
                before = sp.snap(n - 1)
                sp.wait_ge(b["pool_weighted"][s], before)
                sp.wait_ge(b["dve_weighted"][s], before)
                if loops:
                    sp.dma_start(back[s][:, 0, :], rows(xl_d, j)).then_inc(b["back_ready"][s], 16)
                else:
                    load_pair(back, s, pair, b["back_ready"])

            def finish(j):
                sp.wait_ge(block_out, sp.snap(j + 2))
                sp.dma_start(rows(mixed_d, j), mixed[:, :]).then_inc(mixed_stored, 16)

            visits(sp, early=load_back, finish=finish)
            sp.wait_ge(mixed_stored, 16 * (BLOCKS + 1))

        @block.gpsimd
        def _(pool):
            with pool.Fori(0, stores_of(pool, BLOCKS - 1)[1]) as t:
                before16 = pool.snap(t * 16)
                copied = [pool.snap(t * BATCH + q + 1) for q in range(BATCH)]
                for q in range(BATCH):
                    ks = range(4 * q, 4 * q + 4)
                    pool.wait_ge(edges_stored[q], before16)
                    pool.sem_inc(passed, 1)
                    pool.tensor_copy(index[:, 4 * q:4 * q + 4],
                                     g["src_index"][:, bass.ds(t * BATCH_TILES + 4 * q, 4)])\
                        .then_inc(index_ready, 1)
                    pool.wait_ge(index_ready, copied[q])
                    pool.sem_inc(passed, 1)
                    for k in ks:
                        pool.indirect_dma_start(fetched[:, k, :], None, xl_d,
                                                bass.IndirectOffsetOnAxis(index[:, k:k + 1], 0))\
                            .then_inc(gathered[k], 16)

            def weigh(j, s, n):
                more, n16 = plus(pool, n, 1), times16(pool, n)
                pool.wait_ge(b["exp_ready"][s], more)
                pool.wait_ge(b["back_ready"][s], n16)
                weigh_tile(nc.gpsimd, s, 0).then_inc(b["pool_weighted"][s], 1)

            visits(pool, late=weigh)

        @block.vector
        def _(dve):
            nc.vector.memset(ones[:, :], 1.0)
            nc.vector.memset(att_wide[:, :, :].bitcast(F32), 0.0)
            nc.vector.memset(att_cols[:, :, :], 0.0)
            nc.vector.memset(zero[:, :], 0.0)
            dve.drain()
            dve.wait_ge(loaded, 16)
            for h in range(HEADS):
                r, k = h * HEAD_DIM % P, h * HEAD_DIM // P
                col = att[r:r + HEAD_DIM, k:k + 1]
                nc.vector.tensor_scalar(att_wide[r:r + HEAD_DIM, h, :], ones[r:r + HEAD_DIM, :], col, None,
                                        ALU.mult)
                nc.vector.tensor_copy(att_cols[r:r + HEAD_DIM, k, h:h + 1], col).then_inc(wide_ready, 1)
            nc.vector.memset(node_max[:, :, :], MASKED)
            for s in range(2):
                nc.vector.memset(back[s][:, :, :], 0.0)
                for sem in (a["maxed"], a["bent_ready"], b["shift_ready"]):
                    dve.sem_inc(sem[s], 1)
            dve.sem_inc(block_out, 1)
            dve.drain()
            dve.sem_inc(wide_ready, 1)

            def begin(j):
                block_xr = xr[:, bass.ds(j, 1), :].rearrange("p b n -> p (b n)")
                nc.vector.tensor_copy(xr_hi[:, :], block_xr)
                dve.drain()
                nc.vector.tensor_tensor(xr_lo[:, :], block_xr, xr_hi[:, :].bitcast(F32), ALU.subtract)\
                    .then_inc(xr_ready, 1)

            ahead = hot_by_edge(dve, hot_t, a["mask_ready"], a["hot_ready"])

            def bend(j, s, pair, n, loops, following):
                ahead(j, s, pair, n, loops, following)
                dve.wait_ge(a["spread_ready"][s], n)
                dve.wait_ge(a["scaled_ready"][s], n)
                nc.vector.tensor_tensor(bent[s][:, :], message_ps[s][:, :, :].rearrange("p k e -> p (k e)"),
                                        scaled[s][:, :], ALU.max).then_inc(a["bent_ready"][s], 1)

            def take_max(j, s, n):
                dve.wait_ge(a["spread_ready"][s], dve.snap(n + 1, max_val=VISITS + 1))
                nc.vector.tensor_reduce(tile_max[:, :], spread_ps[s][:, :, :], AX.X, ALU.max)
                dve.drain()
                block_max = node_max[:, bass.ds(j, 1), :].rearrange("p b h -> p (b h)")
                nc.vector.tensor_tensor(block_max, block_max, tile_max[:, :], ALU.max)\
                    .then_inc(a["maxed"][s], 1)
                dve.drain()

            visits(dve, early=bend, late=take_max, begin=begin)
            dve.sem_inc(maxima_whole, 1)

            ahead_max = hot_by_edge(dve, hot_max, b["max_spread"], b["hot_max_ready"])

            def shift_and_weigh(j, s, pair, n, loops, following):
                more, n16 = dve.snap(n + 1), times16(dve, n)
                ahead_max(j, s, pair, n, loops, following)
                dve.wait_ge(b["exp_ready"][s], n)
                dve.wait_ge(b["max_spread"][s], more)
                nc.vector.tensor_tensor(shifted[s][:, :, :], scores[s][:, bass.ds(n * 2 - 2, 2), :],
                                        max_ps[s], ALU.subtract)
                dve.drain()
                nc.vector.tensor_scalar(shifted[s][:, :, :], shifted[s][:, :, :], BOUND, None, ALU.min)\
                    .then_inc(b["shift_ready"][s], 1)
                dve.wait_ge(b["mixed_in"][s], n)
                for u in range(2):
                    nc.vector.tensor_scalar(hot[s][:, u, :], g["iota"][:, bass.ds(j * P, P)],
                                            g["dst"][:, bass.ds(pair * 2 + u, 1)], None, ALU.is_equal)
                dve.wait_ge(b["exp_ready"][s], more)
                dve.wait_ge(b["back_ready"][s], n16)
                weigh_tile(nc.vector, s, 1).then_inc(b["dve_weighted"][s], 1)

            def finish(j):
                c = dve.snap(j + 1)
                c16 = times16(dve, c)
                dve.wait_ge(block_mixed, c)
                nc.vector.tensor_scalar(inverse[:, :], mix_ps[:, HID:], 1e-16, None, ALU.add)
                dve.drain()
                nc.vector.reciprocal(inverse[:, :], inverse[:, :])
                dve.drain()
                dve.wait_ge(mixed_stored, c16)
                nc.vector.tensor_tensor(mixed[:, :].rearrange("p (h d) -> p h d", h=HEADS),
                                        mix_ps[:, 0:HID].rearrange("p (h d) -> p h d", h=HEADS),
                                        inverse[:, :].unsqueeze(2).to_broadcast([P, HEADS, HEAD_DIM]),
                                        ALU.mult).then_inc(block_out, 1)

            visits(dve, early=shift_and_weigh, finish=finish)

        @block.scalar
        def _(act):
            load_table(nc, g, ACT.Exp)
            for s in range(2):
                for sem in (a["mask_ready"], a["score_kept"], b["exp_ready"]):
                    act.sem_inc(sem[s], 1)

            def bend(j, s, pair, n, loops, following):
                more = act.snap(n + 1)
                act.wait_ge(a["message_ready"][s], more)
                nc.scalar.activation(scaled[s][:, :], message_ps[s][:, :, :].rearrange("p k e -> p (k e)"),
                                     ACT.Copy, scale=SLOPE).then_inc(a["scaled_ready"][s], 1)
                act.wait_ge(a["spread_ready"][s], n)
                nc.scalar.activation(mask[s][:, :], hot_t[s][:, :].bitcast(F32), ACT.Copy, scale=-MASKED,
                                     bias=MASKED).then_inc(a["mask_ready"][s], 1)
                act.wait_ge(a["bent_ready"][s], more)
                nc.scalar.activation(bent_r[s][:, :], bent[s][:, :], ACT.Copy)\
                    .then_inc(a["bent_r_ready"][s], 1)

            def keep(j, s, n):
                act.wait_ge(a["spread_ready"][s], act.snap(n + 1))
                nc.scalar.activation(scores[s][:, bass.ds(n * 2 - 2, 2), :], score_ps[s], ACT.Copy)\
                    .then_inc(a["score_kept"][s], 1)

            visits(act, early=bend, late=keep)
            act.drain()
            act.sem_inc(scores_whole, 1)

            def exponentials(j, s, pair, n, loops, following):
                more = act.snap(n + 1)
                act.wait_ge(b["mixed_in"][s], n)
                act.wait_ge(b["shift_ready"][s], more)
                nc.scalar.activation(weighted[s][:, :, HID:], shifted[s][:, :, :], ACT.Exp)\
                    .then_inc(b["exp_ready"][s], 1)

            visits(act, early=exponentials)

        @block.tensor
        def _(pe):
            for s in range(2):
                for sem in (a["message_ready"], a["spread_ready"], b["max_spread"], b["mixed_in"]):
                    pe.sem_inc(sem[s], 1)
            pe.wait_ge(wide_ready, HEADS + 1)

            def messages(j, s, pair, n, loops, following):
                blocks, n16 = pe.snap(j + 1), times16(pe, n)
                made = pe.snap(n + j, max_val=2 * VISITS) if s == 0 else n
                pe.wait_ge(a["got_ready"][s], n16)
                pe.wait_ge(a["hot_ready"][s], made)
                pe.wait_ge(a["bent_ready"][s], n)
                pe.wait_ge(xr_ready, blocks)
                for u in range(1 if loops else 2):
                    for k in range(KH):
                        nc.tensor.matmul(message_ps[s][:, k, u * P:(u + 1) * P],
                                         got[s][:, u, k * P:(k + 1) * P], g["ident"][:, :],
                                         is_transpose=True, start=(u == 0 and k == 0), stop=False,
                                         skip_group_check=True)
                for k in range(KH):
                    for part in (xr_hi, xr_lo):
                        last = nc.tensor.matmul(message_ps[s][:, k, :], part[:, k * P:(k + 1) * P],
                                                hot_t[s][:, :], start=False,
                                                stop=(k == KH - 1 and part is xr_lo),
                                                skip_group_check=True)
                last.then_inc(a["message_ready"][s], 1)

            def score(j, s, n):
                more = pe.snap(n + 1)
                pe.wait_ge(a["maxed"][s], n)
                pe.wait_ge(a["score_kept"][s], n)
                pe.wait_ge(a["mask_ready"][s], more)
                for h in range(0, HEADS, 2):
                    nc.tensor.matmul(spread_ps[s][:, h:h + 2, :], g["ident_b"][:, :],
                                     mask[s][:, :].unsqueeze(1).to_broadcast([P, 2, PAIR]), start=True,
                                     stop=False, skip_group_check=True)
                pe.wait_ge(a["bent_r_ready"][s], n)
                for u in range(2):
                    for k in range(KH):
                        nc.tensor.matmul(score_ps[s][:, u, :],
                                         bent[s][:, k * PAIR + u * P:k * PAIR + (u + 1) * P],
                                         att_cols[:, k, :], start=(u == 0 and k == 0),
                                         stop=(u == 1 and k == KH - 1), skip_group_check=True)
                for h in range(HEADS):
                    k = h * HEAD_DIM // P
                    last = nc.tensor.matmul(spread_ps[s][:, h, :], att_wide[:, h, :],
                                            bent_r[s][:, k * PAIR:(k + 1) * PAIR], start=False,
                                            stop=(h % 2 == 1), skip_group_check=True)
                last.then_inc(a["spread_ready"][s], 1)

            visits(pe, early=messages, late=score)
            pe.wait_ge(maxima_whole, 1)
            pe.wait_ge(scores_whole, 1)

            def begin(j):
                pe.wait_ge(block_out, pe.snap(j + 1))
                nc.tensor.matmul(mix_ps[:, :], zero[:, 0:P], zero[:, :], start=True, stop=False,
                                 skip_group_check=True)

            def maxima(j, s, pair, n, loops, following):
                made = pe.snap(n + j, max_val=2 * VISITS) if s == 0 else n
                pe.wait_ge(b["hot_max_ready"][s], made)
                pe.wait_ge(b["shift_ready"][s], n)
                for u in range(2):
                    last = nc.tensor.matmul(max_ps[s][:, u, :], hot_max[s][:, u * P:(u + 1) * P],
                                            node_max[:, bass.ds(j, 1), :].rearrange("p b h -> p (b h)"),
                                            start=(u == 0), stop=(u == 1), skip_group_check=True)
                last.then_inc(b["max_spread"][s], 1)

            def mix(j, s, n):
                pe.wait_ge(b["pool_weighted"][s], n)
                pe.wait_ge(b["dve_weighted"][s], n)
                for u in range(2):
                    last = nc.tensor.matmul(mix_ps[:, :], hot[s][:, u, :], weighted[s][:, u, :],
                                            start=False, stop=False, skip_group_check=True)
                last.then_inc(b["mixed_in"][s], 1)

            def finish(j):
                nc.tensor.matmul(mix_ps[:, :], zero[:, 0:P], zero[:, :], start=False, stop=True,
                                 skip_group_check=True).then_inc(block_mixed, 1)

            visits(pe, early=maxima, late=mix, begin=begin, finish=finish)


def attention_out_stage(nc, g, mixed_d, up_d, x_d, y_d, parts):
    KH = HID // P
    with ExitStack() as ctx:
        m = Memory(nc, ctx, "attention_out")
        w = WeightSplit(m, "up", up_d, FEAT, blocks=KH)
        moves = Moves(m)
        mixed, mixed_ready, mixed_free = moves.load("mixed", mixed_d, [HID])
        x, x_ready, x_free = moves.load("x", x_d, [FEAT])
        y, y_ready, y_stored = moves.store("y", y_d)
        mt_hi = m.sb("mt_hi", [P, 2, KH, P], F32R)
        mt_lo = m.sb("mt_lo", [P, 2, KH, P], F32R)
        norm = Norm(m)
        mt_ps = [m.ps(f"mt_ps{u}", [P, HID]) for u in range(2)]
        y_ps = [m.ps(f"y_ps{u}", [P, FEAT]) for u in range(2)]
        hi_ready = m.sems("hi_ready")
        lo_ready = m.sems("lo_ready")
        multiplied = m.sems("multiplied")
        y_ps_free = m.sems("y_ps_free")
        part_ready = m.sems("part_ready")
        scaled = m.sb("scaled", [P, 2, FEAT])
        scaled_used = m.sems("scaled_used")
        block = m.block(gpsimd_works=True)

        @block.sync
        def _(sp):
            moves.program(sp, w)

        @block.tensor
        def _(pe):
            for u in range(2):
                pe.sem_inc(multiplied[u], 1)
                pe.sem_inc(mixed_free[u], 1)

            def turn(tile, u, n):
                pe.wait_ge(mixed_ready[u], times16(pe, n))
                for k in range(KH):
                    last = nc.tensor.transpose(mt_ps[u][:, k * P:(k + 1) * P],
                                               mixed[:, u, k * P:(k + 1) * P], g["ident"][:, :])
                last.then_inc(mixed_free[u], 1)

            def multiply(tile, u, n):
                pe.wait_ge(lo_ready[u], n)
                pe.wait_ge(y_ps_free[u], n)
                product(nc, y_ps[u], mt_hi[:, u], mt_lo[:, u], w)\
                    .then_inc(multiplied[u], 1)

            skewed(pe, turn, multiply)

        @block.scalar
        def _(act):
            load_table(nc, g, ACT.Sqrt)

            def early(tile, u, n):
                act.wait_ge(mixed_free[u], plus(act, n, 1))
                act.wait_ge(multiplied[u], n)
                nc.scalar.activation(mt_hi[:, u].rearrange("p b n -> p (b n)"), mt_ps[u][:, :], ACT.Copy)\
                    .then_inc(hi_ready[u], 1)

            for u in range(2):
                act.sem_inc(part_ready[u], 1)

            def late(tile, u, n):
                norm.root(act, nc, g, plus(act, tile, 1))
                act.wait_ge(y_ready[u], n)
                act.wait_ge(scaled_used[u], n)
                nc.scalar.activation(scaled[:, u, :], y[:, u, :], ACT.Copy,
                                     scale=g["root"][:, bass.ds(tile, 1)])
                act.drain()
                nc.scalar.activation(parts[0][:, bass.ds(tile, 1), :].rearrange("p b n -> p (b n)"),
                                     scaled[:, u, :], ACT.Copy).then_inc(part_ready[u], 1)

            skewed(act, early, late, lambda: w.high(act, nc))

        @block.vector
        def _(dve):
            for u in range(2):
                dve.sem_inc(y_ps_free[u], 1)
                dve.sem_inc(x_free[u], 1)

            def early(tile, u, n):
                dve.wait_ge(hi_ready[u], n)
                nc.vector.tensor_tensor(mt_lo[:, u].rearrange("p b n -> p (b n)"), mt_ps[u][:, :],
                                        mt_hi[:, u].rearrange("p b n -> p (b n)").bitcast(F32),
                                        ALU.subtract).then_inc(lo_ready[u], 1)

            def late(tile, u, n):
                more = plus(dve, n, 1)
                n16 = times16(dve, n)
                out = y[:, u, :]
                dve.wait_ge(y_stored[u], n16)
                dve.wait_ge(part_ready[u], n)
                dve.wait_ge(x_ready[u], n16)
                dve.wait_ge(multiplied[u], more)
                nc.vector.tensor_tensor(out, y_ps[u][:, :], x[:, u, :], ALU.add)\
                    .then_inc(y_ps_free[u], 1)
                dve.drain()
                dve.sem_inc(x_free[u], 1)
                norm.program(dve, nc, out, out, plus(dve, tile, 1)).then_inc(y_ready[u], 1)

            skewed(dve, early, late, lambda: w.low(dve, nc))

        @block.gpsimd
        def _(pool):
            for u in range(2):
                pool.sem_inc(scaled_used[u], 1)

            def step(tile, u, n):
                pool.wait_ge(part_ready[u], pool.snap(n + 1))
                nc.gpsimd.tensor_tensor(parts[1][:, bass.ds(tile, 1), :].rearrange("p b n -> p (b n)"),
                                        scaled[:, u, :],
                                        parts[0][:, bass.ds(tile, 1), :].rearrange("p b n -> p (b n)")
                                        .bitcast(F32), ALU.subtract).then_inc(scaled_used[u], 1)

            plain(pool, step)


def graph_layers(nc, io, out):
    def dram(name, shape):
        return nc.dram_tensor(name, shape, F32, kind="Internal").ap()

    x1_d, x2_d, x3_d = (dram(f"x{n}_d", [ROWS, FEAT]) for n in (1, 2, 3))
    self_d, hidden_d = dram("self_d", [ROWS, FEAT]), dram("hidden_d", [ROWS, FEAT])
    xl_d, mixed_d = dram("xl_d", [ROWS, HID]), dram("mixed_d", [ROWS, HID])
    edge_xl_d = dram("edge_xl_d", [STORED * P, HID])
    with ExitStack() as ctx:
        m = Memory(nc, ctx, "all")
        g = {
            "ident": m.sb("ident", [P, P]),
            "ident_r": m.sb("ident_r", [P, P], F32R),
            "ident_b": m.sb("ident_b", [P, P], BF16),
            "eps": m.sb("eps", [P, 1]),
            "rms_eps": m.sb("rms_eps", [P, 1]),
            "one": m.sb("one", [P, 1]),
            "table_loaded": m.sb("table_loaded", [P, 1]),
            "degree": m.sb("degree", [P, BLOCKS]),
            "root": m.sb("root", [P, BLOCKS]),
            "inverse": m.sb("inverse", [P, BLOCKS]),
            "counts_d": dram("counts_d", [ROWS, BLOCKS * P]),
            "gathered": m.sems("gathered", BATCH_TILES),
        }
        with ExitStack() as edges:
            m = Memory(nc, edges, "edges")
            g |= {
                "iota": m.sb("iota", [P, ROWS]),
                "node": m.sb("node", [P, BLOCKS]),
                "dst": m.sb("dst", [P, TILES]),
                "src": m.sb("src", [P, TILES]),
                "src_index": m.sb("src_index", [P, STORED], I32),
                "weight": m.sb("weight", [P, TILES]),
                "weight_hi": m.sb("weight_hi", [P, TILES], F32R),
                "weight_lo": m.sb("weight_lo", [P, TILES], F32R),
                "pairs": m.sb("pairs", [1, 2 * BLOCKS], I32),
                "quads": m.sb("quads", [1, 2 * BLOCKS], I32),
                "stores": m.sb("stores", [1, BLOCKS + 1], I32),
            }
            setup(nc, io, g)
            with ExitStack() as inner:
                m = Memory(nc, inner, "first")
                wt = [m.sb(f"wt_{x}", [P, KB, FEAT], F32R) for x in ("hi", "lo")]
                build_graph(nc, g, *wt)
                dense_stage(nc, g, "first", io["x"], x1_d, io["L0_gnn_bias"], weight_parts=wt)
            with ExitStack() as inner:
                m = Memory(nc, inner, "heads")
                xr = m.sb("xr", [P, BLOCKS, HID])
                dst_all = m.sb("dst_all", [P, (PAIRS + BLOCKS) * PAIR], I32)
                project_stage(nc, g, x1_d, io["rms_cols"], io["L1_gnn_W_down"], io["L1_gnn_Wl"],
                              io["L1_gnn_Wr"], xl_d, xr, io["dst_pairs"], dst_all)
                attention_stage(nc, g, io["att_cols"], dst_all, xl_d, edge_xl_d, xr, mixed_d)
        m = Memory(nc, ctx, "layers")
        parts = [m.sb(f"parts_{x}", [P, BLOCKS, FEAT], F32R) for x in ("hi", "lo")]
        attention_out_stage(nc, g, mixed_d, io["L1_gnn_W_up"], x1_d, x2_d, parts)
        graph_stage(nc, g, "gcn", parts, x3_d, io["L2_gnn_W"], g["root"], "gcn", bias_d=io["L2_gnn_b"],
                    x_d=x2_d)
        dense_stage(nc, g, "self0", x3_d, self_d, io["L3_gnn_b0"], weight_d=io["L3_gnn_W_self0"],
                    parts_out=parts)
        graph_stage(nc, g, "sage0", parts, hidden_d, io["L3_gnn_W_neigh0"], g["inverse"], "hidden",
                    added_d=self_d)
        dense_stage(nc, g, "self1", hidden_d, self_d, io["L3_gnn_b1"], weight_d=io["L3_gnn_W_self1"],
                    parts_out=parts)
        graph_stage(nc, g, "sage1", parts, out, io["L3_gnn_W_neigh1"], g["inverse"], "last",
                    added_d=self_d, x_d=x3_d)


def kernel(**inputs):
    import numpy as np
    import concourse.bacc as bacc
    from concourse.bass_utils import run_bass_kernel_spmd

    edges = {n: np.asarray(inputs[n]) for n in ("src", "dst", "edge_weight")}

    def pad(a, size, value):
        return np.concatenate([a, np.full(size - a.shape[0], value, a.dtype)])

    def columns(a):
        return np.ascontiguousarray(a.reshape(-1, P).T)

    nodes = np.arange(ROWS, dtype=np.int32).reshape(BLOCKS, P)
    loops_dst = np.concatenate([nodes, np.full_like(nodes, NO_NODE)], axis=1).reshape(-1)
    loops_src = np.concatenate([nodes, np.zeros_like(nodes)], axis=1).reshape(-1)
    dst = pad(edges["dst"], PAIRS * PAIR, PAD_NODE)
    src = pad(edges["src"], PAIRS * PAIR, PAD_NODE)
    dst_all = np.concatenate([dst, loops_dst])
    arrays = {
        "x": np.concatenate([np.asarray(inputs["x"]), np.zeros((ROWS - NODES, FEAT), np.float32)]),
        "dst_by_pair": pad(dst, P * PAIR, NO_NODE).reshape(P, PAIR),
        "dst_by_quad": pad(dst, P * 2 * PAIR, NO_NODE).reshape(P, 2 * PAIR),
        "dst_pairs": dst_all,
        "dst_cols": columns(dst_all),
        "src_cols": columns(np.concatenate([src, loops_src])),
        "weight_cols": columns(pad(edges["edge_weight"], TILES * P, 0)),
        "rms_cols": columns(np.asarray(inputs["L1_gnn_rms_w"])),
        "att_cols": columns(np.asarray(inputs["L1_gnn_att"]).reshape(-1)),
    }
    for name in ("L0_gnn_bias", "L1_gnn_W_down", "L1_gnn_Wl", "L1_gnn_Wr", "L1_gnn_W_up", "L2_gnn_W", "L2_gnn_b",
                 "L3_gnn_W_self0", "L3_gnn_W_neigh0", "L3_gnn_b0", "L3_gnn_W_self1", "L3_gnn_W_neigh1",
                 "L3_gnn_b1"):
        arrays[name] = np.ascontiguousarray(np.asarray(inputs[name]))
    nc = bacc.Bacc("TRN2", target_bir_lowering=False, num_devices=1)
    io = {n: nc.dram_tensor(f"in_{n}", a.shape, mybir.dt.from_np(a.dtype), kind="ExternalInput").ap()
          for n, a in arrays.items()}
    out = nc.dram_tensor("out", (ROWS, FEAT), F32, kind="ExternalOutput").ap()
    graph_layers(nc, io, out)
    result = run_bass_kernel_spmd(nc, [{f"in_{n}": a for n, a in arrays.items()}], core_ids=[0])
    return result.results[0]["out"][:NODES]
```
